# Optimizing a Trainium2 kernel written in Bass

```python
import numpy as np
import jax
import jax.numpy as jnp

def _softmax(x, axis=-1):
    return jax.nn.softmax(x, axis=axis)

def _gelu(x):
    return jax.nn.gelu(x, approximate=True)

def _silu(x):
    return jax.nn.silu(x)

def _sigmoid(x):
    return jax.nn.sigmoid(x)

def _layernorm(x, axis=-1, eps=1e-05):
    m = jnp.mean(x, axis=axis, keepdims=True)
    v = jnp.var(x, axis=axis, keepdims=True)
    return (x - m) / jnp.sqrt(v + eps)

def _scatter_add(tgt, idx, src, axis=0):
    return tgt.at[idx].add(src)

def _segment_sum(src, seg, n):
    return jax.ops.segment_sum(src, seg, n)
kernel_name = 'mk_gnn_resnorm_d4_gnn_r8_17b971'

def setup_inputs(seed: int=0):
    np.random.seed(seed)
    _w = jnp.asarray

    def _rec_inputs():
        import jax
        import jax.numpy as jnp
        _gk = jax.random.key(seed)
        x = -0.000202 + 1 * jax.random.normal(jax.random.fold_in(_gk, 1), (6250, 128), jnp.float32)
        src = jax.random.randint(jax.random.fold_in(_gk, 2), (100000,), 0, 6250, jnp.int32)
        dst = jax.random.randint(jax.random.fold_in(_gk, 3), (100000,), 0, 6250, jnp.int32)
        _o = jnp.argsort(dst, stable=True)
        src = src[_o]
        dst = dst[_o]
        edge_type_8 = jax.random.randint(jax.random.fold_in(_gk, 13), (100000,), 0, 8, jnp.int32)
        edge_weight = jax.random.uniform(jax.random.fold_in(_gk, 14), (100000,), jnp.float32, 0.0, 1)
        node_type_8 = jax.random.randint(jax.random.fold_in(_gk, 15), (6250,), 0, 8, jnp.int32)
        return (x, src, dst, edge_type_8, edge_weight, node_type_8)
    x, src, dst, edge_type_8, edge_weight, node_type_8 = _rec_inputs()

    def _L0_gnn_setup():
        import jax, jax.numpy as jnp
        import numpy as np
        N = 6250
        F_DIM = 128
        H_DIM = 128
        E = 100000

        def _gcn_norm(src, dst, edge_weight, num_nodes):
            loop = jnp.arange(num_nodes, dtype=src.dtype)
            src2 = jnp.concatenate([src, loop])
            dst2 = jnp.concatenate([dst, loop])
            w2 = jnp.concatenate([edge_weight, jnp.ones((num_nodes,), edge_weight.dtype)])
            deg = jax.ops.segment_sum(w2, dst2, num_segments=num_nodes)
            dinv = jnp.where(deg > 0, jax.lax.rsqrt(jnp.where(deg > 0, deg, 1.0)), 0.0)
            norm = dinv[src2] * w2 * dinv[dst2]
            return (src2, dst2, norm)

        def _gcn_conv(x, W, b, src, dst, norm, num_nodes):
            h = x @ W
            msg = norm[:, None] * h[src]
            agg = jax.ops.segment_sum(msg, dst, num_segments=num_nodes)
            return agg + b
        key = jax.random.key(seed)
        ks = jax.random.split(key, 8)
        x = jax.random.normal(ks[0], (N, F_DIM), dtype=jnp.float32)
        edge_weight = jax.random.uniform(ks[1], (E,), dtype=jnp.float32)
        src = jax.random.randint(ks[2], (E,), 0, N)
        dst = jax.random.randint(ks[3], (E,), 0, N)
        edge_index = jnp.stack([src, dst]).astype(jnp.int64)
        sc = 1.0 / np.sqrt(F_DIM)
        W1 = jax.random.normal(ks[4], (F_DIM, H_DIM), dtype=jnp.float32) * sc
        W2 = jax.random.normal(ks[5], (H_DIM, H_DIM), dtype=jnp.float32) * sc
        Wfc = jax.random.normal(ks[6], (H_DIM, F_DIM), dtype=jnp.float32) * sc
        b1 = jnp.zeros((H_DIM,), jnp.float32)
        b2 = jnp.zeros((H_DIM,), jnp.float32)
        bfc = jnp.zeros((F_DIM,), jnp.float32)
        return {'x': x, 'edge_weight': edge_weight, 'W1': W1, 'b1': b1, 'W2': W2, 'b2': b2, 'Wfc': Wfc, 'bfc': bfc, 'edge_index': edge_index}
    _L0_gnn_all = _L0_gnn_setup()
    _L0_gnn_in = {k: v for k, v in _L0_gnn_all.items() if k in ('W1', 'b1', 'W2', 'b2', 'Wfc', 'bfc')}
    del _L0_gnn_all

    def _L1_gnn_setup():
        import jax, jax.numpy as jnp
        import numpy as np
        N_NODES = 6250
        N_EDGES = 100000
        DIM = 128
        N_HEADS = 8
        HEAD_DIM = DIM // N_HEADS
        LN_EPS = 1e-05
        NEG_SLOPE = 0.2

        def _gat_forward(x, src, dst, ln_gamma, ln_beta, W_in, b_in, W_u, b_u, W_v, W_ff, b_ff):
            mu = jnp.mean(x, axis=-1, keepdims=True)
            var = jnp.mean(jnp.square(x - mu), axis=-1, keepdims=True)
            x = (x - mu) * jax.lax.rsqrt(var + LN_EPS) * ln_gamma + ln_beta
            x = x @ W_in + b_in
            scores_u = x @ W_u + b_u
            scores_v = x @ W_v
            e = scores_u[src] + scores_v[dst]
            e = jnp.where(e >= 0, e, NEG_SLOPE * e)
            m = jax.ops.segment_max(e, dst, num_segments=N_NODES)
            ex = jnp.exp(e - m[dst])
            s = jax.ops.segment_sum(ex, dst, num_segments=N_NODES)
            probs = ex / s[dst]
            xh = x.reshape(N_NODES, HEAD_DIM, N_HEADS)
            msg = xh[src] * probs[:, None, :]
            agg = jax.ops.segment_sum(msg, dst, num_segments=N_NODES)
            out = agg.reshape(N_NODES, DIM)
            return out @ W_ff + b_ff
        key = jax.random.key(seed)
        ks = jax.random.split(key, 10)
        inp = {'x': jax.random.normal(ks[0], (N_NODES, DIM), dtype=jnp.float32), 'src': jax.random.randint(ks[1], (N_EDGES,), 0, N_NODES, dtype=jnp.int32), 'dst': jax.random.randint(ks[2], (N_EDGES,), 0, N_NODES, dtype=jnp.int32), 'ln_gamma': jnp.ones((DIM,), dtype=jnp.float32), 'ln_beta': jnp.zeros((DIM,), dtype=jnp.float32), 'W_in': jax.random.normal(ks[3], (DIM, DIM), dtype=jnp.float32) * DIM ** (-0.5), 'b_in': jax.random.normal(ks[4], (DIM,), dtype=jnp.float32) * 0.02, 'W_u': jax.random.normal(ks[5], (DIM, N_HEADS), dtype=jnp.float32) * DIM ** (-0.5), 'b_u': jax.random.normal(ks[6], (N_HEADS,), dtype=jnp.float32) * 0.02, 'W_v': jax.random.normal(ks[7], (DIM, N_HEADS), dtype=jnp.float32) * DIM ** (-0.5), 'W_ff': jax.random.normal(ks[8], (DIM, DIM), dtype=jnp.float32) * DIM ** (-0.5), 'b_ff': jax.random.normal(ks[9], (DIM,), dtype=jnp.float32) * 0.02}
        return inp
    _L1_gnn_all = _L1_gnn_setup()
    _L1_gnn_in = {k: v for k, v in _L1_gnn_all.items() if k in ('ln_gamma', 'ln_beta', 'W_in', 'b_in', 'W_u', 'b_u', 'W_v', 'W_ff', 'b_ff')}
    del _L1_gnn_all

    def _L2_gnn_setup():
        import jax, jax.numpy as jnp
        import numpy as np
        N = 6250
        E = 100000
        DIN = 128
        DH = 128
        H = 8
        DK = DH // H
        TN = 8
        TE = 8
        NB = 4

        def _decomp(x, nt, w_comp, w_basis):
            T = w_comp.shape[0]
            W = (w_comp @ w_basis).reshape(T, x.shape[-1], -1)
            h_all = jnp.einsum('ni,tio->tno', x, W)
            return h_all[nt, jnp.arange(x.shape[0])]
        key = jax.random.key(seed)
        ks = jax.random.split(key, 20)
        inp = {}
        inp['node_feat'] = jax.random.normal(ks[0], (N, DIN), jnp.float32)
        inp['node_type'] = jax.random.randint(ks[1], (N,), 0, TN)
        inp['src'] = jax.random.randint(ks[2], (E,), 0, N)
        inp['dst'] = jax.random.randint(ks[3], (E,), 0, N)
        inp['edge_type'] = jax.random.randint(ks[4], (E,), 0, TE)
        s = 0.05
        for i, nm in enumerate(['k', 'q', 'v', 'a']):
            inp['w_comp_' + nm] = jax.random.normal(ks[5 + 2 * i], (TN, NB), jnp.float32) * s
            inp['w_basis_' + nm] = jax.random.normal(ks[6 + 2 * i], (NB, DIN * DH), jnp.float32) * s
        inp['relation_pri'] = jnp.ones((TE, H), jnp.float32)
        inp['relation_att'] = jax.random.uniform(ks[13], (TE, H, DK, DK), jnp.float32, -0.25, 0.25)
        inp['relation_msg'] = jax.random.uniform(ks[14], (TE, H, DK, DK), jnp.float32, -0.25, 0.25)
        inp['loop_weight'] = jax.random.uniform(ks[15], (DIN, DH), jnp.float32, -0.08, 0.08)
        inp['bias'] = jnp.zeros((DH,), jnp.float32)
        return inp
    _L2_gnn_all = _L2_gnn_setup()
    _L2_gnn_in = {k: v for k, v in _L2_gnn_all.items() if k in ('w_comp_k', 'w_basis_k', 'w_comp_q', 'w_basis_q', 'w_comp_v', 'w_basis_v', 'w_comp_a', 'w_basis_a', 'relation_pri', 'relation_att', 'relation_msg', 'loop_weight', 'bias')}
    del _L2_gnn_all

    def _L3_gnn_setup():
        import jax, jax.numpy as jnp
        import numpy as np
        N = 6250
        E = 100000
        F = 128

        def _xavier(key, fan_out, fan_in):
            lim = np.sqrt(6.0 / (fan_in + fan_out)).astype(np.float32)
            return jax.random.uniform(key, (fan_out, fan_in), jnp.float32, -lim, lim)
        key = jax.random.key(seed)
        ks = jax.random.split(key, 14)
        x = jax.random.normal(ks[0], (N, F), jnp.float32)
        src = jax.random.randint(ks[1], (E,), 0, N)
        off = jax.random.randint(ks[2], (E,), 1, N)
        dst = (src + off) % N
        edge_index = jnp.stack([src, dst]).astype(jnp.int64)
        return {'x': x, 'edge_index': edge_index, 'W_w': _xavier(ks[3], F, F), 'W_b': jnp.zeros((F,), jnp.float32), 'U_w': _xavier(ks[4], F, F), 'U_b': jnp.zeros((F,), jnp.float32), 'V_w': _xavier(ks[5], F, 2 * F), 'V_b': jnp.zeros((F,), jnp.float32), 'D_w': _xavier(ks[6], F, F), 'D_b': jnp.zeros((F,), jnp.float32), 'E_w': _xavier(ks[7], F, F), 'E_b': jnp.zeros((F,), jnp.float32)}
    _L3_gnn_all = _L3_gnn_setup()
    _L3_gnn_in = {k: v for k, v in _L3_gnn_all.items() if k in ('W_w', 'W_b', 'U_w', 'U_b', 'V_w', 'V_b', 'D_w', 'D_b', 'E_w', 'E_b')}
    del _L3_gnn_all
    return {'x': x, 'src': src, 'dst': dst, 'edge_type_8': edge_type_8, 'edge_weight': edge_weight, 'node_type_8': node_type_8, 'L0_gnn_W1': _L0_gnn_in['W1'], 'L0_gnn_b1': _L0_gnn_in['b1'], 'L0_gnn_W2': _L0_gnn_in['W2'], 'L0_gnn_b2': _L0_gnn_in['b2'], 'L0_gnn_Wfc': _L0_gnn_in['Wfc'], 'L0_gnn_bfc': _L0_gnn_in['bfc'], 'L1_gnn_ln_gamma': _L1_gnn_in['ln_gamma'], 'L1_gnn_ln_beta': _L1_gnn_in['ln_beta'], 'L1_gnn_W_in': _L1_gnn_in['W_in'], 'L1_gnn_b_in': _L1_gnn_in['b_in'], 'L1_gnn_W_u': _L1_gnn_in['W_u'], 'L1_gnn_b_u': _L1_gnn_in['b_u'], 'L1_gnn_W_v': _L1_gnn_in['W_v'], 'L1_gnn_W_ff': _L1_gnn_in['W_ff'], 'L1_gnn_b_ff': _L1_gnn_in['b_ff'], 'L2_gnn_w_comp_k': _L2_gnn_in['w_comp_k'], 'L2_gnn_w_basis_k': _L2_gnn_in['w_basis_k'], 'L2_gnn_w_comp_q': _L2_gnn_in['w_comp_q'], 'L2_gnn_w_basis_q': _L2_gnn_in['w_basis_q'], 'L2_gnn_w_comp_v': _L2_gnn_in['w_comp_v'], 'L2_gnn_w_basis_v': _L2_gnn_in['w_basis_v'], 'L2_gnn_w_comp_a': _L2_gnn_in['w_comp_a'], 'L2_gnn_w_basis_a': _L2_gnn_in['w_basis_a'], 'L2_gnn_relation_pri': _L2_gnn_in['relation_pri'], 'L2_gnn_relation_att': _L2_gnn_in['relation_att'], 'L2_gnn_relation_msg': _L2_gnn_in['relation_msg'], 'L2_gnn_loop_weight': _L2_gnn_in['loop_weight'], 'L2_gnn_bias': _L2_gnn_in['bias'], 'L3_gnn_W_w': _L3_gnn_in['W_w'], 'L3_gnn_W_b': _L3_gnn_in['W_b'], 'L3_gnn_U_w': _L3_gnn_in['U_w'], 'L3_gnn_U_b': _L3_gnn_in['U_b'], 'L3_gnn_V_w': _L3_gnn_in['V_w'], 'L3_gnn_V_b': _L3_gnn_in['V_b'], 'L3_gnn_D_w': _L3_gnn_in['D_w'], 'L3_gnn_D_b': _L3_gnn_in['D_b'], 'L3_gnn_E_w': _L3_gnn_in['E_w'], 'L3_gnn_E_b': _L3_gnn_in['E_b']}

def reference(x, src, dst, edge_type_8, edge_weight, node_type_8, L0_gnn_W1, L0_gnn_b1, L0_gnn_W2, L0_gnn_b2, L0_gnn_Wfc, L0_gnn_bfc, L1_gnn_ln_gamma, L1_gnn_ln_beta, L1_gnn_W_in, L1_gnn_b_in, L1_gnn_W_u, L1_gnn_b_u, L1_gnn_W_v, L1_gnn_W_ff, L1_gnn_b_ff, L2_gnn_w_comp_k, L2_gnn_w_basis_k, L2_gnn_w_comp_q, L2_gnn_w_basis_q, L2_gnn_w_comp_v, L2_gnn_w_basis_v, L2_gnn_w_comp_a, L2_gnn_w_basis_a, L2_gnn_relation_pri, L2_gnn_relation_att, L2_gnn_relation_msg, L2_gnn_loop_weight, L2_gnn_bias, L3_gnn_W_w, L3_gnn_W_b, L3_gnn_U_w, L3_gnn_U_b, L3_gnn_V_w, L3_gnn_V_b, L3_gnn_D_w, L3_gnn_D_b, L3_gnn_E_w, L3_gnn_E_b):
    import jax
    import jax.numpy as jnp

    def _L0_gnn_ref(x, edge_weight, W1, b1, W2, b2, Wfc, bfc, edge_index):
        import jax, jax.numpy as jnp
        import numpy as np
        N = 6250
        F_DIM = 128
        H_DIM = 128
        E = 100000

        def _gcn_norm(src, dst, edge_weight, num_nodes):
            loop = jnp.arange(num_nodes, dtype=src.dtype)
            src2 = jnp.concatenate([src, loop])
            dst2 = jnp.concatenate([dst, loop])
            w2 = jnp.concatenate([edge_weight, jnp.ones((num_nodes,), edge_weight.dtype)])
            deg = jax.ops.segment_sum(w2, dst2, num_segments=num_nodes)
            dinv = jnp.where(deg > 0, jax.lax.rsqrt(jnp.where(deg > 0, deg, 1.0)), 0.0)
            norm = dinv[src2] * w2 * dinv[dst2]
            return (src2, dst2, norm)

        def _gcn_conv(x, W, b, src, dst, norm, num_nodes):
            h = x @ W
            msg = norm[:, None] * h[src]
            agg = jax.ops.segment_sum(msg, dst, num_segments=num_nodes)
            return agg + b
        src, dst = (edge_index[0], edge_index[1])
        src2, dst2, norm = _gcn_norm(src, dst, edge_weight, N)
        h = jax.nn.relu(_gcn_conv(x, W1, b1, src2, dst2, norm, N))
        h = jax.nn.relu(_gcn_conv(h, W2, b2, src2, dst2, norm, N))
        return h @ Wfc + bfc

    def _L1_gnn_ref(x, src, dst, ln_gamma, ln_beta, W_in, b_in, W_u, b_u, W_v, W_ff, b_ff):
        import jax, jax.numpy as jnp
        import numpy as np
        N_NODES = 6250
        N_EDGES = 100000
        DIM = 128
        N_HEADS = 8
        HEAD_DIM = DIM // N_HEADS
        LN_EPS = 1e-05
        NEG_SLOPE = 0.2

        def _gat_forward(x, src, dst, ln_gamma, ln_beta, W_in, b_in, W_u, b_u, W_v, W_ff, b_ff):
            mu = jnp.mean(x, axis=-1, keepdims=True)
            var = jnp.mean(jnp.square(x - mu), axis=-1, keepdims=True)
            x = (x - mu) * jax.lax.rsqrt(var + LN_EPS) * ln_gamma + ln_beta
            x = x @ W_in + b_in
            scores_u = x @ W_u + b_u
            scores_v = x @ W_v
            e = scores_u[src] + scores_v[dst]
            e = jnp.where(e >= 0, e, NEG_SLOPE * e)
            m = jax.ops.segment_max(e, dst, num_segments=N_NODES)
            ex = jnp.exp(e - m[dst])
            s = jax.ops.segment_sum(ex, dst, num_segments=N_NODES)
            probs = ex / s[dst]
            xh = x.reshape(N_NODES, HEAD_DIM, N_HEADS)
            msg = xh[src] * probs[:, None, :]
            agg = jax.ops.segment_sum(msg, dst, num_segments=N_NODES)
            out = agg.reshape(N_NODES, DIM)
            return out @ W_ff + b_ff
        return _gat_forward(x, src, dst, ln_gamma, ln_beta, W_in, b_in, W_u, b_u, W_v, W_ff, b_ff)

    def _L2_gnn_ref(node_feat, node_type, src, dst, edge_type, w_comp_k, w_basis_k, w_comp_q, w_basis_q, w_comp_v, w_basis_v, w_comp_a, w_basis_a, relation_pri, relation_att, relation_msg, loop_weight, bias):
        import jax, jax.numpy as jnp
        import numpy as np
        N = 6250
        E = 100000
        DIN = 128
        DH = 128
        H = 8
        DK = DH // H
        TN = 8
        TE = 8
        NB = 4

        def _decomp(x, nt, w_comp, w_basis):
            T = w_comp.shape[0]
            W = (w_comp @ w_basis).reshape(T, x.shape[-1], -1)
            h_all = jnp.einsum('ni,tio->tno', x, W)
            return h_all[nt, jnp.arange(x.shape[0])]
        n = node_feat.shape[0]
        scale = (DH / H) ** (-0.5)
        k = _decomp(node_feat, node_type, w_comp_k, w_basis_k).reshape(n, H, DK)
        q = _decomp(node_feat, node_type, w_comp_q, w_basis_q).reshape(n, H, DK)
        v = _decomp(node_feat, node_type, w_comp_v, w_basis_v).reshape(n, H, DK)
        kt = jnp.einsum('nhi,thij->tnhj', k, relation_att)[edge_type, src]
        e = (q[dst] * kt).sum(-1) * relation_pri[edge_type] * scale
        m = jax.ops.segment_max(e, dst, num_segments=n)
        ex = jnp.exp(e - m[dst])
        denom = jax.ops.segment_sum(ex, dst, num_segments=n)
        a = ex / denom[dst]
        vt = jnp.einsum('nhi,thij->tnhj', v, relation_msg)[edge_type, src]
        agg = jax.ops.segment_sum(a[..., None] * vt, dst, num_segments=n)
        agg = agg.reshape(n, DH)
        out = _decomp(agg, node_type, w_comp_a, w_basis_a)
        out = out + node_feat @ loop_weight + bias
        return jax.nn.relu(out)

    def _L3_gnn_ref(x, edge_index, W_w, W_b, U_w, U_b, V_w, V_b, D_w, D_b, E_w, E_b):
        import jax, jax.numpy as jnp
        import numpy as np
        N = 6250
        E = 100000
        F = 128

        def _xavier(key, fan_out, fan_in):
            lim = np.sqrt(6.0 / (fan_in + fan_out)).astype(np.float32)
            return jax.random.uniform(key, (fan_out, fan_in), jnp.float32, -lim, lim)
        n = x.shape[0]
        loops = jnp.arange(n, dtype=edge_index.dtype)
        src = jnp.concatenate([edge_index[0], loops])
        dst = jnp.concatenate([edge_index[1], loops])
        h_tilde = x @ U_w.T + U_b
        h_src = h_tilde[src]
        h_dst = h_tilde[dst]
        e = jax.nn.relu(jnp.concatenate([h_src, h_dst], axis=1) @ V_w.T + V_b)
        e = e + (h_src @ D_w.T + D_b) + (h_dst @ E_w.T + E_b)
        xw = x @ W_w.T + W_b
        deg = jax.ops.segment_sum(jnp.ones_like(src, dtype=xw.dtype), src, num_segments=n)
        inv_sqrt = jax.lax.rsqrt(deg)
        scaler = (inv_sqrt[src] * inv_sqrt[dst])[:, None]
        msgs = xw[dst] * scaler * e
        out = jax.ops.segment_sum(msgs, src, num_segments=n)
        return out
    edge_index = jnp.stack([src, dst])
    x = _layernorm(x + _L0_gnn_ref(x, edge_weight, L0_gnn_W1, L0_gnn_b1, L0_gnn_W2, L0_gnn_b2, L0_gnn_Wfc, L0_gnn_bfc, edge_index), axis=-1)
    x = _layernorm(x + _L1_gnn_ref(x, src, dst, L1_gnn_ln_gamma, L1_gnn_ln_beta, L1_gnn_W_in, L1_gnn_b_in, L1_gnn_W_u, L1_gnn_b_u, L1_gnn_W_v, L1_gnn_W_ff, L1_gnn_b_ff), axis=-1)
    x = _layernorm(x + _L2_gnn_ref(x, node_type_8, src, dst, edge_type_8, L2_gnn_w_comp_k, L2_gnn_w_basis_k, L2_gnn_w_comp_q, L2_gnn_w_basis_q, L2_gnn_w_comp_v, L2_gnn_w_basis_v, L2_gnn_w_comp_a, L2_gnn_w_basis_a, L2_gnn_relation_pri, L2_gnn_relation_att, L2_gnn_relation_msg, L2_gnn_loop_weight, L2_gnn_bias), axis=-1)
    x = _layernorm(x + _L3_gnn_ref(x, edge_index, L3_gnn_W_w, L3_gnn_W_b, L3_gnn_U_w, L3_gnn_U_b, L3_gnn_V_w, L3_gnn_V_b, L3_gnn_D_w, L3_gnn_D_b, L3_gnn_E_w, L3_gnn_E_b), axis=-1)
    return x

_drawn_inputs = setup_inputs


def setup_inputs(seed=0):
    import zlib

    import numpy as np

    out = dict(_drawn_inputs(seed))
    spreads = {'L0_gnn_b1': (0.0, 0.1),
     'L0_gnn_b2': (0.0, 0.1),
     'L0_gnn_bfc': (0.0, 0.1),
     'L1_gnn_ln_gamma': (1.0, 0.2),
     'L1_gnn_ln_beta': (0.0, 0.1),
     'L2_gnn_relation_pri': (1.0, 0.6),
     'L2_gnn_bias': (0.0, 0.8),
     'L3_gnn_W_b': (0.0, 0.1),
     'L3_gnn_U_b': (0.0, 0.1),
     'L3_gnn_V_b': (0.0, 0.395),
     'L3_gnn_D_b': (0.0, 0.323),
     'L3_gnn_E_b': (0.0, 0.327)}
    factors = {'L1_gnn_b_u': 8.0,
     'L2_gnn_w_comp_k': 8.0,
     'L2_gnn_w_basis_k': 8.0,
     'L2_gnn_w_comp_q': 8.0,
     'L2_gnn_w_basis_q': 8.0,
     'L2_gnn_w_comp_v': 8.0,
     'L2_gnn_w_basis_v': 8.0,
     'L2_gnn_w_comp_a': 8.0,
     'L2_gnn_w_basis_a': 8.0,
     'L2_gnn_relation_att': 8.0,
     'L2_gnn_relation_msg': 8.0,
     'L2_gnn_loop_weight': 3.044}
    for name, (base, spread) in spreads.items():
        noise = np.random.default_rng([zlib.crc32(name.encode()), seed]).standard_normal(out[name].shape)
        drawn = base * np.exp(spread * noise) if base else spread * noise
        out[name] = jnp.asarray(drawn.astype(out[name].dtype))
    for name, factor in factors.items():
        out[name] = (out[name] * factor).astype(out[name].dtype)
    return out
```

```python
import concourse.bass as bass
from concourse import mybir
from contextlib import ExitStack

F32 = mybir.dt.float32
I32 = mybir.dt.int32
ALU = mybir.AluOpType
ACT = mybir.ActivationFunctionType
AX = mybir.AxisListType

N = 6250
E = 100000
D = 128
P = 128
NT = -(-N // P)
NP = NT * P
GT = 7
NG = NT // GT
GC = GT * D
LAST = N - (NT - 1) * P
EC = 125
UC = E // EC
UG = UC // 8
GROUPS = 16
JC = 52
SC = GROUPS * JC
HALVES = SC // 8
ITER = HALVES // 2
ROWS = SC * P
H = 8
DK = D // H
TN = 8
NB = 4
TL = JC * P
SX = SC + 8
BIG = 1.0e30
PAD_KEY = 1.0e6
HALF = (P - 1) / 2
EPS = 1e-5
assert SC >= (E + NT * (P - 1)) // P and NG * GT == NT and UG % 2 == 0


class Chain:

    def __init__(self, eng, sem, base=0):
        self.eng, self.sem, self.base, self.n = eng, sem, base, 0

    def __call__(self, ins):
        self.n += 1
        ins.then_inc(self.sem, 1)
        self.eng.wait_ge(self.sem, self.base + self.n)


def settle(eng):
    eng.nop(nofuse=True)


def turns(eng, count, body):
    body(0)
    with eng.Fori(1, count) as k:
        body(k)


def need(eng, sem, value):
    if not isinstance(value, int) or value > 0:
        eng.wait_ge(sem, value)


def bcast_last(ap, n):
    shape = list(ap.shape) + [n]
    return ap.unsqueeze(len(shape) - 1).to_broadcast(shape)


def bcast_mid(ap, n):
    return ap.unsqueeze(1).to_broadcast([ap.shape[0], n] + list(ap.shape[1:]))


def build(nc, t, out):
    ctx = ExitStack()
    with ctx:
        def sb(name, cols, dt=F32):
            return ctx.enter_context(nc.sbuf_tensor(name, [P, cols], dt))

        stage_sems = []

        def sem(name):
            stage_sems.append(nc.alloc_semaphore(name))
            return stage_sems[-1]

        def new_stage():
            nc.clear_and_free_semaphores(list(stage_sems))
            nc.all_engine_barrier()
            stage_sems.clear()

        def dram(name, shape, dt=F32):
            return nc.dram_tensor(name, shape, dt).ap()

        x_cur = sb("x_cur", NT * D)
        iota_row = sb("iota_row", P)
        iota_part = sb("iota_part", 1)
        ident = sb("ident", P)
        earlier = sb("earlier", P)
        before = sb("before", P)
        ones = sb("ones", P)
        int_tmp = sb("int_tmp", P, I32)
        int_tmp2 = sb("int_tmp2", 1, I32)
        d_src = sb("d_src", SX, I32)
        d_typed = sb("d_typed", SX, I32)
        d_lw = sb("d_lw", SX * 2)
        s_dst = sb("s_dst", SX, I32)
        s_lo = sb("s_lo", SX)
        d_tile = sb("d_tile", SC, I32)
        s_tile = sb("s_tile", SC, I32)
        dinv = sb("dinv", NT)
        inv = sb("inv", NT)
        small = sb("small", 512)
        neg_half = sb("neg_half", 64)
        stage_idx = sb("stage_idx", 16, I32)
        stage_lw = sb("stage_lw", 32)
        bias_names = ["L0_gnn_b1", "L0_gnn_bfc", "L1_gnn_ln_gamma", "L1_gnn_ln_beta", "L1_gnn_b_in", "L1_gnn_b_ff",
                      "L2_gnn_bias", "L3_gnn_W_b", "L3_gnn_V_b", "L3_gnn_D_b", "L3_gnn_E_b"]
        bias_sb = sb("bias_sb", len(bias_names) * D)
        bias = {n: bias_sb[:, i * D:(i + 1) * D] for i, n in enumerate(bias_names)}
        b_u = sb("b_u", H)
        col_names = ["L0_gnn_b2", "L1_gnn_b_in", "L3_gnn_U_b"]
        col_sb = sb("col_sb", len(col_names))
        col = {n: col_sb[:, i:i + 1] for i, n in enumerate(col_names)}
        w_names = ["L0_gnn_W1", "L0_gnn_W2", "L0_gnn_Wfc", "L1_gnn_W_in", "L1_gnn_W_ff", "L2_gnn_loop_weight"]
        w_sb = sb("w_sb", len(w_names) * D)
        w = {n: w_sb[:, i * D:(i + 1) * D] for i, n in enumerate(w_names)}
        w_uv = sb("w_uv", 2 * H)
        l3_T = sb("l3_T", 6 * D)
        arena = sb("arena", 34000)

        ps = ctx.enter_context(nc.psum_tensor("ps", [P, 8 * 512], F32))

        def bank(b, n=512, parts=P):
            return ps[0:parts, b * 512:b * 512 + n]

        d_rec = dram("d_rec", [ROWS, 4])
        s_rec = dram("s_rec", [ROWS, 2])
        d_loT = dram("d_loT", [SC, P])
        s_loT = dram("s_loT", [SC, P])
        penT = dram("penT", [P, TL + 1])
        t0 = dram("t0", [NP, D])
        t1 = dram("t1", [NP, D])
        t2 = dram("t2", [NP, D + H])
        t3 = dram("t3", [TN * NP, 2 * D])
        t4 = dram("t4", [NP, 3 * D])
        spill = dram("spill", [HALVES, P, 8 * D])
        p_dram = dram("p_dram", [P, NT * D])
        dp_dram = dram("dp_dram", [P, NT * D])

        landed = [ctx.enter_context(nc.semaphore("landed0")), ctx.enter_context(nc.semaphore("landed1"))]
        gather_pass = [0]
        carry = sb("carry", 3 * P)

        e_in = {}
        o = 0
        for n in ("src", "dst", "typ", "wgt"):
            e_in[n] = arena[0:EC, o:o + UC]
            o += UC
        ld_i = arena[:, o:o + 3 * 7 * EC].bitcast(I32).rearrange("p (a j e) -> p a j e", a=3, j=7)
        o += 3 * 7 * EC
        ld_f = arena[:, o:o + 4 * 7 * EC].rearrange("p (a j e) -> p a j e", a=4, j=7)
        l3_raw = arena[:, o + 4 * 7 * EC:o + 4 * 7 * EC + 6 * D]
        SORT0 = 4 * UC
        loads = sem("loads")
        iotas = sem("iotas")
        zeroed = sem("zeroed")
        v_set = sem("v_set")
        edge_T = sem("edge_T")
        edge_f = sem("edge_f")
        l3_up = sem("l3_up")
        n_loads = [0]
        with nc.Block() as block:
            @block.sync
            def _(sp):
                def load(dst, src):
                    n_loads[0] += 16
                    sp.dma_start(dst, src).then_inc(loads, 16)

                sp.wait_ge(zeroed, 1)
                full = UC // P
                for a, name in enumerate(("src", "dst", "edge_type_8", "edge_weight")):
                    dst = ld_i[:, a] if a < 3 else ld_f[:, 3]
                    load(dst[:, 0:full, :], t[name][0:full * P * EC].rearrange("(j p e) -> p j e", p=P, e=EC))
                    load(dst[0:UC - full * P, full, :], t[name][full * P * EC:E].rearrange("(p e) -> p e", e=EC))
                for i, name in enumerate(("L3_gnn_U_w", "L3_gnn_W_w")):
                    load(l3_raw[:, i * D:(i + 1) * D], t[name])
                load(l3_raw[:, 2 * D:4 * D], t["L3_gnn_V_w"])
                load(l3_raw[:, 4 * D:5 * D], t["L3_gnn_D_w"])
                load(l3_raw[:, 5 * D:6 * D], t["L3_gnn_E_w"])
                for n in w_names:
                    load(w[n], t[n])
                load(w_uv[:, 0:H], t["L1_gnn_W_u"])
                load(w_uv[:, H:2 * H], t["L1_gnn_W_v"])
                for n in bias_names:
                    load(bias[n], t[n].partition_broadcast(P))
                load(b_u[:, :], t["L1_gnn_b_u"].partition_broadcast(P))
                for n in col_names:
                    load(col[n], t[n].rearrange("(p o) -> p o", o=1))
                xt = x_cur[:, :].rearrange("p (t f) -> p t f", f=D)
                load(xt[:, 0:NT - 1, :], t["x"][0:(NT - 1) * P, :].rearrange("(t p) f -> p t f", p=P))
                load(xt[0:LAST, NT - 1, :], t["x"][(NT - 1) * P:N, :])
                sp.wait_ge(loads, n_loads[0])

            @block.gpsimd
            def _(pool):
                nc.gpsimd.iota(int_tmp[:, :], [[1, P]], base=0, channel_multiplier=0).then_inc(iotas, 1)
                nc.gpsimd.iota(int_tmp2[:, :], [[1, 1]], base=0, channel_multiplier=1).then_inc(iotas, 1)

            n_all = 16 * (8 + 5 + len(w_names) + 2 + len(bias_names) + 1 + len(col_names) + 2)

            @block.vector
            def _(dve):
                step = Chain(dve, v_set)
                nc.vector.memset(x_cur[:, (NT - 1) * D:NT * D], 0.0)
                nc.vector.memset(ld_i[:, :, 6, :], 0)
                nc.vector.memset(ld_f[:, 3, 6, :], 0.0).then_inc(zeroed, 1)
                nc.vector.memset(ones[:, :], 1.0)
                nc.vector.memset(neg_half[:, :], -0.5)
                nc.vector.memset(d_src[:, :], 0)
                nc.vector.memset(d_typed[:, :], 0)
                step(nc.vector.memset(s_dst[:, :], 0))
                dve.wait_ge(iotas, 2)
                step(nc.vector.tensor_copy(iota_row[:, :], int_tmp[:, :]))
                step(nc.vector.tensor_copy(iota_part[:, :], int_tmp2[:, :]))
                for m, op in ((ident, ALU.is_equal), (earlier, ALU.is_lt), (before, ALU.is_gt)):
                    step(nc.vector.tensor_scalar(m[:, :], iota_row[:, :], iota_part[:, 0:1], None, op))
                dve.wait_ge(loads, n_all)
                nc.vector.tensor_copy(ld_f[:, 0:3], ld_i).then_inc(edge_f, 1)
                for a, n in enumerate(("src", "dst", "typ", "wgt")):
                    dve.wait_ge(edge_T, a + 1)
                    b = 2 * (a % 2)
                    step(nc.vector.tensor_copy(e_in[n], ps[0:EC, b * 512:b * 512 + UC]))
                step(nc.vector.scalar_tensor_tensor(e_in["typ"], e_in["typ"], float(NP), e_in["src"], ALU.mult, ALU.add))
                dve.wait_ge(l3_up, 1)
                step(nc.vector.tensor_copy(l3_T[:, :], ps[:, 2048:2048 + 6 * D]))

            @block.tensor
            def _(pe):
                pe.wait_ge(edge_f, 1)
                for a in range(4):
                    if a >= 2:
                        pe.wait_ge(v_set, 6 + a - 1)
                    for j in range(7):
                        b = 2 * (a % 2) * 512 + j * P
                        k = min(P, UC - j * P)
                        last = nc.tensor.transpose(ps[0:EC, b:b + k], ld_f[0:k, a, j, :], ident[0:k, 0:k])
                    last.then_inc(edge_T, 1)
                for i in range(6):
                    last = nc.tensor.transpose(ps[:, 2048 + i * D:2048 + (i + 1) * D], l3_raw[:, i * D:(i + 1) * D], ident[:, :])
                last.then_inc(l3_up, 1)

        def sort_edges(which, key, fields, key_dram, rec, loT, tile_row, weights, finish):
            new_stage()
            R = len(fields)
            o = SORT0

            def part(n):
                nonlocal o
                o += n
                return arena[:, o - n:o]
            HC = 2 * NT if weights is not None else NT
            lo = part(UC)[0:EC]
            hi = part(UC)[0:EC]
            hi_i = part(UC)[0:EC].bitcast(I32)
            recs = part(UC * R)[0:EC].rearrange("p (c r) -> p c r", r=R)
            at_lo = part(2 * 8 * P)[0:EC].rearrange("p (b i l) -> p b i l", b=2, i=8)
            at_hi = part(2 * 8 * HC)[0:EC].rearrange("p (b i l) -> p b i l", b=2, i=8)
            zeros = part(P)[0:EC]
            running = part(NT)
            counts = part(NT)
            n_chunks = part(NT)
            tmp = part(NT)
            hi_i_all = part(NT).bitcast(I32)
            first_chunk = part(NT)
            first_col = part(1)
            tile_ge = part(SC)
            tile_rep = part(SC)
            iota_c = part(SC)
            iota_ci = part(SC).bitcast(I32)
            fill = part(JC * 16 * R)
            keys_all = part(2 * 8 * EC).bitcast(I32).rearrange("p (b c) -> p b c", b=2)
            at_loT = part(2 * 8 * EC).rearrange("p (b c) -> p b c", b=2)
            lo_all = part(8 * EC).bitcast(I32)
            same = part(8 * EC)[0:EC].rearrange("p (i e) -> p i e", i=8)
            rank = part(16)[0:EC]
            val = part(16)[0:EC]
            q = part(16)[0:EC].bitcast(I32)
            junk = part(8 * NT)[0:EC].rearrange("p (i l) -> p i l", i=8)
            row = part(16)[0:EC].bitcast(I32)
            recs_st = part(16 * R)[0:EC].rearrange("p (c r) -> p c r", r=R)
            key_st = part(16)[0:EC]
            srt = part(SC * R).rearrange("p (c r) -> p c r", r=R)
            lo_s = part(SC)
            lo_T = part(7 * P)
            assert o <= 34000, o

            pre = which + "_"
            split = sem(pre + "split")
            filled = sem(pre + "filled")
            fill_set = sem(pre + "fill_set")
            hot = sem(pre + "hot")
            hist_free = sem(pre + "hist_free")
            hist_done = sem(pre + "hist_done")
            base_v = sem(pre + "base_v")
            base_p = sem(pre + "base_p")
            iota_done = sem(pre + "iota_done")
            root_in = sem(pre + "root_in")
            root_out = sem(pre + "root_out")

            with nc.Block() as block:
                @block.gpsimd
                def _(pool):
                    nc.gpsimd.iota(iota_ci, [[1, SC]], base=0, channel_multiplier=0).then_inc(iota_done, 1)
                    pool.wait_ge(root_in, 1)
                    nc.gpsimd.tensor_tensor(small[:, 128:128 + NT], small[:, 0:NT], neg_half[:, 0:NT], ALU.pow).then_inc(root_out, 1)

                @block.sync
                def _(sp):
                    sp.wait_ge(fill_set, 1)
                    sp.dma_start(rec.rearrange("(p c) r -> p (c r)", p=P), fill).then_inc(filled, 16)
                    sp.wait_ge(filled, 16)

                @block.vector
                def _(dve):
                    step = Chain(dve, split)
                    step(nc.vector.memset(fill, 0.0))
                    nc.vector.memset(fill.rearrange("p (c r) -> p c r", r=R)[:, :, 1], PAD_KEY).then_inc(fill_set, 1)
                    step(nc.vector.memset(zeros, 0.0))
                    step(nc.vector.tensor_scalar(hi_i, key, -HALF, 1.0 / P, ALU.add, ALU.mult))
                    step(nc.vector.tensor_copy(hi, hi_i))
                    step(nc.vector.scalar_tensor_tensor(lo, hi, -float(P), key, ALU.mult, ALU.add))
                    for f, a in enumerate(fields):
                        step(nc.vector.tensor_copy(recs[:, :, f], a))
                    dve.wait_ge(iota_done, 1)
                    step(nc.vector.tensor_copy(iota_c, iota_ci))
                    with dve.Fori(0, UG // 2) as k:
                        for b in range(2):
                            c0 = 16 * k + 8 * b
                            dve.wait_ge(hist_free, 2 * k + b + 1)
                            nc.vector.tensor_tensor(at_lo[:, b], bcast_mid(iota_row[0:EC, :], 8),
                                                    bcast_last(lo[:, bass.ds(c0, 8)], P), ALU.is_equal).then_inc(hot, 1)
                            nc.vector.tensor_tensor(at_hi[:, b, :, 0:NT], bcast_mid(iota_row[0:EC, 0:NT], 8),
                                                    bcast_last(hi[:, bass.ds(c0, 8)], NT), ALU.is_equal).then_inc(hot, 1)
                            if weights is not None:
                                dve.wait_ge(hot, 3 * (2 * k + b) + 2)
                                nc.vector.tensor_tensor(at_hi[:, b, :, NT:HC], at_hi[:, b, :, 0:NT],
                                                        bcast_last(weights[:, bass.ds(c0, 8)], NT), ALU.mult).then_inc(hot, 1)
                    dve.wait_ge(hist_done, 1)
                    step = Chain(dve, base_v)
                    step(nc.vector.tensor_copy(counts, bank(0, NT)))
                    finish(step, bank(0, HC)[:, NT:HC], counts, small[:, 0:NT], root_in, root_out)
                    dve.wait_ge(base_p, 1)
                    step(nc.vector.tensor_scalar(hi_i_all, bank(1, NT), P - 1 - HALF, 1.0 / P, ALU.add, ALU.mult))
                    step(nc.vector.tensor_copy(n_chunks, hi_i_all))
                    step(nc.vector.memset(tmp, 0.0))
                    step(nc.vector.tensor_tensor_scan(first_chunk, n_chunks, tmp, 0.0, ALU.add, ALU.add))
                    step(nc.vector.tensor_tensor(first_chunk, first_chunk, n_chunks, ALU.subtract))
                    step(nc.vector.scalar_tensor_tensor(running, first_chunk, float(P), bank(2, NT), ALU.mult, ALU.add))
                    dve.wait_ge(base_p, 2)
                    step(nc.vector.tensor_copy(first_col[0:NT], bank(3, 1, NT)))
                    step(nc.vector.tensor_scalar(tile_ge[0:NT], iota_c[0:NT], first_col[0:NT, 0:1], None, ALU.is_ge))
                    dve.wait_ge(base_p, 3)
                    step(nc.vector.tensor_scalar(tile_rep, ps[:, 2048:2048 + SC], -1.0, None, ALU.add))
                    step(nc.vector.tensor_copy(tile_row[0:1, :], tile_rep[0:1, :]))

                n_fin = finish(None, None, None, None, None, None)
                per = 3 if weights is not None else 2

                @block.tensor
                def _(pe):
                    pe.wait_ge(split, 5)
                    nc.tensor.matmul(bank(0, HC), zeros, zeros[:, 0:HC], start=True, stop=False, skip_group_check=True).then_inc(hist_free, 2)
                    with pe.Fori(0, UG // 2) as k:
                        for b in range(2):
                            pe.wait_ge(hot, per * (2 * k + b + 1))
                            for i in range(8):
                                last = nc.tensor.matmul(bank(0, HC), at_lo[:, b, i], at_hi[:, b, i], start=False, stop=False, skip_group_check=True)
                            last.then_inc(hist_free, 1)
                    nc.tensor.matmul(bank(0, HC), zeros, zeros[:, 0:HC], start=False, stop=True, skip_group_check=True).then_inc(hist_done, 1)
                    pe.wait_ge(base_v, 1)
                    nc.tensor.matmul(bank(1, NT), ones[:, :], counts, start=True, stop=True)
                    nc.tensor.matmul(bank(2, NT), before[:, :], counts, start=True, stop=True).then_inc(base_p, 1)
                    pe.wait_ge(base_v, 1 + n_fin + 5)
                    nc.tensor.matmul(bank(3, 1, NT), first_chunk[0:1, :], ones[0:1, 0:1], start=True, stop=True).then_inc(base_p, 1)
                    pe.wait_ge(base_v, 1 + n_fin + 8)
                    for j in range(2):
                        last = nc.tensor.matmul(ps[:, 2048 + j * 512:2048 + j * 512 + min(512, SC - j * 512)], ones[0:NT, :],
                                                tile_ge[0:NT, j * 512:min(SC, (j + 1) * 512)], start=True, stop=True)
                    last.then_inc(base_p, 1)

            keys_in = [sem(pre + "keys_in0"), sem(pre + "keys_in1")]
            keys_free = sem(pre + "keys_free")
            placed = [sem(pre + "placed0"), sem(pre + "placed1")]
            hots = sem(pre + "hots")
            looked_up = sem(pre + "looked_up")
            run_ready = sem(pre + "run_ready")
            rows_ready = sem(pre + "rows_ready")
            v_grp = sem(pre + "v_grp")
            key_rows = key_dram.rearrange("(g c) -> g c", c=8 * EC)
            with nc.Block() as block:
                @block.sync
                def _(sp):
                    with sp.Fori(0, UG // 2) as k:
                        for b in range(2):
                            sp.wait_ge(keys_free, 2 * k + b + 1)
                            sp.dma_start(keys_all[:, b, :], key_rows[bass.ds(2 * k + b, 1), :].to_broadcast([P, 8 * EC])).then_inc(keys_in[b], 16)

                @block.vector
                def _(dve):
                    dve.sem_inc(keys_free, 2)
                    dve.sem_inc(run_ready, 1)
                    def place(k):
                        for b in range(2):
                            n = 2 * k + b
                            c0 = 16 * k + 8 * b
                            step = Chain(dve, v_grp, 7 * n)
                            need(dve, placed[b], 128 * k)
                            nc.vector.tensor_copy(recs_st[:, 8 * b:8 * b + 8, :], recs[:, bass.ds(c0, 8), :])
                            step(nc.vector.tensor_copy(key_st[:, 8 * b:8 * b + 8], key[:, bass.ds(c0, 8)]))
                            nc.vector.tensor_tensor(at_lo[:, b], bcast_mid(iota_row[0:EC, :], 8),
                                                    bcast_last(lo[:, bass.ds(c0, 8)], P), ALU.is_equal)
                            nc.vector.tensor_tensor(at_hi[:, b, :, 0:NT], bcast_mid(iota_row[0:EC, 0:NT], 8),
                                                    bcast_last(hi[:, bass.ds(c0, 8)], NT), ALU.is_equal)
                            dve.wait_ge(keys_in[b], 16 * k + 16)
                            step(nc.vector.tensor_scalar(lo_all, keys_all[:, b, :], P - 1, None, ALU.bitwise_and))
                            nc.vector.tensor_scalar(at_loT[:, b], lo_all, iota_part[:, 0:1], None, ALU.is_equal).then_inc(hots, 1)
                            for i in range(8):
                                nc.vector.scalar_tensor_tensor(same[:, i], keys_all[0:EC, b, i * EC:(i + 1) * EC], key_st[:, 8 * b + i:8 * b + i + 1],
                                                               earlier[0:EC, 0:EC], ALU.is_equal, ALU.mult,
                                                               accum_out=rank[:, 8 * b + i:8 * b + i + 1])
                            for i in range(8):
                                dve.wait_ge(looked_up, 8 * n + i + 1)
                                nc.vector.tensor_tensor(running, running, bank(2 + i % 2, NT), ALU.add).then_inc(run_ready, 1)
                                last = nc.vector.tensor_tensor_reduce(out=junk[:, i], in0=bank(i % 2, NT, EC), in1=at_hi[:, b, i, 0:NT], scale=1.0, scalar=0.0,
                                                               op0=ALU.mult, op1=ALU.add, accum_out=val[:, 8 * b + i:8 * b + i + 1])
                            sl = slice(8 * b, 8 * b + 8)
                            step(last)
                            step(nc.vector.tensor_tensor(val[:, sl], val[:, sl], rank[:, sl], ALU.add))
                            step(nc.vector.tensor_scalar(q[:, sl], val[:, sl], -HALF, 1.0 / P, ALU.add, ALU.mult))
                            step(nc.vector.scalar_tensor_tensor(rank[:, sl], q[:, sl], -float(P), val[:, sl], ALU.mult, ALU.add))
                            step(nc.vector.scalar_tensor_tensor(row[:, sl], rank[:, sl], float(SC), q[:, sl], ALU.mult, ALU.add))
                            assert step.n == 7
                            dve.sem_inc(rows_ready, 1)
                            dve.sem_inc(keys_free, 1)

                    turns(dve, UG // 2, place)

                @block.tensor
                def _(pe):
                    with pe.Fori(0, UG // 2) as k:
                        for b in range(2):
                            n = 2 * k + b
                            pe.wait_ge(hots, n + 1)
                            for i in range(8):
                                pe.wait_ge(run_ready, 8 * n + i + 1)
                                nc.tensor.matmul(bank(i % 2, NT, EC), at_loT[:, b, i * EC:(i + 1) * EC], running, start=True, stop=True)
                                nc.tensor.matmul(bank(2 + i % 2, NT), at_lo[:, b, i], at_hi[:, b, i, 0:NT], start=True, stop=True).then_inc(looked_up, 1)

                @block.gpsimd
                def _(pool):
                    with pool.Fori(0, UG // 2) as k:
                        for b in range(2):
                            pool.wait_ge(rows_ready, 2 * k + b + 1)
                            settle(pool)
                            for i in range(8):
                                pool.indirect_dma_start(out=rec[:, :], out_offset=bass.IndirectOffsetOnAxis(ap=row[:, 8 * b + i:8 * b + i + 1], axis=0),
                                                        in_=recs_st[:, 8 * b + i, :], in_offset=None).then_inc(placed[b], 16)
                    for b in range(2):
                        pool.wait_ge(placed[b], 128 * (UG // 2))

            back = sem(pre + "back")
            v_back = sem(pre + "v_back")
            lo_up = sem(pre + "lo_up")
            lo_out = sem(pre + "lo_out")
            with nc.Block() as block:
                @block.sync
                def _(sp):
                    sp.dma_start(srt, rec.rearrange("(p c) r -> p c r", p=P)).then_inc(back, 16)
                    sp.wait_ge(lo_up, 2)
                    lt = lo_T.rearrange("p (j e) -> p j e", j=7)
                    sp.dma_start(loT[0:6 * P, :].rearrange("(j p) e -> p j e", p=P), lt[:, 0:6, :]).then_inc(lo_out, 16)
                    sp.dma_start(loT[6 * P:SC, :], lt[0:SC - 6 * P, 6, :]).then_inc(lo_out, 16)
                    sp.wait_ge(lo_out, 32)

                @block.vector
                def _(dve):
                    step = Chain(dve, v_back)
                    dve.wait_ge(back, 16)
                    step(nc.vector.scalar_tensor_tensor(lo_s, tile_rep, -float(P), srt[:, :, 1], ALU.mult, ALU.add))
                    if which == "d":
                        lw = d_lw[:, :].rearrange("p (c r) -> p c r", r=2)
                        nc.vector.tensor_copy(d_src[:, 0:SC], srt[:, :, 0])
                        nc.vector.tensor_copy(d_typed[:, 0:SC], srt[:, :, 2])
                        nc.vector.tensor_copy(lw[:, 0:SC, 1], srt[:, :, 3])
                    else:
                        nc.vector.tensor_copy(s_dst[:, 0:SC], srt[:, :, 0])
                    step(nc.vector.tensor_copy(lw[:, 0:SC, 0] if which == "d" else s_lo[:, 0:SC], lo_s))
                    dve.wait_ge(lo_up, 1)
                    nc.vector.tensor_copy(lo_T, ps[:, 0:7 * P]).then_inc(lo_up, 1)

                @block.tensor
                def _(pe):
                    pe.wait_ge(v_back, 1)
                    nc.tensor.matmul(ps[:, 6 * P:7 * P], ident[:, :], ident[:, :], start=True, stop=True)
                    for j in range(7):
                        k = min(P, SC - j * P)
                        last = nc.tensor.transpose(ps[0:k, j * P:(j + 1) * P], lo_s[:, j * P:j * P + k], ident[:, :])
                    last.then_inc(lo_up, 1)
            return srt, lo_s

        def finish_dst(step, weight_sums, counts, arg, root_in, root_out):
            if step is None:
                return 5
            g = small[:, 64:64 + NT]
            step(nc.vector.tensor_scalar(arg, weight_sums, 1.0, None, ALU.add))
            step(nc.vector.tensor_scalar(g, arg, 0.0, None, ALU.is_gt))
            step(nc.vector.tensor_tensor(arg, arg, g, ALU.mult))
            step(nc.vector.scalar_tensor_tensor(arg, arg, 1.0, g, ALU.add, ALU.subtract))
            step.eng.sem_inc(root_in, 1)
            step.eng.wait_ge(root_out, 1)
            step(nc.vector.tensor_tensor(dinv[:, :], small[:, 128:128 + NT], g, ALU.mult))

        def finish_src(step, weight_sums, counts, arg, root_in, root_out):
            if step is None:
                return 2
            step(nc.vector.tensor_scalar(arg, counts, 1.0, None, ALU.add))
            step.eng.sem_inc(root_in, 1)
            step.eng.wait_ge(root_out, 1)
            step(nc.vector.tensor_copy(inv[:, :], small[:, 128:128 + NT]))

        sort_edges("s", e_in["src"], [e_in["dst"], e_in["src"]], t["src"], s_rec, s_loT, s_tile, None, finish_src)
        srt, lo_s = sort_edges("d", e_in["dst"], [e_in["src"], e_in["dst"], e_in["typ"], e_in["wgt"]], t["dst"], d_rec, d_loT, d_tile, e_in["wgt"], finish_dst)
        keys_sorted = srt[:, :, 1]

        W0 = 0
        AT_E = 6400
        AT_ACC = 13056
        AT_Q = 19720
        AT_BUF = 25992
        AW = 34000
        w_typed = {n: arena[:, W0 + i * TN * D:W0 + (i + 1) * TN * D].rearrange("p (t o) -> p t o", t=TN)
                   for i, n in enumerate(("a", "k", "q", "v"))}
        rel = {n: arena[:, W0 + (4 + i) * TN * D:W0 + (5 + i) * TN * D] for i, n in enumerate(("att", "msg"))}
        e_all = arena[:, AT_E:AT_E + SC * H]
        ntb = arena[:, AT_E:AT_E + NP].bitcast(I32)
        acc_att = arena[:, AT_ACC:AT_ACC + NT * (D + H)]
        acc_gcn = arena[:, AT_ACC:AT_ACC + NP]
        q_tab = arena[:, AT_Q:AT_Q + NP]
        v_tab = arena[:, AT_Q:AT_Q + NT * H]

        def tiled(ap, width=D):
            return ap.rearrange("p (t f) -> p t f", f=width)

        def stage_index(dve, idx, staged, base, k, b):
            n_before = 128 * (k + b)
            need(dve, landed[1 - b], base + n_before if not isinstance(n_before, int) or n_before else 0)
            settle(nc.vector)
            nc.vector.tensor_copy(stage_idx[:, 8 * (1 - b):8 * (1 - b) + 8], idx[:, bass.ds(16 * k + 8 * b + 8, 8)]).then_inc(staged, 1)

        def stage_first(idx, staged):
            nc.vector.tensor_copy(stage_idx[:, 0:8], idx[:, 0:8]).then_inc(staged, 1)

        def gathers(pool, table, rows, staged, buffer_free):
            def body(k):
                for b in range(2):
                    pool.wait_ge(staged, 2 * k + b + 1)
                    buffer_free(k, b)
                    settle(pool)
                    for i in range(8):
                        pool.indirect_dma_start(out=rows[:, 8 * b + i, :], out_offset=None, in_=table,
                                                in_offset=bass.IndirectOffsetOnAxis(ap=stage_idx[:, 8 * b + i:8 * b + i + 1], axis=0)).then_inc(landed[b], 16)
            turns(pool, ITER, body)

        def next_pass():
            gather_pass[0] += 1
            return (gather_pass[0] - 1) * 128 * ITER

        def tile_numbers(eng, regs, tile_row, c):
            eng.load(regs, tile_row[0:1, bass.ds(c, 8)])
            return [eng.snap(r, min_val=0, max_val=NT - 1) for r in regs]

        def registers(eng, name):
            return [eng.alloc_register(f"{name}{i}") for i in range(8)]

        class Sums:

            def __init__(self, pre, tile_row, acc, width):
                self.added, self.drained = sem(pre + "added"), sem(pre + "drained")
                self.pre, self.tile_row, self.acc, self.width = pre, tile_row, acc, width

            def start(self, dve):
                self.dve, self.regs = dve, registers(dve, self.pre + "tile")

            def open(self, c):
                self.tiles = tile_numbers(self.dve, self.regs, self.tile_row, c)

            def add(self, i, product):
                if i:
                    self.dve.wait_ge(self.added, i)
                at = self.acc[:, bass.ds(self.tiles[i] * self.width, self.width)]
                nc.vector.tensor_tensor(at, at, product, ALU.add).then_inc(self.added, 1)

            def close(self):
                self.dve.wait_ge(self.added, 8)
                self.dve.sem_inc(self.added, -8)
                self.dve.sem_inc(self.drained, 1)

        AT_T = AT_ACC
        scan = [arena[:, AT_T + i * (TL + 1):AT_T + (i + 1) * (TL + 1)] for i in range(3)]
        stage_T = arena[:, AT_T + 3 * (TL + 1):AT_T + 3 * (TL + 1) + 512]
        assert AT_T + 3 * (TL + 1) + 512 <= AW

        def by_group(ap):
            return ap.rearrange("p (g j) -> p j g", g=GROUPS)

        new_stage()
        f_st = sem("f_st")
        f_ps = sem("f_ps")
        f_out = sem("f_out")
        f_v = sem("f_v")
        f_row = sem("f_row")
        f_dma = sem("f_dma")
        K_T = arena[:, 0:TL]
        pen_f = arena[:, TL:2 * TL + 1]
        f_stage = arena[:, 2 * TL + 8:2 * TL + 8 + 512]
        f_rows = arena[0:1, 2 * TL + 520:2 * TL + 520 + 4 * P]
        pw_row, pb_row, pc_row = (carry[0:1, i * P:(i + 1) * P] for i in range(3))
        keys_keep = arena[:, 2 * TL + 1040:2 * TL + 1040 + SC]
        f_key = sem("f_key")
        with nc.Block() as block:
            @block.vector
            def _(dve):
                nc.vector.tensor_copy(keys_keep, keys_sorted).then_inc(f_key, 1)
        with nc.Block() as block:
            @block.scalar
            def _(act):
                def body(k):
                    need(act, f_ps, k)
                    nc.scalar.activation(f_stage.rearrange("p (j g h) -> p j g h", j=4, g=GROUPS),
                                         bcast_last(by_group(keys_keep)[:, bass.ds(4 * k, 4), :], H), ACT.Copy).then_inc(f_st, 1)
                turns(act, JC // 4, body)

            @block.tensor
            def _(pe):
                def body(k):
                    pe.wait_ge(f_st, k + 1)
                    need(pe, f_out, k)
                    for q in range(4):
                        last = nc.tensor.transpose(ps[:, q * P:(q + 1) * P], f_stage[:, q * P:(q + 1) * P], ident[:, :])
                    last.then_inc(f_ps, 1)
                turns(pe, JC // 4, body)
                pe.wait_ge(f_out, JC // 4)
                nc.tensor.matmul(ps[0:1, 512:512 + P], K_T[:, 0:1], ident[:, :], start=True, stop=True)
                nc.tensor.matmul(ps[0:1, 512 + P:512 + 2 * P], K_T[:, TL - 1:TL], ident[:, :], start=True, stop=True).then_inc(f_row, 1)

            @block.vector
            def _(dve):
                def body(k):
                    dve.wait_ge(f_ps, k + 1)
                    settle(nc.vector)
                    nc.vector.tensor_copy(K_T[:, bass.ds(512 * k, 512)], ps[:, 0:512]).then_inc(f_out, 1)
                turns(dve, JC // 4, body)
                dve.wait_ge(f_out, JC // 4)
                step = Chain(dve, f_v)
                step(nc.vector.memset(pen_f, 0.0))
                step(nc.vector.tensor_tensor(pen_f[:, 1:TL], K_T[:, 1:TL], K_T[:, 0:TL - 1], ALU.not_equal))
                step(nc.vector.tensor_scalar(pen_f[:, 1:TL], pen_f[:, 1:TL], -BIG, None, ALU.mult))
                dve.wait_ge(f_row, 1)
                first, last, cont, whole = (f_rows[:, i * P:(i + 1) * P] for i in range(4))
                step(nc.vector.tensor_copy(f_rows[:, 0:2 * P], ps[0:1, 512:512 + 2 * P]))
                step(nc.vector.memset(cont, 0.0))
                step(nc.vector.tensor_tensor(cont[:, H:P], first[:, H:P], last[:, 0:P - H], ALU.is_equal))
                step(nc.vector.tensor_tensor(whole, first, last, ALU.is_equal))

                def swapped(ap):
                    return ap.rearrange("p (g h) -> p h g", h=H)

                def rows(ap):
                    return ap.rearrange("p (h g) -> p h g", h=H)
                step(nc.vector.tensor_copy(rows(pc_row), swapped(cont)))
                step(nc.vector.tensor_copy(rows(pw_row), swapped(whole)))
                step(nc.vector.memset(pb_row, 0.0))
                step(nc.vector.tensor_tensor(rows(pb_row)[:, :, 0:GROUPS - 1], rows(pw_row)[:, :, 0:GROUPS - 1], rows(pc_row)[:, :, 1:GROUPS], ALU.mult))
                step(nc.vector.tensor_tensor(pw_row, pw_row, pc_row, ALU.mult))
                step(nc.vector.tensor_scalar(carry[0:1, :], carry[0:1, :], -1.0, BIG, ALU.add, ALU.mult))

            @block.sync
            def _(sp):
                sp.wait_ge(f_v, 3)
                sp.dma_start(penT, pen_f).then_inc(f_dma, 16)
                sp.wait_ge(f_dma, 16)

        def softmax_weights(which):
            new_stage()
            pre = which + "_sm_"
            s_in, s_st, s_ps, s_out, s_v = (sem(pre + n) for n in ("in", "st", "ps", "out", "v"))
            s_row, s_col, s_d, s_ex, s_exps, s_back = (sem(pre + n) for n in ("row", "col", "d", "ex", "exps", "back"))
            eT = scan[0][:, 0:TL]
            pen = scan[1]
            top = scan[2][:, 0:TL]
            fwd = e_all
            st = stage_T[:, 0:512]
            c_col = small[:, 300:301]
            rows = small[0:1, 0:2 * P]
            by_head = e_all.rearrange("p (g j h) -> p j g h", g=GROUPS, h=H)
            with nc.Block() as block:
                @block.sync
                def _(sp):
                    sp.dma_start(pen, penT).then_inc(s_in, 16)

                @block.scalar
                def _(act):
                    def lay(k):
                        need(act, s_ps, k)
                        nc.scalar.activation(st.rearrange("p (j g h) -> p j g h", j=4, g=GROUPS),
                                             by_head[:, bass.ds(4 * k, 4)], ACT.Copy).then_inc(s_st, 1)
                    turns(act, JC // 4, lay)
                    act.wait_ge(s_d, 1)
                    act.wait_ge(s_ps, JC // 4)

                    def exps(k):
                        need(act, s_exps, k)
                        nc.scalar.activation(st, eT[:, bass.ds(512 * k, 512)], ACT.Exp).then_inc(s_ex, 1)
                    turns(act, JC // 4, exps)

                @block.tensor
                def _(pe):
                    def lay(k):
                        pe.wait_ge(s_st, k + 1)
                        need(pe, s_out, k)
                        for q in range(4):
                            last = nc.tensor.transpose(ps[:, q * P:(q + 1) * P], st[:, q * P:(q + 1) * P], ident[:, :])
                        last.then_inc(s_ps, 1)
                    turns(pe, JC // 4, lay)
                    for d in range(2):
                        pe.wait_ge(s_v, 1 + 5 * d)
                        edge = fwd[:, TL - 1:TL] if d == 0 else top[:, 0:1]
                        nc.tensor.matmul(ps[0:1, 512:512 + P], edge, ident[:, :], start=True, stop=True).then_inc(s_row, 1)
                        pe.wait_ge(s_v, 4 + 5 * d)
                        nc.tensor.matmul(ps[:, 1024:1025], rows[:, P:2 * P], ones[0:1, 0:1], start=True, stop=True).then_inc(s_col, 1)

                    def back(k):
                        pe.wait_ge(s_ex, k + 1)
                        need(pe, s_back, k)
                        for q in range(4):
                            last = nc.tensor.transpose(ps[:, 1536 + q * P:1536 + (q + 1) * P], st[:, q * P:(q + 1) * P], ident[:, :])
                        last.then_inc(s_exps, 1)
                    turns(pe, JC // 4, back)

                @block.vector
                def _(dve):
                    def lay(k):
                        dve.wait_ge(s_ps, k + 1)
                        settle(nc.vector)
                        nc.vector.tensor_copy(eT[:, bass.ds(512 * k, 512)], ps[:, 0:512]).then_inc(s_out, 1)
                    turns(dve, JC // 4, lay)
                    dve.wait_ge(s_out, JC // 4)
                    dve.wait_ge(s_in, 16)
                    step = Chain(dve, s_v)

                    def hg(ap):
                        return ap.rearrange("p (h g) -> p h g", h=H)

                    def gh(ap):
                        return ap.rearrange("p (g h) -> p h g", h=H)
                    for d in range(2):
                        if d == 0:
                            data0, data1, res = pen[:, 0:TL], eT, fwd
                            f_row_ps, pen_row, shut = gh(ps[0:1, 512:512 + P]), pw_row, slice(0, 1)
                        else:
                            data0, data1, res = pen[:, 1:TL + 1][:, ::-1], fwd[:, ::-1], top[:, ::-1]
                            f_row_ps, pen_row, shut = gh(ps[0:1, 512:512 + P]), pb_row, slice(GROUPS - 1, GROUPS)
                        step(nc.vector.tensor_tensor_scan(res, data0, data1, -BIG, ALU.add, ALU.max))
                        dve.wait_ge(s_row, d + 1)
                        run = rows[:, 0:P]
                        step(nc.vector.tensor_copy(hg(run), f_row_ps))
                        if d == 0:
                            step(nc.vector.tensor_tensor_scan(run, pen_row, run, -BIG, ALU.add, ALU.max))
                        else:
                            step(nc.vector.tensor_tensor_scan(run[:, ::-1], pen_row[:, ::-1], run[:, ::-1], -BIG, ALU.add, ALU.max))
                        into = gh(rows[:, P:2 * P])
                        nc.vector.memset(into[:, :, shut], -BIG)
                        if d == 0:
                            step(nc.vector.tensor_tensor(into[:, :, 1:GROUPS], hg(run)[:, :, 0:GROUPS - 1], hg(pc_row)[:, :, 1:GROUPS], ALU.add))
                        else:
                            step(nc.vector.tensor_tensor(into[:, :, 0:GROUPS - 1], hg(run)[:, :, 1:GROUPS], hg(pc_row)[:, :, 1:GROUPS], ALU.add))
                        dve.wait_ge(s_col, d + 1)
                        nc.vector.tensor_copy(c_col, ps[:, 1024:1025]).then_inc(s_out, 1)
                        dve.wait_ge(s_out, JC // 4 + d + 1)
                        step(nc.vector.tensor_tensor_scan(res, data0, data1, c_col, ALU.add, ALU.max))
                    nc.vector.tensor_tensor(eT, eT, top, ALU.subtract).then_inc(s_d, 1)

                    def back(k):
                        dve.wait_ge(s_exps, k + 1)
                        settle(nc.vector)
                        nc.vector.tensor_copy(by_head[:, bass.ds(4 * k, 4)],
                                              ps[:, 1536:2048].rearrange("p (j g h) -> p j g h", j=4, g=GROUPS)).then_inc(s_back, 1)
                    turns(dve, JC // 4, back)

        class Norm:

            def __init__(self, pre, per):
                self.arg, self.root, self.per = sem(pre + "ln_arg"), sem(pre + "ln_root"), per

            def vector(self, step, r, sq, res, k, j):
                m, v, inv_std = small[:, 0:GT], small[:, 16:16 + GT], small[:, 32:32 + GT]
                step(nc.vector.tensor_reduce(m, r, AX.X, ALU.add))
                step(nc.vector.tensor_scalar(m, m, -1.0 / D, None, ALU.mult))
                step(nc.vector.tensor_tensor(r, r, bcast_last(m, D), ALU.add))
                step(nc.vector.tensor_tensor(sq, r, r, ALU.mult))
                step(nc.vector.tensor_reduce(v, sq, AX.X, ALU.add))
                step(nc.vector.tensor_scalar(v, v, 1.0 / D, EPS, ALU.mult, ALU.add))
                step.eng.sem_inc(self.arg, 1)
                step.eng.wait_ge(self.root, self.per * k + j + 1)
                step(nc.vector.tensor_tensor(res, r, bcast_last(inv_std, D), ALU.mult))

            def gpsimd(self, pool):
                def body(k):
                    for j in range(self.per):
                        pool.wait_ge(self.arg, self.per * k + j + 1)
                        nc.gpsimd.tensor_tensor(small[:, 32:32 + GT], small[:, 16:16 + GT], neg_half[:, 0:GT], ALU.pow).then_inc(self.root, 1)
                turns(pool, NG, body)

        def cols(ap, k, width=D):
            return ap[:, bass.ds(GT * width * k, GT * width)].rearrange("p (t f) -> p t f", f=width)

        def transposes(src, b):
            for i in range(GT):
                last = nc.tensor.transpose(ps[:, b * 512 + i * P:b * 512 + (i + 1) * P], src[:, i * D:(i + 1) * D], ident[:, :])
            return last

        def products(xT, weight, b, start=True, stop=True):
            for i in range(GT):
                last = nc.tensor.matmul(ps[:, b * 512 + i * D:b * 512 + (i + 1) * D], xT[:, i * P:(i + 1) * P], weight,
                                        start=start and i % 4 == 0, stop=stop, skip_group_check=True)
            return last

        def products_T(weight, xT, b, start=True, stop=True):
            for lo_c in (0, 512):
                hi_c = min(GC, lo_c + 512)
                last = nc.tensor.matmul(ps[:, b * 512 + lo_c:b * 512 + hi_c], weight, xT[:, lo_c:hi_c], start=start, stop=stop, skip_group_check=True)
            return last

        def pair(b):
            return ps[:, b * 512:b * 512 + GC]

        def table_rows(table):
            return table.rearrange("(t p) f -> p t f", p=P)

        new_stage()
        g_first = sem("g_first")
        g_dma = sem("g_dma")
        with nc.Block() as block:
            @block.vector
            def _(dve):
                nc.vector.tensor_tensor(tiled(acc_gcn), tiled(x_cur[:, :]), bcast_last(dinv[:, :], D), ALU.mult).then_inc(g_first, 1)

            @block.sync
            def _(sp):
                sp.wait_ge(g_first, 1)
                sp.dma_start(table_rows(t0), tiled(acc_gcn)).then_inc(g_dma, 16)
                sp.wait_ge(g_dma, 16)

        def convolve(which, table):
            new_stage()
            pre = which + "_"
            staged, lw_in, hot, mm = (sem(pre + n) for n in ("staged", "lw_in", "hot", "mm"))
            sums = Sums(pre, d_tile, acc_gcn, D)
            rows = arena[:, AT_BUF:AT_BUF + 16 * D].rearrange("p (s f) -> p s f", f=D)
            at = arena[:, AT_BUF + 16 * D:AT_BUF + 32 * D].rearrange("p (s f) -> p s f", f=D)
            lw_st = stage_lw[:, :].rearrange("p (s r) -> p s r", r=2)
            lw = d_lw[:, :].rearrange("p (c r) -> p c r", r=2)
            base = next_pass()

            def product(b, i):
                return ps[:, b * 1024 + i * D:b * 1024 + (i + 1) * D]
            with nc.Block() as block:
                @block.gpsimd
                def _(pool):
                    def free(k, b):
                        need(pool, mm, 2 * k + b - 1)
                    gathers(pool, table, rows, staged, free)

                @block.vector
                def _(dve):
                    sums.start(dve)
                    stage_first(d_src, staged)

                    def body(k):
                        for b in range(2):
                            n = 2 * k + b
                            stage_index(dve, d_src, staged, base, k, b)
                            settle(nc.vector)
                            nc.vector.tensor_copy(lw_st[:, 8 * b:8 * b + 8, :], lw[:, bass.ds(16 * k + 8 * b, 8), :]).then_inc(lw_in, 1)
                            adds = not isinstance(k, int) or b > 0
                            if adds:
                                sums.open(16 * k + 8 * b - 8)
                                dve.wait_ge(mm, n)
                            dve.wait_ge(lw_in, n + 1)
                            for i in range(8):
                                s = 8 * b + i
                                one_hot = nc.vector.tensor_scalar(at[:, s, :], iota_row[:, :], lw_st[:, s, 0:1], lw_st[:, s, 1:2],
                                                                  ALU.is_equal, ALU.mult)
                                if i == 7:
                                    one_hot.then_inc(hot, 1)
                                if adds:
                                    sums.add(i, product(1 - b, i))
                            if adds:
                                sums.close()
                    turns(dve, ITER, body)
                    sums.open(SC - 8)
                    dve.wait_ge(mm, HALVES)
                    for i in range(8):
                        sums.add(i, product(1, i))

                @block.tensor
                def _(pe):
                    def body(k):
                        for b in range(2):
                            n = 2 * k + b
                            pe.wait_ge(hot, n + 1)
                            need(pe, sums.drained, n - 1)
                            pe.wait_ge(landed[b], base + 128 * k + 128)
                            for i in range(8):
                                last = nc.tensor.matmul(product(b, i), at[:, 8 * b + i, :], rows[:, 8 * b + i, :], start=True, stop=True)
                            last.then_inc(mm, 1)
                    turns(pe, ITER, body)

        def scratch(o, n):
            return arena[:, o:o + n]

        convolve("c1", t0)

        new_stage()
        a_rdy, t_ps, t_sb, h_ps, n1_v, n1_dma = (sem("n1_" + n) for n in ("a", "tps", "tsb", "hps", "v", "dma"))
        A, aT, r = (scratch(AT_BUF + i * GC, GC) for i in range(3))
        with nc.Block() as block:
            @block.vector
            def _(dve):
                def body(k):
                    step = Chain(dve, n1_v, 3 * k)
                    step(nc.vector.tensor_tensor(tiled(A), cols(acc_gcn, k), bcast_last(dinv[:, bass.ds(GT * k, GT)], D), ALU.mult))
                    dve.sem_inc(a_rdy, 1)
                    dve.wait_ge(h_ps, k + 1)
                    step(nc.vector.tensor_tensor(tiled(r), tiled(pair(2)), bcast_mid(bias["L0_gnn_b1"], GT), ALU.add))
                    step(nc.vector.scalar_tensor_tensor(cols(acc_gcn, k), tiled(r), 0.0, bcast_last(dinv[:, bass.ds(GT * k, GT)], D), ALU.max, ALU.mult))
                turns(dve, NG, body)

            @block.tensor
            def _(pe):
                def body(k):
                    pe.wait_ge(a_rdy, k + 1)
                    transposes(A, 0).then_inc(t_ps, 1)
                    pe.wait_ge(t_sb, k + 1)
                    products(aT, w["L0_gnn_W1"], 2).then_inc(h_ps, 1)
                turns(pe, NG, body)

            @block.scalar
            def _(act):
                def body(k):
                    act.wait_ge(t_ps, k + 1)
                    nc.scalar.activation(aT, pair(0), ACT.Copy).then_inc(t_sb, 1)
                turns(act, NG, body)

            @block.sync
            def _(sp):
                sp.wait_ge(n1_v, 3 * NG)
                sp.dma_start(table_rows(t1), tiled(acc_gcn)).then_inc(n1_dma, 16)
                sp.wait_ge(n1_dma, 16)

        convolve("c2", t1)

        new_stage()
        a_rdy, t_ps, t_sb, h_ps, h_sb, y_ps, v_n, dma_n = (sem("n2_" + n) for n in ("a", "tps", "tsb", "hps", "hsb", "yps", "v", "dma"))
        z_rdy, zt_ps, zt_sb, xi_ps, xi_sb, uv_ps = (sem("n2_" + n) for n in ("z", "ztps", "ztsb", "xips", "xisb", "uvps"))
        norm = Norm("n2_", 2)
        A, aT, hT, r, sq = (scratch(AT_BUF + i * GC, GC) for i in range(5))
        rows2 = scratch(AT_BUF + 5 * GC, GT * (D + H)).rearrange("p (t f) -> p t f", f=D + H)
        with nc.Block() as block:
            @block.vector
            def _(dve):
                def body(k):
                    step = Chain(dve, v_n, 23 * k)
                    step(nc.vector.tensor_tensor(tiled(A), cols(acc_gcn, k), bcast_last(dinv[:, bass.ds(GT * k, GT)], D), ALU.mult))
                    dve.sem_inc(a_rdy, 1)
                    dve.wait_ge(y_ps, k + 1)
                    step(nc.vector.tensor_tensor(tiled(r), tiled(pair(4)), cols(x_cur, k), ALU.add))
                    step(nc.vector.tensor_tensor(tiled(r), tiled(r), bcast_mid(bias["L0_gnn_bfc"], GT), ALU.add))
                    norm.vector(step, tiled(r), tiled(sq), cols(x_cur, k), k, 0)
                    settle(nc.vector)
                    step(nc.vector.tensor_copy(tiled(r), cols(x_cur, k)))
                    norm.vector(step, tiled(r), tiled(sq), tiled(A), k, 1)
                    step(nc.vector.tensor_tensor(tiled(A), tiled(A), bcast_mid(bias["L1_gnn_ln_gamma"], GT), ALU.mult))
                    step(nc.vector.tensor_tensor(tiled(A), tiled(A), bcast_mid(bias["L1_gnn_ln_beta"], GT), ALU.add))
                    dve.sem_inc(z_rdy, 1)
                    dve.wait_ge(xi_ps, k + 1)
                    need(dve, dma_n, 16 * k)
                    step(nc.vector.tensor_tensor(rows2[:, :, 0:D], tiled(pair(2)), bcast_mid(bias["L1_gnn_b_in"], GT), ALU.add))
                    dve.wait_ge(uv_ps, k + 1)
                    uv = ps[:, 2048:2048 + GT * 2 * H].rearrange("p (t f) -> p t f", f=2 * H)
                    step(nc.vector.tensor_tensor(rows2[:, :, D:D + H], uv[:, :, 0:H], bcast_mid(b_u[:, :], GT), ALU.add))
                    settle(nc.vector)
                    step(nc.vector.tensor_copy(cols(v_tab, k, H), uv[:, :, H:2 * H]))
                    assert step.n == 23, step.n
                turns(dve, NG, body)

            @block.gpsimd
            def _(pool):
                norm.gpsimd(pool)

            @block.tensor
            def _(pe):
                def body(k):
                    pe.wait_ge(a_rdy, k + 1)
                    transposes(A, 0).then_inc(t_ps, 1)
                    pe.wait_ge(t_sb, k + 1)
                    products_T(w["L0_gnn_W2"], aT, 2).then_inc(h_ps, 1)
                    pe.wait_ge(h_sb, k + 1)
                    products(hT, w["L0_gnn_Wfc"], 4).then_inc(y_ps, 1)
                    pe.wait_ge(z_rdy, k + 1)
                    transposes(A, 0).then_inc(zt_ps, 1)
                    pe.wait_ge(zt_sb, k + 1)
                    products_T(w["L1_gnn_W_in"], aT, 6)
                    products(aT, w["L1_gnn_W_in"], 2).then_inc(xi_ps, 1)
                    pe.wait_ge(xi_sb, k + 1)
                    for i in range(GT):
                        last = nc.tensor.matmul(ps[:, 2048 + i * 2 * H:2048 + (i + 1) * 2 * H], hT[:, i * P:(i + 1) * P], w_uv[:, :], start=True, stop=True)
                    last.then_inc(uv_ps, 1)
                turns(pe, NG, body)

            @block.scalar
            def _(act):
                def body(k):
                    act.wait_ge(t_ps, k + 1)
                    nc.scalar.activation(aT, pair(0), ACT.Copy).then_inc(t_sb, 1)
                    act.wait_ge(h_ps, k + 1)
                    nc.scalar.activation(hT, pair(2), ACT.Relu, bias=col["L0_gnn_b2"]).then_inc(h_sb, 1)
                    act.wait_ge(zt_ps, k + 1)
                    nc.scalar.activation(aT, pair(0), ACT.Copy).then_inc(zt_sb, 1)
                    act.wait_ge(xi_ps, k + 1)
                    nc.scalar.activation(hT, pair(6), ACT.Identity, bias=col["L1_gnn_b_in"]).then_inc(xi_sb, 1)
                turns(act, NG, body)

            @block.sync
            def _(sp):
                def body(k):
                    sp.wait_ge(v_n, 23 * k + 23)
                    sp.dma_start(table_rows(t2)[:, bass.ds(GT * k, GT), :], rows2).then_inc(dma_n, 16)
                turns(sp, NG, body)
                sp.wait_ge(dma_n, 16 * NG)

        def score_pass(which, idx, table, width, keep, tab, tab_w):
            new_stage()
            pre = which + "_"
            staged, oT_hot, exp_ps, scored, v_s = (sem(pre + n) for n in ("staged", "hot", "expps", "scored", "v"))
            lo_in = [sem(pre + "lo0"), sem(pre + "lo1")]
            spilled = [sem(pre + "sp0"), sem(pre + "sp1")]
            gat = which == "gat"
            o = AT_BUF
            rows = arena[:, o:o + 16 * width].rearrange("p (s f) -> p s f", f=width)
            o += 16 * width
            if gat:
                o = AT_BUF + 16 * (D + H)
            lo_b = arena[:, o:o + 2048].rearrange("p (b c) -> p b c", b=2)
            hot_T = (arena[:, o + 2048:o + 4096] if gat else arena[:, AT_ACC + 2048:AT_ACC + 4096]).rearrange("p (b c) -> p b c", b=2)
            prod = arena[:, AT_ACC:AT_ACC + 2048].rearrange("p (b c) -> p b c", b=4)
            assert o + 2048 <= AW
            base = next_pass()
            lo_rows = d_loT.rearrange("(n c) e -> n (c e)", c=8)
            steps = 2 if gat else 4
            with nc.Block() as block:
                @block.gpsimd
                def _(pool):
                    def free(k, b):
                        need(pool, scored, 2 * k + b - 1)
                        need(pool, spilled[b], 16 * k)
                    gathers(pool, table, rows, staged, free)

                @block.sync
                def _(sp):
                    def body(k):
                        for b in range(2):
                            n = 2 * k + b
                            need(sp, oT_hot, n - 1)
                            sp.dma_start(lo_b[:, b, :], lo_rows[bass.ds(n, 1), :].to_broadcast([P, 8 * P])).then_inc(lo_in[b], 16)
                    turns(sp, ITER, body)

                @block.scalar
                def _(act):
                    def body(k):
                        for b in range(2):
                            n = 2 * k + b
                            act.wait_ge(landed[b], base + 128 * k + 128)
                            act.dma_start(spill[bass.ds(n, 1)].rearrange("o p (c f) -> p (o c) f", f=D),
                                          rows[:, 8 * b:8 * b + 8, keep:keep + D]).then_inc(spilled[b], 16)
                    turns(act, ITER, body)
                    for b in range(2):
                        act.wait_ge(spilled[b], 16 * ITER)

                @block.tensor
                def _(pe):
                    regs = registers(pe, pre + "tile")

                    def body(k):
                        for b in range(2):
                            n = 2 * k + b
                            tiles = tile_numbers(pe, regs, d_tile, 16 * k + 8 * b)
                            need(pe, scored, n - 1)
                            pe.wait_ge(oT_hot, n + 1)
                            for i in range(8):
                                o_ps = b * 1024 + i * tab_w
                                last = nc.tensor.matmul(ps[:, o_ps:o_ps + tab_w], hot_T[:, b, i * P:(i + 1) * P],
                                                        tab[:, bass.ds(tiles[i] * tab_w, tab_w)], start=True, stop=True)
                            last.then_inc(exp_ps, 1)
                    turns(pe, ITER, body)

                @block.vector
                def _(dve):
                    stage_first(idx, staged)

                    def body(k):
                        for b in range(2):
                            n = 2 * k + b
                            step = Chain(dve, v_s, steps * n)
                            stage_index(dve, idx, staged, base, k, b)
                            dve.wait_ge(lo_in[b], 16 * k + 16)
                            nc.vector.tensor_scalar(hot_T[:, b, :], lo_b[:, b, :], iota_part[:, 0:1], None, ALU.is_equal).then_inc(oT_hot, 1)
                            dve.wait_ge(landed[b], base + 128 * k + 128)
                            dve.wait_ge(exp_ps, n + 1)
                            e_out = e_all[:, bass.ds(64 * n, 64)]
                            if gat:
                                raw = prod[:, b, 0:64].rearrange("p (c h) -> p c h", h=H)
                                step(nc.vector.tensor_tensor(raw, ps[:, b * 1024:b * 1024 + 64].rearrange("p (c h) -> p c h", h=H),
                                                             rows[:, 8 * b:8 * b + 8, D:D + H], ALU.add))
                                step(nc.vector.scalar_tensor_tensor(e_out, prod[:, b, 0:64], 0.2, prod[:, b, 0:64], ALU.mult, ALU.max))
                            else:
                                for z in range(2):
                                    pr = prod[:, 2 * b + z, :]
                                    step(nc.vector.tensor_tensor(tiled(pr), tiled(ps[:, b * 1024 + z * 512:b * 1024 + z * 512 + 512]),
                                                                 rows[:, 8 * b + 4 * z:8 * b + 4 * z + 4, 0:D], ALU.mult))
                                    step(nc.vector.tensor_reduce(e_out[:, 32 * z:32 * z + 32], pr.rearrange("p (c d) -> p c d", d=DK), AX.X, ALU.add))
                            dve.sem_inc(scored, 1)
                    turns(dve, ITER, body)

        def weigh_pass(which, head_last):
            new_stage()
            pre = which + "_w_"
            W = D + H
            msg, mm, msg_v, zero, hot = (sem(pre + n) for n in ("msg", "mm", "v", "zero", "hot"))
            back_in = [sem(pre + "in0"), sem(pre + "in1")]
            sums = Sums(pre, d_tile, acc_att, W)
            rows = arena[:, AT_Q:AT_Q + 2048].rearrange("p (b c) -> p b c", b=2)
            at = arena[:, AT_Q + 2048:AT_Q + 4096].rearrange("p (b c n) -> p b c n", b=2, c=8)
            m = arena[:, AT_Q + 4096:AT_Q + 4096 + 16 * W].rearrange("p (b c f) -> p b c f", b=2, c=8)
            lw = d_lw[:, :].rearrange("p (c r) -> p c r", r=2)

            def product(b, i):
                o = b * 2048 + i // 3 * 512 + i % 3 * W
                return ps[:, o:o + W]
            with nc.Block() as block:
                @block.sync
                def _(sp):
                    def body(k):
                        for b in range(2):
                            n = 2 * k + b
                            need(sp, msg, n - 1)
                            sp.dma_start(rows[:, b, :], spill[bass.ds(n, 1)].rearrange("o p c -> p (o c)")).then_inc(back_in[b], 16)
                    turns(sp, ITER, body)

                @block.scalar
                def _(act):
                    def body(k):
                        for b in range(2):
                            n = 2 * k + b
                            need(act, mm, n - 1)
                            nc.scalar.activation(m[:, b, :, D:W], e_all[:, bass.ds(64 * n, 64)].rearrange("p (c h) -> p c h", h=H), ACT.Copy).then_inc(msg_v, 1)
                    turns(act, ITER, body)

                @block.gpsimd
                def _(pool):
                    def body(k):
                        for b in range(2):
                            n = 2 * k + b
                            need(pool, mm, n - 1)
                            pool.wait_ge(back_in[b], 16 * k + 16)
                            for i in range(8):
                                ex = e_all[:, bass.ds(64 * n + 8 * i, 8)]
                                if head_last:
                                    out_m = m[:, b, i, 0:D].rearrange("p (d h) -> p d h", h=H)
                                    in_m = rows[:, b, i * D:(i + 1) * D].rearrange("p (d h) -> p d h", h=H)
                                    ex = bcast_mid(ex, DK)
                                else:
                                    out_m = m[:, b, i, 0:D].rearrange("p (h d) -> p h d", h=H)
                                    in_m = rows[:, b, i * D:(i + 1) * D].rearrange("p (h d) -> p h d", h=H)
                                    ex = bcast_last(ex, DK)
                                last = nc.gpsimd.tensor_tensor(out_m, in_m, ex, ALU.mult)
                            last.then_inc(msg, 1)
                    turns(pool, ITER, body)

                @block.tensor
                def _(pe):
                    def body(k):
                        for b in range(2):
                            n = 2 * k + b
                            pe.wait_ge(hot, n + 1)
                            need(pe, sums.drained, n - 1)
                            pe.wait_ge(msg_v, n + 1)
                            pe.wait_ge(msg, n + 1)
                            for i in range(8):
                                last = nc.tensor.matmul(product(b, i), at[:, b, i], m[:, b, i], start=True, stop=True)
                            last.then_inc(mm, 1)
                    turns(pe, ITER, body)

                @block.vector
                def _(dve):
                    sums.start(dve)
                    nc.vector.memset(acc_att, 0.0).then_inc(zero, 1)
                    dve.wait_ge(zero, 1)

                    def body(k):
                        for b in range(2):
                            n = 2 * k + b
                            adds = not isinstance(k, int) or b > 0
                            nc.vector.tensor_tensor(at[:, b], bcast_mid(iota_row[:, :], 8), bcast_last(lw[:, bass.ds(8 * n, 8), 0], P), ALU.is_equal).then_inc(hot, 1)
                            if adds:
                                sums.open(16 * k + 8 * b - 8)
                                dve.wait_ge(mm, n)
                                for i in range(8):
                                    sums.add(i, product(1 - b, i))
                                sums.close()
                    turns(dve, ITER, body)
                    sums.open(SC - 8)
                    dve.wait_ge(mm, HALVES)
                    for i in range(8):
                        sums.add(i, product(1, i))

        score_pass("gat", d_src, t2, D + H, 0, v_tab, H)
        softmax_weights("gat")
        weigh_pass("gat", True)

        new_stage()
        wt_in, wt_v, wt_blk = sem("wt_in"), sem("wt_v"), sem("wt_blk")
        basis = {n: scratch(AT_Q + i * NB * D, NB * D).rearrange("p (b o) -> p b o", b=NB) for i, n in enumerate("akqv")}
        comp = {n: scratch(AT_Q + 16 * D + i * TN * NB, TN * NB).rearrange("p (t b) -> p t b", b=NB) for i, n in enumerate("akqv")}
        w_tmp = scratch(AT_Q + 20 * D, TN * D).rearrange("p (t o) -> p t o", t=TN)
        pri = scratch(AT_Q + 30 * D, TN * H)
        with nc.Block() as block:
            @block.sync
            def _(sp):
                for n in "akqv":
                    sp.dma_start(basis[n], t["L2_gnn_w_basis_" + n].rearrange("b (i o) -> i b o", o=D)).then_inc(wt_in, 16)
                    sp.dma_start(comp[n].rearrange("p t b -> p (t b)"), t["L2_gnn_w_comp_" + n].rearrange("t b -> (t b)").partition_broadcast(P)).then_inc(wt_in, 16)
                sp.dma_start(pri, t["L2_gnn_relation_pri"].rearrange("t h -> (t h)").partition_broadcast(P)).then_inc(wt_in, 16)
                sp.wait_ge(wt_v, 2)
                for n in ("att", "msg"):
                    for h in range(H):
                        sp.dma_start(rel[n][h * DK:(h + 1) * DK, :].rearrange("p (t o) -> p t o", t=TN)[:, :, h * DK:(h + 1) * DK],
                                     t["L2_gnn_relation_" + n][:, h].rearrange("t i j -> i t j")).then_inc(wt_blk, 16)
                sp.wait_ge(wt_blk, 16 * 2 * H)

            @block.vector
            def _(dve):
                step = Chain(dve, wt_v)
                step(nc.vector.memset(rel["att"], 0.0))
                step(nc.vector.memset(rel["msg"], 0.0))
                dve.wait_ge(wt_in, 16 * 9)
                for n in "akqv":
                    for b in range(NB):
                        res = w_typed[n] if b == 0 else w_tmp
                        step(nc.vector.tensor_tensor(res, bcast_mid(basis[n][:, b, :], TN), bcast_last(comp[n][:, :, b], D), ALU.mult))
                        if b:
                            step(nc.vector.tensor_tensor(w_typed[n], w_typed[n], w_tmp, ALU.add))
                dve.wait_ge(wt_blk, 16 * 2 * H)
                step(nc.vector.tensor_scalar(pri, pri, DK ** -0.5, None, ALU.mult))
                att = rel["att"].rearrange("p (c j) -> p c j", j=DK)
                step(nc.vector.tensor_tensor(att, att, bcast_last(pri, DK), ALU.mult))

        def load_types(sp, done):
            sp.dma_start(ntb[:, 0:N], t["node_type_8"].partition_broadcast(P)).then_inc(done, 16)

        def attention_out(step, k, out_ap, head_last):
            den = small[:, 64:64 + GT * H].rearrange("p (t h) -> p t h", h=H)
            acc = cols(acc_att, k, D + H)
            step(nc.vector.tensor_scalar(den, acc[:, :, D:D + H], 1e-30, None, ALU.max))
            step(nc.vector.reciprocal(den, den))
            if head_last:
                step(nc.vector.tensor_tensor(out_ap.rearrange("p (t d h) -> p t d h", t=GT, h=H), acc[:, :, 0:D].rearrange("p t (d h) -> p t d h", h=H),
                                             den.unsqueeze(2).to_broadcast([P, GT, DK, H]), ALU.mult))
            else:
                step(nc.vector.tensor_tensor(out_ap.rearrange("p (t h d) -> p t h d", t=GT, h=H), acc[:, :, 0:D].rearrange("p t (h d) -> p t h d", h=H),
                                             den.unsqueeze(3).to_broadcast([P, GT, H, DK]), ALU.mult))

        new_stage()
        a_rdy, t_ps, t_sb, y_ps, x_rdy, xt_ps, xt_sb, xm_rdy, xm_used, v_n = (sem("n3_" + n) for n in (
            "a", "tps", "tsb", "yps", "x", "xtps", "xtsb", "xm", "xmused", "v"))
        kv_sb, q_sb, kv_ps, k_out, v_out, nt_in, nt_pad = (sem("n3_" + n) for n in ("kvsb", "qsb", "kvps", "kout", "vout", "nt", "ntpad"))
        kv_dma = [sem("n3_dma0"), sem("n3_dma1")]
        norm = Norm("n3_", 1)
        S = [scratch(AT_BUF + i * GC, GC) for i in range(5)]
        A, aT, r, sq, x2T = S
        kT, vT, xm = S[0], S[1], [S[2], S[3]]
        kv_st = scratch(AT_BUF + 5 * GC, 2 * 1024).rearrange("p (z t f) -> p z t f", z=2, f=2 * D)
        t3_rows = t3.rearrange("(t n) f -> n t f", t=TN)
        with nc.Block() as block:
            @block.sync
            def _(sp):
                sp.wait_ge(nt_pad, 1)
                load_types(sp, nt_in)

                def body(k):
                    for i in range(GT):
                        for z in range(2):
                            n = 2 * GT * k + 2 * i + z
                            sp.wait_ge(k_out, n + 1)
                            sp.wait_ge(v_out, n + 1)
                            sp.dma_start(t3_rows[bass.ds(P * (GT * k + i), P), 4 * z:4 * z + 4, :], kv_st[:, z]).then_inc(kv_dma[z], 16)
                turns(sp, NG, body)
                for z in range(2):
                    sp.wait_ge(kv_dma[z], 16 * GT * NG)

            @block.gpsimd
            def _(pool):
                norm.gpsimd(pool)

            @block.vector
            def _(dve):
                nc.vector.memset(ntb[:, N:NP], 0).then_inc(nt_pad, 1)

                def body(k):
                    step = Chain(dve, v_n, 14 * k)
                    attention_out(step, k, A, True)
                    dve.sem_inc(a_rdy, 1)
                    dve.wait_ge(y_ps, k + 1)
                    need(dve, xm_used, 8 * k)
                    step(nc.vector.tensor_tensor(tiled(r), tiled(pair(2)), cols(x_cur, k), ALU.add))
                    step(nc.vector.tensor_tensor(tiled(r), tiled(r), bcast_mid(bias["L1_gnn_b_ff"], GT), ALU.add))
                    norm.vector(step, tiled(r), tiled(sq), tiled(sq), k, 0)
                    dve.sem_inc(x_rdy, 1)
                    settle(nc.vector)
                    step(nc.vector.tensor_copy(cols(x_cur, k), tiled(sq)))
                    dve.wait_ge(xt_sb, k + 1)
                    if isinstance(k, int):
                        dve.wait_ge(nt_in, 16)
                    for ty in range(TN):
                        if ty >= 2:
                            dve.wait_ge(xm_used, TN * k + ty - 1)
                        nc.vector.scalar_tensor_tensor(xm[ty % 2], ntb[:, bass.ds(GC * k, GC)], float(ty), x2T, ALU.is_equal, ALU.mult).then_inc(xm_rdy, 1)
                    dve.wait_ge(xm_used, TN * k + TN)
                    settle(nc.vector)
                    step(nc.vector.tensor_copy(q_tab[:, bass.ds(GC * k, GC)], pair(6)))
                    dve.sem_inc(q_sb, 1)
                    assert step.n == 14, step.n
                    for i in range(GT):
                        for z in range(2):
                            n = 2 * GT * k + 2 * i + z
                            dve.wait_ge(kv_ps, GT * k + i + 1)
                            need(dve, kv_dma[z], 16 * (GT * k + i))
                            b = 4 * (i % 2) + 2 + z
                            nc.vector.tensor_copy(kv_st[:, z, :, D:2 * D], tiled(bank(b))).then_inc(v_out, 1)
                turns(dve, NG, body)

            @block.tensor
            def _(pe):
                def body(k):
                    pe.wait_ge(a_rdy, k + 1)
                    need(pe, v_out, 2 * GT * k)
                    need(pe, k_out, 2 * GT * k)
                    transposes(A, 0).then_inc(t_ps, 1)
                    pe.wait_ge(t_sb, k + 1)
                    products(aT, w["L1_gnn_W_ff"], 2).then_inc(y_ps, 1)
                    pe.wait_ge(x_rdy, k + 1)
                    for i in range(GT):
                        tile = sq[:, i * D:(i + 1) * D]
                        last = nc.tensor.transpose(ps[:, i * P:(i + 1) * P], tile, ident[:, :])
                    last.then_inc(xt_ps, 1)
                    for ty in range(TN):
                        pe.wait_ge(xm_rdy, TN * k + ty + 1)
                        f = dict(start=ty == 0, stop=ty == TN - 1)
                        products_T(w_typed["k"][:, ty, :], xm[ty % 2], 2, **f)
                        products_T(w_typed["v"][:, ty, :], xm[ty % 2], 4, **f)
                        products(xm[ty % 2], w_typed["q"][:, ty, :], 6, **f).then_inc(xm_used, 1)
                    pe.wait_ge(kv_sb, 2 * k + 2)
                    pe.wait_ge(q_sb, k + 1)
                    for i in range(GT):
                        if i >= 2:
                            pe.wait_ge(k_out, 2 * GT * k + 2 * (i - 1))
                            pe.wait_ge(v_out, 2 * GT * k + 2 * (i - 1))
                        for src_T, name, b in ((kT, "att", 4 * (i % 2)), (vT, "msg", 4 * (i % 2) + 2)):
                            for z in range(2):
                                last = nc.tensor.matmul(bank(b + z), src_T[:, i * P:(i + 1) * P], rel[name][:, z * 512:(z + 1) * 512], start=True, stop=True)
                        last.then_inc(kv_ps, 1)
                turns(pe, NG, body)

            @block.scalar
            def _(act):
                def body(k):
                    act.wait_ge(t_ps, k + 1)
                    nc.scalar.activation(aT, pair(0), ACT.Copy).then_inc(t_sb, 1)
                    act.wait_ge(xt_ps, k + 1)
                    nc.scalar.activation(x2T, pair(0), ACT.Copy).then_inc(xt_sb, 1)
                    act.wait_ge(xm_used, TN * k + TN)
                    nc.scalar.activation(kT, pair(2), ACT.Copy).then_inc(kv_sb, 1)
                    nc.scalar.activation(vT, pair(4), ACT.Copy).then_inc(kv_sb, 1)
                    for i in range(GT):
                        for z in range(2):
                            act.wait_ge(kv_ps, GT * k + i + 1)
                            need(act, kv_dma[z], 16 * (GT * k + i))
                            nc.scalar.activation(kv_st[:, z, :, 0:D], tiled(bank(4 * (i % 2) + z)), ACT.Copy).then_inc(k_out, 1)
                turns(act, NG, body)

        score_pass("hgt", d_typed, t3, 2 * D, D, q_tab, D)
        softmax_weights("hgt")
        weigh_pass("hgt", False)

        AT_L3 = 21000
        acc_l3 = arena[:, AT_L3:AT_L3 + NT * 2 * D]
        U_T, W_T, VDE = l3_T[:, 0:D], l3_T[:, D:2 * D], l3_T[:, 2 * D:6 * D]
        new_stage()
        a_rdy, t_ps, t_sb, xm_rdy, xm_used, o_ps, x_rdy, v_n = (sem("n4_" + n) for n in ("a", "tps", "tsb", "xm", "xmused", "ops", "x", "v"))
        xt_ps, xt_sb, h_ps, h_sb, w_ps, vde_ps, vde_used, nt_in, nt_pad, rows_rdy = (sem("n4_" + n) for n in (
            "xtps", "xtsb", "hps", "hsb", "wps", "vdeps", "vdeused", "nt", "ntpad", "rows"))
        dma_n = sem("n4_dma")
        norm = Norm("n4_", 1)
        rows4 = scratch(1024, GT * 3 * D).rearrange("p (t f) -> p t f", f=3 * D)
        xm = [scratch(1024, GC), scratch(1024 + GC, GC)]
        A, aT, sq = scratch(3712, GC), scratch(3712 + GC, GC), scratch(3712 + 2 * GC, GC)
        r = scratch(19720, GC)
        x2T, x3T, hT = sq, aT, A
        p_st, d_st = r, sq
        with nc.Block() as block:
            @block.sync
            def _(sp):
                sp.wait_ge(nt_pad, 1)
                load_types(sp, nt_in)

                def body(k):
                    sp.wait_ge(rows_rdy, k + 1)
                    sp.dma_start(table_rows(t4)[:, bass.ds(GT * k, GT), :], rows4).then_inc(dma_n, 16)
                    sp.dma_start(p_dram[:, bass.ds(GC * k, GC)], p_st).then_inc(dma_n, 16)
                    sp.dma_start(dp_dram[:, bass.ds(GC * k, GC)], d_st).then_inc(dma_n, 16)
                turns(sp, NG, body)
                sp.wait_ge(dma_n, 48 * NG)

            @block.gpsimd
            def _(pool):
                norm.gpsimd(pool)

            @block.vector
            def _(dve):
                nc.vector.memset(ntb[:, N:NP], 0).then_inc(nt_pad, 1)
                PER = 3 + 1 + 2 + 8 + 2 + 5 * GT + 4

                def body(k):
                    step = Chain(dve, v_n, PER * k)
                    inv_b = bcast_last(inv[:, bass.ds(GT * k, GT)], D)
                    attention_out(step, k, A, False)
                    need(dve, dma_n, 48 * k)
                    settle(nc.vector)
                    step(nc.vector.tensor_copy(tiled(sq), cols(x_cur, k)))
                    dve.sem_inc(a_rdy, 1)
                    dve.wait_ge(t_sb, 2 * k + 2)
                    if isinstance(k, int):
                        dve.wait_ge(nt_in, 16)
                    for ty in range(TN):
                        if ty >= 2:
                            dve.wait_ge(xm_used, TN * k + ty - 1)
                        nc.vector.scalar_tensor_tensor(xm[ty % 2], ntb[:, bass.ds(GC * k, GC)], float(ty), aT, ALU.is_equal, ALU.mult).then_inc(xm_rdy, 1)
                    dve.wait_ge(o_ps, k + 1)
                    step(nc.vector.tensor_tensor(tiled(r), tiled(pair(2)), bcast_mid(bias["L2_gnn_bias"], GT), ALU.add))
                    step(nc.vector.scalar_tensor_tensor(tiled(r), tiled(r), 0.0, cols(x_cur, k), ALU.max, ALU.add))
                    norm.vector(step, tiled(r), tiled(sq), tiled(sq), k, 0)
                    dve.sem_inc(x_rdy, 1)
                    settle(nc.vector)
                    step(nc.vector.tensor_copy(cols(x_cur, k), tiled(sq)))
                    dve.wait_ge(w_ps, k + 1)
                    y = rows4[:, :, 2 * D:3 * D]
                    step(nc.vector.tensor_tensor(y, tiled(pair(2)), bcast_mid(bias["L3_gnn_W_b"], GT), ALU.add))
                    step(nc.vector.tensor_tensor(y, y, inv_b, ALU.mult))
                    for i in range(GT):
                        dve.wait_ge(vde_ps, GT * k + i + 1)
                        b = 6 + i % 2
                        z = rows4[:, i, D:2 * D]
                        part = [ps[:, b * 512 + j * D:b * 512 + (j + 1) * D] for j in range(4)]
                        step(nc.vector.tensor_tensor(p_st[:, i * D:(i + 1) * D], part[0], bias["L3_gnn_V_b"], ALU.add))
                        step(nc.vector.tensor_copy(rows4[:, i, 0:D], part[1]))
                        step(nc.vector.tensor_tensor(d_st[:, i * D:(i + 1) * D], part[2], bias["L3_gnn_D_b"], ALU.add))
                        step(nc.vector.tensor_tensor(z, part[3], bias["L3_gnn_E_b"], ALU.add))
                        dve.sem_inc(vde_used, 1)
                        step(nc.vector.tensor_tensor(z, z, rows4[:, i, 2 * D:3 * D], ALU.mult))
                    dve.sem_inc(rows_rdy, 1)
                    acc = cols(acc_l3, k, 2 * D)
                    step(nc.vector.tensor_tensor(acc[:, :, 0:D], tiled(p_st), rows4[:, :, 0:D], ALU.add))
                    step(nc.vector.scalar_tensor_tensor(acc[:, :, 0:D], acc[:, :, 0:D], 0.0, y, ALU.max, ALU.mult))
                    step(nc.vector.tensor_tensor(acc[:, :, 0:D], acc[:, :, 0:D], rows4[:, :, D:2 * D], ALU.add))
                    step(nc.vector.tensor_copy(acc[:, :, D:2 * D], y))
                    assert step.n == PER, (step.n, PER)
                turns(dve, NG, body)

            @block.tensor
            def _(pe):
                def body(k):
                    pe.wait_ge(a_rdy, k + 1)
                    transposes(A, 0).then_inc(t_ps, 1)
                    for i in range(GT):
                        last = nc.tensor.transpose(ps[:, 2048 + i * P:2048 + (i + 1) * P], sq[:, i * D:(i + 1) * D], ident[:, :])
                    last.then_inc(t_ps, 1)
                    for ty in range(TN):
                        pe.wait_ge(xm_rdy, TN * k + ty + 1)
                        products(xm[ty % 2], w_typed["a"][:, ty, :], 2, start=ty == 0, stop=False).then_inc(xm_used, 1)
                    products(x2T, w["L2_gnn_loop_weight"], 2, start=False, stop=True).then_inc(o_ps, 1)
                    pe.wait_ge(x_rdy, k + 1)
                    for i in range(GT):
                        last = nc.tensor.transpose(ps[:, i * P:(i + 1) * P], sq[:, i * D:(i + 1) * D], ident[:, :])
                    last.then_inc(xt_ps, 1)
                    pe.wait_ge(xt_sb, k + 1)
                    products_T(U_T, x3T, 4).then_inc(h_ps, 1)
                    products(x3T, W_T, 2).then_inc(w_ps, 1)
                    pe.wait_ge(h_sb, k + 1)
                    for i in range(GT):
                        need(pe, vde_used, GT * k + i - 1)
                        nc.tensor.matmul(bank(6 + i % 2), hT[:, i * P:(i + 1) * P], VDE, start=True, stop=True).then_inc(vde_ps, 1)
                turns(pe, NG, body)

            @block.scalar
            def _(act):
                def body(k):
                    act.wait_ge(t_ps, 2 * k + 1)
                    nc.scalar.activation(aT, pair(0), ACT.Copy).then_inc(t_sb, 1)
                    act.wait_ge(t_ps, 2 * k + 2)
                    nc.scalar.activation(x2T, pair(4), ACT.Copy).then_inc(t_sb, 1)
                    act.wait_ge(xt_ps, k + 1)
                    nc.scalar.activation(x3T, pair(0), ACT.Copy).then_inc(xt_sb, 1)
                    act.wait_ge(h_ps, k + 1)
                    nc.scalar.activation(hT, pair(4), ACT.Identity, bias=col["L3_gnn_U_b"]).then_inc(h_sb, 1)
                turns(act, NG, body)

        new_stage()
        staged, oT_hot, hot, p_ps, mm, v_s = (sem("l3_" + n) for n in ("staged", "hotT", "hot", "pps", "mm", "v"))
        lo_in = [sem("l3_lo0"), sem("l3_lo1")]
        p_in, a_abs, minus = sem("l3_p_in"), sem("l3_abs"), sem("l3_minus")
        sums = Sums("l3_", s_tile, acc_l3, 2 * D)
        p_tab = arena[:, 1024:1024 + NP]
        o = 1024 + NP
        rows = arena[:, o:o + 16 * 3 * D].rearrange("p (s f) -> p s f", f=3 * D)
        o += 16 * 3 * D
        lo_b = arena[:, o:o + 2048].rearrange("p (b c) -> p b c", b=2)
        o += 2048
        hot_T = arena[:, o:o + 2048].rearrange("p (b c) -> p b c", b=2)
        o += 2048
        at = arena[:, o:o + 2048].rearrange("p (b c n) -> p b c n", b=2, c=8)
        o += 2048
        prod = arena[:, o:o + 1024].rearrange("p (z c) -> p z c", z=2)
        o += 1024
        minus_part = small[:, 0:1]
        assert o <= AT_L3, o
        base = next_pass()
        lo_rows = s_loT.rearrange("(n c) e -> n (c e)", c=8)

        def product(i):
            return ps[:, 2048 + i * 2 * D:2048 + (i + 1) * 2 * D]
        with nc.Block() as block:
            @block.gpsimd
            def _(pool):
                def free(k, b):
                    need(pool, mm, 4 * k + 2 * b - 2)
                gathers(pool, t4, rows, staged, free)

            @block.sync
            def _(sp):
                sp.dma_start(p_tab, p_dram).then_inc(p_in, 16)

                def body(k):
                    for b in range(2):
                        n = 2 * k + b
                        need(sp, oT_hot, n - 1)
                        sp.dma_start(lo_b[:, b, :], lo_rows[bass.ds(n, 1), :].to_broadcast([P, 8 * P])).then_inc(lo_in[b], 16)
                turns(sp, ITER, body)

            @block.scalar
            def _(act):
                act.wait_ge(minus, 1)

                def body(k):
                    for b in range(2):
                        n = 2 * k + b
                        need(act, p_ps, 2 * n - 2)
                        act.wait_ge(lo_in[b], 16 * k + 16)
                        nc.scalar.activation(hot_T[:, b, :], lo_b[:, b, :], ACT.Abs, bias=minus_part).then_inc(a_abs, 1)
                        act.wait_ge(a_abs, n + 1)
                        nc.scalar.activation(hot_T[:, b, :], hot_T[:, b, :], ACT.Relu, bias=ones[:, 0:1], scale=-1.0).then_inc(oT_hot, 1)
                turns(act, ITER, body)

            @block.tensor
            def _(pe):
                regs = registers(pe, "l3_p_tile")
                pe.wait_ge(p_in, 16)

                def expand(k, b):
                    n = 2 * k + b
                    tiles = tile_numbers(pe, regs, s_tile, 16 * k + 8 * b)
                    pe.wait_ge(oT_hot, n + 1)
                    need(pe, v_s, 4 * n - 4)
                    for i in range(8):
                        o_ps = b * 1024 + i * D
                        last = nc.tensor.matmul(ps[:, o_ps:o_ps + D], hot_T[:, b, i * P:(i + 1) * P],
                                                p_tab[:, bass.ds(tiles[i] * D, D)], start=True, stop=True)
                        if i % 4 == 3:
                            last.then_inc(p_ps, 1)

                def sum_up(k, b):
                    n = 2 * k + b
                    pe.wait_ge(hot, n + 1)
                    need(pe, sums.drained, n)
                    for i in range(8):
                        if i % 4 == 0:
                            pe.wait_ge(v_s, 4 * n + i // 2 + 2)
                        nc.tensor.matmul(product(i), at[:, b, i], rows[:, 8 * b + i, D:3 * D], start=i % 2 == 0, stop=False, skip_group_check=True)
                        last = nc.tensor.matmul(product(i)[:, 0:D], at[:, b, i], prod[:, i // 4, (i % 4) * D:(i % 4 + 1) * D],
                                                start=False, stop=True, skip_group_check=True)
                        if i % 4 == 3:
                            last.then_inc(mm, 1)

                def body(k):
                    for b in range(2):
                        expand(k, b)
                        sum_up(k, b)
                turns(pe, ITER, body)

            @block.vector
            def _(dve):
                sums.start(dve)
                nc.vector.tensor_scalar(minus_part, iota_part[:, 0:1], -1.0, None, ALU.mult).then_inc(minus, 1)
                stage_first(s_dst, staged)

                def body(k):
                    for b in range(2):
                        n = 2 * k + b
                        step = Chain(dve, v_s, 4 * n)
                        adds = not isinstance(k, int) or b > 0
                        stage_index(dve, s_dst, staged, base, k, b)
                        nc.vector.tensor_tensor(at[:, b], bcast_mid(iota_row[:, :], 8), bcast_last(s_lo[:, bass.ds(8 * n, 8)], P), ALU.is_equal).then_inc(hot, 1)
                        if adds:
                            sums.open(16 * k + 8 * b - 8)
                            for z in range(2):
                                dve.wait_ge(mm, 2 * n - 1 + z)
                                for i in range(4 * z, 4 * z + 4):
                                    sums.add(i, product(i))
                            sums.close()
                        dve.wait_ge(landed[b], base + 128 * k + 128)
                        for z in range(2):
                            dve.wait_ge(p_ps, 2 * n + z + 1)
                            got = rows[:, 8 * b + 4 * z:8 * b + 4 * z + 4, :]
                            pr = tiled(prod[:, z, :])
                            step(nc.vector.tensor_tensor(pr, tiled(ps[:, b * 1024 + z * 512:b * 1024 + z * 512 + 512]), got[:, :, 0:D], ALU.add))
                            step(nc.vector.scalar_tensor_tensor(pr, pr, 0.0, got[:, :, 2 * D:3 * D], ALU.max, ALU.mult))
                turns(dve, ITER, body)
                sums.open(SC - 8)
                for i in range(8):
                    if i % 4 == 0:
                        dve.wait_ge(mm, 2 * HALVES - 1 + i // 4)
                    sums.add(i, product(i))

        new_stage()
        dp_in, v_n, out_dma = sem("n5_dp"), sem("n5_v"), sem("n5_out")
        norm = Norm("n5_", 1)
        dp_all = arena[:, 1024:1024 + NP]
        r, sq = scratch(8192, GC), scratch(8192 + GC, GC)
        with nc.Block() as block:
            @block.gpsimd
            def _(pool):
                norm.gpsimd(pool)

            @block.vector
            def _(dve):
                dve.wait_ge(dp_in, 16)

                def body(k):
                    step = Chain(dve, v_n, 11 * k)
                    acc = cols(acc_l3, k, 2 * D)
                    step(nc.vector.tensor_tensor(tiled(r), cols(dp_all, k), acc[:, :, D:2 * D], ALU.mult))
                    step(nc.vector.tensor_tensor(tiled(r), tiled(r), acc[:, :, 0:D], ALU.add))
                    step(nc.vector.tensor_tensor(tiled(r), tiled(r), bcast_last(inv[:, bass.ds(GT * k, GT)], D), ALU.mult))
                    step(nc.vector.tensor_tensor(tiled(r), tiled(r), cols(x_cur, k), ALU.add))
                    norm.vector(step, tiled(r), tiled(sq), cols(x_cur, k), k, 0)
                turns(dve, NG, body)

            @block.sync
            def _(sp):
                sp.dma_start(dp_all, dp_dram).then_inc(dp_in, 16)
                sp.wait_ge(v_n, 11 * NG)
                sp.dma_start(out[0:(NT - 1) * P, :].rearrange("(t p) f -> p t f", p=P), tiled(x_cur[:, 0:(NT - 1) * D])).then_inc(out_dma, 16)
                sp.dma_start(out[(NT - 1) * P:N, :], x_cur[0:LAST, (NT - 1) * D:NT * D]).then_inc(out_dma, 16)
                sp.wait_ge(out_dma, 32)


def kernel(**inputs):
    import numpy as np
    import concourse.bacc as bacc
    from concourse.bass_utils import run_bass_kernel_spmd as run

    nc = bacc.Bacc("TRN2", target_bir_lowering=False, num_devices=1)
    arrays, t = {}, {}
    for n in inputs:
        a = np.ascontiguousarray(inputs[n])
        arrays["in_" + n] = a
        t[n] = nc.dram_tensor("in_" + n, a.shape, mybir.dt.from_np(a.dtype), kind="ExternalInput").ap()
    out = nc.dram_tensor("out", (N, D), F32, kind="ExternalOutput").ap()
    build(nc, t, out)
    r = run(nc, [arrays], core_ids=[0])
    return r.results[0]["out"]
```

```python
import concourse.bass as bass
from concourse import mybir
from contextlib import ExitStack

F32 = mybir.dt.float32
BF16 = mybir.dt.bfloat16
I32 = mybir.dt.int32
ALU = mybir.AluOpType
ACT = mybir.ActivationFunctionType
AX = mybir.AxisListType

N = 6250
E = 100000
D = 128
P = 128
NT = -(-N // P)
NP = NT * P
GT = 7
NG = NT // GT
GC = GT * D
LAST = N - (NT - 1) * P
EC = 125
UC = E // EC
UG = UC // 8
GROUPS = 16
JC = 52
SC = GROUPS * JC
HALVES = SC // 8
ITER = HALVES // 2
ROWS = SC * P
H = 8
DK = D // H
TN = 8
NB = 4
TL = JC * P
SX = SC + 8
BIG = 1.0e30
PAD_KEY = 1.0e6
HALF = (P - 1) / 2
EPS = 1e-5
assert SC >= (E + NT * (P - 1)) // P and NG * GT == NT and UG % 2 == 0


class Chain:

    def __init__(self, eng, sem, base=0):
        self.eng, self.sem, self.base, self.n = eng, sem, base, 0

    def __call__(self, ins):
        self.n += 1
        ins.then_inc(self.sem, 1)
        self.eng.wait_ge(self.sem, self.base + self.n)


def settle(eng):
    eng.nop(nofuse=True)


def turns(eng, count, body):
    body(0)
    with eng.Fori(1, count) as k:
        body(k)


def need(eng, sem, value):
    if not isinstance(value, int) or value > 0:
        eng.wait_ge(sem, value)


def bcast_last(ap, n):
    shape = list(ap.shape) + [n]
    return ap.unsqueeze(len(shape) - 1).to_broadcast(shape)


def bcast_mid(ap, n):
    return ap.unsqueeze(1).to_broadcast([ap.shape[0], n] + list(ap.shape[1:]))


def build(nc, t, out):
    ctx = ExitStack()
    with ctx:
        def sb(name, cols, dt=F32):
            return ctx.enter_context(nc.sbuf_tensor(name, [P, cols], dt))

        stage_sems = []

        def sem(name):
            stage_sems.append(nc.alloc_semaphore(name))
            return stage_sems[-1]

        def new_stage():
            nc.clear_and_free_semaphores(list(stage_sems))
            nc.all_engine_barrier()
            stage_sems.clear()

        def dram(name, shape, dt=F32):
            return nc.dram_tensor(name, shape, dt).ap()

        x_cur = sb("x_cur", NT * D)
        iota_row = sb("iota_row", P)
        iota_part = sb("iota_part", 1)
        ident = sb("ident", P)
        earlier = sb("earlier", P)
        before = sb("before", P)
        ones = sb("ones", P)
        int_tmp = sb("int_tmp", P, I32)
        int_tmp2 = sb("int_tmp2", 1, I32)
        d_src = sb("d_src", SX, I32)
        d_typed = sb("d_typed", SX, I32)
        d_lw = sb("d_lw", SX * 2)
        s_dst = sb("s_dst", SX, I32)
        s_lo = sb("s_lo", SX)
        d_tile = sb("d_tile", SC, I32)
        s_tile = sb("s_tile", SC, I32)
        dinv = sb("dinv", NT)
        inv = sb("inv", NT)
        small = sb("small", 512)
        neg_half = sb("neg_half", 64)
        stage_idx = sb("stage_idx", 16, I32)
        stage_lw = sb("stage_lw", 32)
        bias_names = ["L0_gnn_b1", "L0_gnn_bfc", "L1_gnn_ln_gamma", "L1_gnn_ln_beta", "L1_gnn_b_in", "L1_gnn_b_ff",
                      "L2_gnn_bias", "L3_gnn_W_b", "L3_gnn_V_b", "L3_gnn_D_b", "L3_gnn_E_b"]
        bias_sb = sb("bias_sb", len(bias_names) * D)
        bias = {n: bias_sb[:, i * D:(i + 1) * D] for i, n in enumerate(bias_names)}
        b_u = sb("b_u", H)
        col_names = ["L0_gnn_b2", "L1_gnn_b_in", "L3_gnn_U_b"]
        col_sb = sb("col_sb", len(col_names))
        col = {n: col_sb[:, i:i + 1] for i, n in enumerate(col_names)}
        w_names = ["L0_gnn_W1", "L0_gnn_W2", "L0_gnn_Wfc", "L1_gnn_W_in", "L1_gnn_W_ff", "L2_gnn_loop_weight"]
        w_sb = sb("w_sb", len(w_names) * D)
        w = {n: w_sb[:, i * D:(i + 1) * D] for i, n in enumerate(w_names)}
        w_uv = sb("w_uv", 2 * H)
        l3_T = sb("l3_T", 6 * D)
        arena = sb("arena", 34000)

        ps = ctx.enter_context(nc.psum_tensor("ps", [P, 8 * 512], F32))

        def bank(b, n=512, parts=P):
            return ps[0:parts, b * 512:b * 512 + n]

        d_rec = dram("d_rec", [ROWS, 4])
        s_rec = dram("s_rec", [ROWS, 2])
        d_loT = dram("d_loT", [SC, P])
        s_loT = dram("s_loT", [SC, P])
        penT = dram("penT", [P, TL + 1])
        t0 = dram("t0", [NP, D])
        t1 = dram("t1", [NP, D])
        t2 = dram("t2", [NP, D + H])
        t3 = dram("t3", [TN * NP, 2 * D])
        t4 = dram("t4", [NP, 3 * D])
        spill = dram("spill", [HALVES, P, 8 * D])
        p_dram = dram("p_dram", [P, NT * D])
        dp_dram = dram("dp_dram", [P, NT * D])

        landed = [ctx.enter_context(nc.semaphore("landed0")), ctx.enter_context(nc.semaphore("landed1"))]
        gather_pass = [0]
        carry = sb("carry", 3 * P)

        e_in = {}
        o = 0
        for n in ("src", "dst", "typ", "wgt"):
            e_in[n] = arena[0:EC, o:o + UC]
            o += UC
        ld_i = arena[:, o:o + 3 * 7 * EC].bitcast(I32).rearrange("p (a j e) -> p a j e", a=3, j=7)
        o += 3 * 7 * EC
        ld_f = arena[:, o:o + 4 * 7 * EC].rearrange("p (a j e) -> p a j e", a=4, j=7)
        l3_raw = arena[:, o + 4 * 7 * EC:o + 4 * 7 * EC + 6 * D]
        SORT0 = 4 * UC
        loads = sem("loads")
        iotas = sem("iotas")
        zeroed = sem("zeroed")
        v_set = sem("v_set")
        edge_T = sem("edge_T")
        edge_f = sem("edge_f")
        l3_up = sem("l3_up")
        n_loads = [0]
        with nc.Block() as block:
            @block.sync
            def _(sp):
                def load(dst, src):
                    n_loads[0] += 16
                    sp.dma_start(dst, src).then_inc(loads, 16)

                sp.wait_ge(zeroed, 1)
                full = UC // P
                for a, name in enumerate(("src", "dst", "edge_type_8", "edge_weight")):
                    dst = ld_i[:, a] if a < 3 else ld_f[:, 3]
                    load(dst[:, 0:full, :], t[name][0:full * P * EC].rearrange("(j p e) -> p j e", p=P, e=EC))
                    load(dst[0:UC - full * P, full, :], t[name][full * P * EC:E].rearrange("(p e) -> p e", e=EC))
                for i, name in enumerate(("L3_gnn_U_w", "L3_gnn_W_w")):
                    load(l3_raw[:, i * D:(i + 1) * D], t[name])
                load(l3_raw[:, 2 * D:4 * D], t["L3_gnn_V_w"])
                load(l3_raw[:, 4 * D:5 * D], t["L3_gnn_D_w"])
                load(l3_raw[:, 5 * D:6 * D], t["L3_gnn_E_w"])
                for n in w_names:
                    load(w[n], t[n])
                load(w_uv[:, 0:H], t["L1_gnn_W_u"])
                load(w_uv[:, H:2 * H], t["L1_gnn_W_v"])
                for n in bias_names:
                    load(bias[n], t[n].partition_broadcast(P))
                load(b_u[:, :], t["L1_gnn_b_u"].partition_broadcast(P))
                for n in col_names:
                    load(col[n], t[n].rearrange("(p o) -> p o", o=1))
                xt = x_cur[:, :].rearrange("p (t f) -> p t f", f=D)
                load(xt[:, 0:NT - 1, :], t["x"][0:(NT - 1) * P, :].rearrange("(t p) f -> p t f", p=P))
                load(xt[0:LAST, NT - 1, :], t["x"][(NT - 1) * P:N, :])
                sp.wait_ge(loads, n_loads[0])

            @block.gpsimd
            def _(pool):
                nc.gpsimd.iota(int_tmp[:, :], [[1, P]], base=0, channel_multiplier=0).then_inc(iotas, 1)
                nc.gpsimd.iota(int_tmp2[:, :], [[1, 1]], base=0, channel_multiplier=1).then_inc(iotas, 1)

            n_all = 16 * (8 + 5 + len(w_names) + 2 + len(bias_names) + 1 + len(col_names) + 2)

            @block.vector
            def _(dve):
                step = Chain(dve, v_set)
                nc.vector.memset(x_cur[:, (NT - 1) * D:NT * D], 0.0)
                nc.vector.memset(ld_i[:, :, 6, :], 0)
                nc.vector.memset(ld_f[:, 3, 6, :], 0.0).then_inc(zeroed, 1)
                nc.vector.memset(ones[:, :], 1.0)
                nc.vector.memset(neg_half[:, :], -0.5)
                nc.vector.memset(d_src[:, :], 0)
                nc.vector.memset(d_typed[:, :], 0)
                nc.vector.memset(d_lw[:, :], 0.0)
                step(nc.vector.memset(s_dst[:, :], 0))
                dve.wait_ge(iotas, 2)
                step(nc.vector.tensor_copy(iota_row[:, :], int_tmp[:, :]))
                step(nc.vector.tensor_copy(iota_part[:, :], int_tmp2[:, :]))
                for m, op in ((ident, ALU.is_equal), (earlier, ALU.is_lt), (before, ALU.is_gt)):
                    step(nc.vector.tensor_scalar(m[:, :], iota_row[:, :], iota_part[:, 0:1], None, op))
                dve.wait_ge(loads, n_all)
                nc.vector.tensor_copy(ld_f[:, 0:3], ld_i).then_inc(edge_f, 1)
                for a, n in enumerate(("src", "dst", "typ", "wgt")):
                    dve.wait_ge(edge_T, a + 1)
                    b = 2 * (a % 2)
                    step(nc.vector.tensor_copy(e_in[n], ps[0:EC, b * 512:b * 512 + UC]))
                step(nc.vector.scalar_tensor_tensor(e_in["typ"], e_in["typ"], float(NP), e_in["src"], ALU.mult, ALU.add))
                dve.wait_ge(l3_up, 1)
                step(nc.vector.tensor_copy(l3_T[:, :], ps[:, 2048:2048 + 6 * D]))

            @block.tensor
            def _(pe):
                pe.wait_ge(edge_f, 1)
                for a in range(4):
                    if a >= 2:
                        pe.wait_ge(v_set, 6 + a - 1)
                    for j in range(7):
                        b = 2 * (a % 2) * 512 + j * P
                        k = min(P, UC - j * P)
                        last = nc.tensor.transpose(ps[0:EC, b:b + k], ld_f[0:k, a, j, :], ident[0:k, 0:k])
                    last.then_inc(edge_T, 1)
                for i in range(6):
                    last = nc.tensor.transpose(ps[:, 2048 + i * D:2048 + (i + 1) * D], l3_raw[:, i * D:(i + 1) * D], ident[:, :])
                last.then_inc(l3_up, 1)

        sort_top = SORT0

        def part(n, dt=F32):
            nonlocal sort_top
            sort_top += n
            assert sort_top <= 34000, sort_top
            ap = arena[:, sort_top - n:sort_top]
            return ap if dt == F32 else ap.bitcast(dt)

        class Side:

            def __init__(self, name, key, fields, key_dram, rec, loT, tile_row):
                self.name, self.key, self.key_dram, self.fields = name, key, key_dram, fields
                self.rec, self.loT, self.tile_row, self.R = rec, loT, tile_row, len(fields)
                self.lo = part(UC)[0:EC]
                self.hi = part(UC)[0:EC]
                self.recs = part(UC * self.R)[0:EC].rearrange("p (c r) -> p c r", r=self.R)
                self.start = part(NT)
                self.tile_rep = part(SC)

        by_src = Side("s", e_in["src"], [e_in["dst"], e_in["src"]], t["src"], s_rec, s_loT, s_tile)
        by_dst = Side("d", e_in["dst"], [e_in["src"], e_in["dst"], e_in["typ"], e_in["wgt"]], t["dst"], d_rec, d_loT, d_tile)
        SORT1 = sort_top

        new_stage()
        HW = 4 * NT
        s_lo_hot = part(8 * P, BF16)[0:EC].rearrange("p (b i l) -> p b i l", b=2, i=8)
        s_hi_hot = part(8 * NT, BF16)[0:EC].rearrange("p (b i l) -> p b i l", b=2, i=8)
        s_hi_diff = part(16 * NT)[0:EC].rearrange("p (b i l) -> p b i l", b=2, i=8)
        d_lo_hot = part(8 * P, BF16)[0:EC].rearrange("p (b i l) -> p b i l", b=2, i=8)
        d_hi_hot = part(8 * HW, BF16)[0:EC].rearrange("p (b i l) -> p b i l", b=2, i=8)
        w_part = part(3 * UC // 2, BF16)[0:EC].rearrange("p (a c) -> p a c", a=3)
        w_rest = part(UC)[0:EC]
        zeros = part(HW)[0:EC]
        hi_int = [part(UC)[0:EC].bitcast(I32) for _ in range(2)]
        fill = [part(JC * 16 * side.R) for side in (by_src, by_dst)]
        counts, n_chunks, tmp, first_chunk = (part(NT) for _ in range(4))
        chunks_int = part(NT).bitcast(I32)
        first_col = part(1)
        tile_ge = part(SC)
        iota_c = part(SC)
        iota_ci = part(SC).bitcast(I32)
        split, filled, fill_set, iota_done = (sem("h_" + n) for n in ("split", "filled", "fill_set", "iota_done"))
        d_tiles, weighed, nodes, diff, dist, hot_a, free, hist_done = (sem("h_" + n) for n in (
            "d_tiles", "weighed", "nodes", "diff", "dist", "hot_a", "free", "done"))
        base_v, base_p, root_in, root_out = (sem("h_" + n) for n in ("base_v", "base_p", "root_in", "root_out"))
        s_counts, d_counts = bank(0, NT), bank(1, HW)
        with nc.Block() as block:
            @block.gpsimd
            def _(pool):
                nc.gpsimd.iota(iota_ci, [[1, SC]], base=0, channel_multiplier=0).then_inc(iota_done, 1)
                pool.wait_ge(split, 12)

                def body(k):
                    for b in range(2):
                        n = 2 * k + b
                        need(pool, free, n - 1)
                        need(pool, hot_a, n - 1)
                        nc.gpsimd.tensor_tensor(s_hi_diff[:, b], bcast_mid(iota_row[0:EC, 0:NT], 8),
                                                bcast_last(by_src.hi[:, bass.ds(8 * n, 8)], NT), ALU.subtract).then_inc(diff, 1)
                        pool.wait_ge(d_tiles, n + 1)
                        for a in range(3):
                            nc.gpsimd.tensor_tensor(d_hi_hot[:, b, :, (a + 1) * NT:(a + 2) * NT], d_hi_hot[:, b, :, 0:NT],
                                                    bcast_last(w_part[:, a, bass.ds(8 * n, 8)], NT), ALU.mult).then_inc(weighed, 1)
                turns(pool, UG // 2, body)
                for i in range(2):
                    pool.wait_ge(root_in, i + 1)
                    nc.gpsimd.tensor_tensor(small[:, 128:128 + NT], small[:, 0:NT], neg_half[:, 0:NT], ALU.pow).then_inc(root_out, 1)

            @block.sync
            def _(sp):
                sp.wait_ge(fill_set, 2)
                for side, f in ((by_src, fill[0]), (by_dst, fill[1])):
                    sp.dma_start(side.rec.rearrange("(p c) r -> p (c r)", p=P), f).then_inc(filled, 16)
                sp.wait_ge(filled, 32)

            @block.scalar
            def _(act):
                for side in (by_src, by_dst):
                    for f, a in enumerate(side.fields):
                        nc.scalar.activation(side.recs[:, :, f], a, ACT.Copy)

                def body(k):
                    for b in range(2):
                        n = 2 * k + b
                        act.wait_ge(diff, n + 1)
                        nc.scalar.activation(s_hi_diff[:, b], s_hi_diff[:, b], ACT.Abs).then_inc(dist, 1)
                        need(act, free, n - 1)
                        act.wait_ge(dist, n + 1)
                        nc.scalar.activation(s_hi_hot[:, b], s_hi_diff[:, b], ACT.Relu, bias=ones[0:EC, 0:1], scale=-1.0).then_inc(hot_a, 1)
                turns(act, UG // 2, body)

            @block.vector
            def _(dve):
                step = Chain(dve, split)
                step(nc.vector.memset(zeros, 0.0))
                for side, h in ((by_src, hi_int[0]), (by_dst, hi_int[1])):
                    step(nc.vector.tensor_scalar(h, side.key, -HALF, 1.0 / P, ALU.add, ALU.mult))
                    step(nc.vector.tensor_copy(side.hi, h))
                    step(nc.vector.scalar_tensor_tensor(side.lo, side.hi, -float(P), side.key, ALU.mult, ALU.add))
                step(nc.vector.tensor_copy(w_part[:, 0], e_in["wgt"]))
                for a in range(2):
                    step(nc.vector.tensor_tensor(w_rest, w_rest if a else e_in["wgt"], w_part[:, a], ALU.subtract))
                    step(nc.vector.tensor_copy(w_part[:, a + 1], w_rest))

                def body(k):
                    for b in range(2):
                        n = 2 * k + b
                        need(dve, free, n - 1)
                        nc.vector.tensor_tensor(d_hi_hot[:, b, :, 0:NT], bcast_mid(iota_row[0:EC, 0:NT], 8),
                                                bcast_last(by_dst.hi[:, bass.ds(8 * n, 8)], NT), ALU.is_equal).then_inc(d_tiles, 1)
                        nc.vector.tensor_tensor(s_lo_hot[:, b], bcast_mid(iota_row[0:EC, :], 8),
                                                bcast_last(by_src.lo[:, bass.ds(8 * n, 8)], P), ALU.is_equal).then_inc(nodes, 1)
                        nc.vector.tensor_tensor(d_lo_hot[:, b], bcast_mid(iota_row[0:EC, :], 8),
                                                bcast_last(by_dst.lo[:, bass.ds(8 * n, 8)], P), ALU.is_equal).then_inc(nodes, 1)
                turns(dve, UG // 2, body)
                for f in fill:
                    step(nc.vector.memset(f, 0.0))
                for side, f in ((by_src, fill[0]), (by_dst, fill[1])):
                    nc.vector.memset(f.rearrange("p (c r) -> p c r", r=side.R)[:, :, 1], PAD_KEY).then_inc(fill_set, 1)
                dve.wait_ge(iota_done, 1)
                step(nc.vector.tensor_copy(iota_c, iota_ci))
                dve.wait_ge(hist_done, 1)
                step = Chain(dve, base_v)
                deg, linked = small[:, 0:NT], small[:, 64:64 + NT]
                for i, (side, ps_counts) in enumerate(((by_src, s_counts), (by_dst, d_counts[:, 0:NT]))):
                    step(nc.vector.tensor_copy(counts, ps_counts))
                    dve.wait_ge(base_p, 3 * i + 1)
                    step(nc.vector.tensor_scalar(chunks_int, bank(2, NT), P - 1 - HALF, 1.0 / P, ALU.add, ALU.mult))
                    step(nc.vector.tensor_copy(n_chunks, chunks_int))
                    step(nc.vector.memset(tmp, 0.0))
                    step(nc.vector.tensor_tensor_scan(first_chunk, n_chunks, tmp, 0.0, ALU.add, ALU.add))
                    step(nc.vector.tensor_tensor(first_chunk, first_chunk, n_chunks, ALU.subtract))
                    step(nc.vector.scalar_tensor_tensor(side.start, first_chunk, float(P), bank(3, NT), ALU.mult, ALU.add))
                    dve.wait_ge(base_p, 3 * i + 2)
                    step(nc.vector.tensor_copy(first_col[0:NT], bank(4, 1, NT)))
                    step(nc.vector.tensor_scalar(tile_ge[0:NT], iota_c[0:NT], first_col[0:NT, 0:1], None, ALU.is_ge))
                    dve.wait_ge(base_p, 3 * i + 3)
                    step(nc.vector.tensor_scalar(side.tile_rep, ps[:, 2560:2560 + SC], -1.0, None, ALU.add))
                    step(nc.vector.tensor_copy(side.tile_row[0:1, :], side.tile_rep[0:1, :]))
                    assert step.n == 11 * (i + 1)
                step(nc.vector.tensor_scalar(deg, s_counts, 1.0, None, ALU.add))
                dve.sem_inc(root_in, 1)
                dve.wait_ge(root_out, 1)
                step(nc.vector.tensor_copy(inv[:, :], small[:, 128:128 + NT]))
                step(nc.vector.tensor_scalar(deg, d_counts[:, NT:2 * NT], 1.0, None, ALU.add))
                for a in range(2, 4):
                    step(nc.vector.tensor_tensor(deg, deg, d_counts[:, a * NT:(a + 1) * NT], ALU.add))
                step(nc.vector.tensor_scalar(linked, deg, 0.0, None, ALU.is_gt))
                step(nc.vector.tensor_tensor(deg, deg, linked, ALU.mult))
                step(nc.vector.scalar_tensor_tensor(deg, deg, 1.0, linked, ALU.add, ALU.subtract))
                dve.sem_inc(root_in, 1)
                dve.wait_ge(root_out, 2)
                step(nc.vector.tensor_tensor(dinv[:, :], small[:, 128:128 + NT], linked, ALU.mult))

            @block.tensor
            def _(pe):
                pe.wait_ge(split, 1)
                nc.tensor.matmul(s_counts, zeros[:, 0:P], zeros[:, 0:NT], start=True, stop=False, skip_group_check=True)
                nc.tensor.matmul(d_counts, zeros[:, 0:P], zeros[:, 0:HW], start=True, stop=False, skip_group_check=True)

                def body(k):
                    for b in range(2):
                        n = 2 * k + b
                        pe.wait_ge(weighed, 3 * n + 3)
                        pe.wait_ge(hot_a, n + 1)
                        pe.wait_ge(nodes, 2 * n + 2)
                        for i in range(8):
                            nc.tensor.matmul(s_counts, s_lo_hot[:, b, i], s_hi_hot[:, b, i], start=False, stop=False, skip_group_check=True)
                            last = nc.tensor.matmul(d_counts, d_lo_hot[:, b, i], d_hi_hot[:, b, i], start=False, stop=False, skip_group_check=True)
                        last.then_inc(free, 1)
                turns(pe, UG // 2, body)
                nc.tensor.matmul(s_counts, zeros[:, 0:P], zeros[:, 0:NT], start=False, stop=True, skip_group_check=True)
                nc.tensor.matmul(d_counts, zeros[:, 0:P], zeros[:, 0:HW], start=False, stop=True, skip_group_check=True).then_inc(hist_done, 1)
                for i in range(2):
                    pe.wait_ge(base_v, 11 * i + 1)
                    nc.tensor.matmul(bank(2, NT), ones[:, :], counts, start=True, stop=True)
                    nc.tensor.matmul(bank(3, NT), before[:, :], counts, start=True, stop=True).then_inc(base_p, 1)
                    pe.wait_ge(base_v, 11 * i + 6)
                    nc.tensor.matmul(bank(4, 1, NT), first_chunk[0:1, :], ones[0:1, 0:1], start=True, stop=True).then_inc(base_p, 1)
                    pe.wait_ge(base_v, 11 * i + 9)
                    for j in range(2):
                        last = nc.tensor.matmul(ps[:, 2560 + j * 512:2560 + min(SC, (j + 1) * 512)], ones[0:NT, :],
                                                tile_ge[0:NT, j * 512:min(SC, (j + 1) * 512)], start=True, stop=True)
                    last.then_inc(base_p, 1)

        def place_edges(side):
            nonlocal sort_top
            new_stage()
            sort_top = SORT1
            R, key, lo, hi, rec, recs = side.R, side.key, side.lo, side.hi, side.rec, side.recs
            at_lo = part(8 * P, BF16)[0:EC].rearrange("p (b i l) -> p b i l", b=2, i=8)
            at_hi = part(8 * NT, BF16)[0:EC].rearrange("p (b i l) -> p b i l", b=2, i=8)
            at_run = part(2 * 8 * NT).rearrange("p (b i l) -> p b i l", b=2, i=8)
            keys_all = part(2 * 8 * EC).bitcast(I32).rearrange("p (b c) -> p b c", b=2)
            at_loT = part(2 * 8 * EC).rearrange("p (b c) -> p b c", b=2)
            lo_all = part(2 * 8 * EC).bitcast(I32).rearrange("p (b c) -> p b c", b=2)
            same = part(8 * EC)[0:EC].rearrange("p (i e) -> p i e", i=8)
            rank, val, key_st = (part(16)[0:EC] for _ in range(3))
            q, row = (part(16)[0:EC].bitcast(I32) for _ in range(2))
            picks = part(8 * NT)[0:EC].rearrange("p (i l) -> p i l", i=8)
            recs_st = part(16 * R)[0:EC].rearrange("p (c r) -> p c r", r=R)
            minus_part = part(1)
            srt = part(SC * R).rearrange("p (c r) -> p c r", r=R)
            lo_s = part(SC)
            lo_T = part(7 * P)
            pre = side.name + "_"
            keys_in = [sem(pre + "keys_in0"), sem(pre + "keys_in1")]
            placed = [sem(pre + "placed0"), sem(pre + "placed1")]
            begun, hot_c, masked, dist, hot_T, counted, run_set, found, v_grp, ranked, picked = (sem(pre + n) for n in (
                "begun", "hot_c", "masked", "dist", "hot_T", "counted", "run_set", "found", "v_grp", "ranked", "picked"))
            key_rows = side.key_dram.rearrange("(g c) -> g c", c=8 * EC)
            TURNS = UG // 2
            GH = 8 * NT
            PICK = 7

            def count_bank(b):
                return ps[:, b * 512:b * 512 + GH]

            def pick_bank(b):
                return ps[0:EC, (2 + b) * 512:(2 + b) * 512 + GH]
            with nc.Block() as block:
                @block.sync
                def _(sp):
                    def body(k):
                        for b in range(2):
                            n = 2 * k + b
                            need(sp, ranked, n - 1)
                            sp.dma_start(keys_all[:, b, :], key_rows[bass.ds(n, 1), :].to_broadcast([P, 8 * EC])).then_inc(keys_in[b], 16)
                    turns(sp, TURNS, body)

                @block.scalar
                def _(act):
                    act.wait_ge(begun, 2)

                    def body(k):
                        for b in range(2):
                            n = 2 * k + b
                            need(act, found, n - 1)
                            act.wait_ge(masked, n + 1)
                            nc.scalar.activation(at_loT[:, b], lo_all[:, b], ACT.Abs, bias=minus_part).then_inc(dist, 1)
                            act.wait_ge(dist, n + 1)
                            nc.scalar.activation(at_loT[:, b], at_loT[:, b], ACT.Relu, bias=ones[:, 0:1], scale=-1.0).then_inc(hot_T, 1)
                    turns(act, TURNS, body)

                @block.vector
                def _(dve):
                    nc.vector.tensor_copy(at_run[:, 1, 7], side.start).then_inc(begun, 1)
                    nc.vector.tensor_scalar(minus_part, iota_part[:, 0:1], -1.0, None, ALU.mult).then_inc(begun, 1)
                    dve.wait_ge(begun, 2)

                    def run_on(n, b):
                        dve.wait_ge(counted, n + 1)
                        need(dve, run_set, n)
                        nc.vector.tensor_tensor(at_run[:, b], count_bank(b).rearrange("p (i l) -> p i l", i=8),
                                                bcast_mid(at_run[:, 1 - b, 7], 8), ALU.add).then_inc(run_set, 1)

                    def one_hots(k, b):
                        n = 2 * k + b
                        nc.vector.tensor_tensor(at_lo[:, b], bcast_mid(iota_row[0:EC, :], 8),
                                                bcast_last(lo[:, bass.ds(8 * n, 8)], P), ALU.is_equal)
                        nc.vector.tensor_tensor(at_hi[:, b], bcast_mid(iota_row[0:EC, 0:NT], 8),
                                                bcast_last(hi[:, bass.ds(8 * n, 8)], NT), ALU.is_equal).then_inc(hot_c, 1)
                        nc.vector.tensor_copy(key_st[:, 8 * b:8 * b + 8], key[:, bass.ds(8 * n, 8)]).then_inc(v_grp, 1)
                        need(dve, hot_T, n - 1)
                        dve.wait_ge(keys_in[b], 16 * k + 16)
                        nc.vector.tensor_scalar(lo_all[:, b], keys_all[:, b, :], P - 1, None, ALU.bitwise_and).then_inc(masked, 1)

                    def ranks(k, b):
                        n = 2 * k + b
                        need(dve, ranked, n)
                        dve.wait_ge(v_grp, n + 1)
                        for i in range(8):
                            last = nc.vector.scalar_tensor_tensor(same[:, i], keys_all[0:EC, b, i * EC:(i + 1) * EC], key_st[:, 8 * b + i:8 * b + i + 1],
                                                                  earlier[0:EC, 0:EC], ALU.is_equal, ALU.mult,
                                                                  accum_out=rank[:, 8 * b + i:8 * b + i + 1])
                        last.then_inc(ranked, 1)

                    def places(k, b, n, scatters):
                        sl = slice(8 * b, 8 * b + 8)
                        step = Chain(dve, picked, PICK * n)
                        dve.wait_ge(found, n + 1)
                        step(nc.vector.tensor_tensor(picks, pick_bank(b).rearrange("p (i l) -> p i l", i=8), at_hi[:, b], ALU.mult))
                        step(nc.vector.tensor_reduce(val[:, sl], picks, AX.X, ALU.add))
                        step(nc.vector.tensor_tensor(val[:, sl], val[:, sl], rank[:, sl], ALU.add))
                        need(dve, placed[b], scatters)
                        settle(nc.vector)
                        step(nc.vector.tensor_copy(recs_st[:, sl, :], recs[:, bass.ds(8 * n, 8), :]))
                        step(nc.vector.tensor_scalar(q[:, sl], val[:, sl], -HALF, 1.0 / P, ALU.add, ALU.mult))
                        step(nc.vector.scalar_tensor_tensor(rank[:, sl], q[:, sl], -float(P), val[:, sl], ALU.mult, ALU.add))
                        step(nc.vector.scalar_tensor_tensor(row[:, sl], rank[:, sl], float(SC), q[:, sl], ALU.mult, ALU.add))
                        assert step.n == PICK

                    def body(k):
                        for b in range(2):
                            first = isinstance(k, int) and b == 0
                            n = 2 * k + b
                            if not first:
                                run_on(n - 1, 1 - b)
                            one_hots(k, b)
                            ranks(k, b)
                            if not first:
                                places(k, 1 - b, n - 1, 128 * (k - 1 + b))
                    turns(dve, TURNS, body)
                    run_on(UG - 1, 1)
                    dve.wait_ge(ranked, UG)
                    places(TURNS - 1, 1, UG - 1, 128 * (TURNS - 1))

                @block.tensor
                def _(pe):
                    def look_up(n, b):
                        pe.wait_ge(hot_T, n + 1)
                        need(pe, picked, PICK * n - PICK)
                        pe.wait_ge(run_set, n + 1)
                        for i in range(8):
                            run = at_run[:, b, i - 1] if i else at_run[:, 1 - b, 7]
                            last = nc.tensor.matmul(pick_bank(b)[:, i * NT:(i + 1) * NT], at_loT[:, b, i * EC:(i + 1) * EC], run, start=True, stop=True)
                        last.then_inc(found, 1)

                    def body(k):
                        for b in range(2):
                            first = isinstance(k, int) and b == 0
                            n = 2 * k + b
                            if not first:
                                look_up(n - 1, 1 - b)
                            pe.wait_ge(hot_c, n + 1)
                            need(pe, run_set, n - 1)
                            for i in range(8):
                                last = nc.tensor.matmul(count_bank(b)[:, i * NT:GH], at_lo[:, b, i], bcast_mid(at_hi[:, b, i], 8 - i),
                                                        start=i == 0, stop=i == 7, skip_group_check=True)
                            last.then_inc(counted, 1)
                    turns(pe, TURNS, body)
                    look_up(UG - 1, 1)

                @block.gpsimd
                def _(pool):
                    with pool.Fori(0, TURNS) as k:
                        for b in range(2):
                            pool.wait_ge(picked, 2 * PICK * k + PICK * (b + 1))
                            settle(pool)
                            for i in range(8):
                                pool.indirect_dma_start(out=rec[:, :], out_offset=bass.IndirectOffsetOnAxis(ap=row[:, 8 * b + i:8 * b + i + 1], axis=0),
                                                        in_=recs_st[:, 8 * b + i, :], in_offset=None).then_inc(placed[b], 16)
                    for b in range(2):
                        pool.wait_ge(placed[b], 128 * TURNS)

            back, v_back, lo_up, lo_out = (sem(pre + n) for n in ("back", "v_back", "lo_up", "lo_out"))
            with nc.Block() as block:
                @block.sync
                def _(sp):
                    sp.dma_start(srt, rec.rearrange("(p c) r -> p c r", p=P)).then_inc(back, 16)
                    sp.wait_ge(lo_up, 2)
                    lt = lo_T.rearrange("p (j e) -> p j e", j=7)
                    sp.dma_start(side.loT[0:6 * P, :].rearrange("(j p) e -> p j e", p=P), lt[:, 0:6, :]).then_inc(lo_out, 16)
                    sp.dma_start(side.loT[6 * P:SC, :], lt[0:SC - 6 * P, 6, :]).then_inc(lo_out, 16)
                    sp.wait_ge(lo_out, 32)

                @block.vector
                def _(dve):
                    step = Chain(dve, v_back)
                    dve.wait_ge(back, 16)
                    step(nc.vector.scalar_tensor_tensor(lo_s, side.tile_rep, -float(P), srt[:, :, 1], ALU.mult, ALU.add))
                    if side is by_dst:
                        lw = d_lw[:, :].rearrange("p (c r) -> p c r", r=2)
                        nc.vector.tensor_copy(d_src[:, 0:SC], srt[:, :, 0])
                        nc.vector.tensor_copy(d_typed[:, 0:SC], srt[:, :, 2])
                        nc.vector.tensor_copy(lw[:, 0:SC, 1], srt[:, :, 3])
                        step(nc.vector.tensor_copy(lw[:, 0:SC, 0], lo_s))
                    else:
                        nc.vector.tensor_copy(s_dst[:, 0:SC], srt[:, :, 0])
                        step(nc.vector.tensor_copy(s_lo[:, 0:SC], lo_s))
                    dve.wait_ge(lo_up, 1)
                    nc.vector.tensor_copy(lo_T, ps[:, 0:7 * P]).then_inc(lo_up, 1)

                @block.tensor
                def _(pe):
                    pe.wait_ge(v_back, 1)
                    nc.tensor.matmul(ps[:, 6 * P:7 * P], ident[:, :], ident[:, :], start=True, stop=True)
                    for j in range(7):
                        k = min(P, SC - j * P)
                        last = nc.tensor.transpose(ps[0:k, j * P:(j + 1) * P], lo_s[:, j * P:j * P + k], ident[:, :])
                    last.then_inc(lo_up, 1)
            return srt

        place_edges(by_src)
        srt = place_edges(by_dst)
        keys_sorted = srt[:, :, 1]

        W0 = 0
        AT_E = 6400
        AT_ACC = 13056
        AT_Q = 19720
        AT_BUF = 25992
        AW = 34000
        w_typed = {n: arena[:, W0 + i * TN * D:W0 + (i + 1) * TN * D].rearrange("p (t o) -> p t o", t=TN)
                   for i, n in enumerate(("a", "k", "q", "v"))}
        rel = {n: arena[:, W0 + (4 + i) * TN * D:W0 + (5 + i) * TN * D] for i, n in enumerate(("att", "msg"))}
        e_all = arena[:, AT_E:AT_E + SC * H]
        ntb = arena[:, AT_E:AT_E + NP].bitcast(I32)
        acc_att = arena[:, AT_ACC:AT_ACC + NT * (D + H)]
        acc_gcn = arena[:, AT_ACC:AT_ACC + NP]
        q_tab = arena[:, AT_Q:AT_Q + NP]
        v_tab = arena[:, AT_Q:AT_Q + NT * H]

        def tiled(ap, width=D):
            return ap.rearrange("p (t f) -> p t f", f=width)

        def stage_index(dve, idx, staged, base, k, b):
            n_before = 128 * (k + b)
            need(dve, landed[1 - b], base + n_before if not isinstance(n_before, int) or n_before else 0)
            settle(nc.vector)
            nc.vector.tensor_copy(stage_idx[:, 8 * (1 - b):8 * (1 - b) + 8], idx[:, bass.ds(16 * k + 8 * b + 8, 8)]).then_inc(staged, 1)

        def stage_first(idx, staged):
            nc.vector.tensor_copy(stage_idx[:, 0:8], idx[:, 0:8]).then_inc(staged, 1)

        def gathers(pool, table, rows, staged, buffer_free):
            def body(k):
                for b in range(2):
                    pool.wait_ge(staged, 2 * k + b + 1)
                    buffer_free(k, b)
                    settle(pool)
                    for i in range(8):
                        pool.indirect_dma_start(out=rows[:, 8 * b + i, :], out_offset=None, in_=table,
                                                in_offset=bass.IndirectOffsetOnAxis(ap=stage_idx[:, 8 * b + i:8 * b + i + 1], axis=0)).then_inc(landed[b], 16)
            turns(pool, ITER, body)

        def next_pass():
            gather_pass[0] += 1
            return (gather_pass[0] - 1) * 128 * ITER

        def tile_numbers(eng, regs, tile_row, c):
            eng.load(regs, tile_row[0:1, bass.ds(c, 8)])
            return [eng.snap(r, min_val=0, max_val=NT - 1) for r in regs]

        def registers(eng, name):
            return [eng.alloc_register(f"{name}{i}") for i in range(8)]

        class Sums:

            def __init__(self, pre, tile_row, acc, width):
                self.added, self.drained = sem(pre + "added"), sem(pre + "drained")
                self.pre, self.tile_row, self.acc, self.width = pre, tile_row, acc, width

            def start(self, dve):
                self.dve, self.regs = dve, registers(dve, self.pre + "tile")

            def open(self, c, behind=True):
                self.tiles = tile_numbers(self.dve, self.regs, self.tile_row, c)
                if behind:
                    self.drain(8)
                    self.dve.sem_inc(self.added, -8)

            def add(self, i, product):
                if i:
                    self.dve.wait_ge(self.added, i)
                at = self.acc[:, bass.ds(self.tiles[i] * self.width, self.width)]
                nc.vector.tensor_tensor(at, at, product, ALU.add).then_inc(self.added, 1)

            def drain(self, count):
                self.dve.wait_ge(self.added, count)
                self.dve.sem_inc(self.drained, 1)

        AT_T = AT_ACC
        scan = [arena[:, AT_T + i * (TL + 1):AT_T + (i + 1) * (TL + 1)] for i in range(3)]
        stage_T = arena[:, AT_T + 3 * (TL + 1):AT_T + 3 * (TL + 1) + 512]
        assert AT_T + 3 * (TL + 1) + 512 <= AW

        def by_group(ap):
            return ap.rearrange("p (g j) -> p j g", g=GROUPS)

        new_stage()
        f_st = sem("f_st")
        f_ps = sem("f_ps")
        f_out = sem("f_out")
        f_v = sem("f_v")
        f_row = sem("f_row")
        f_dma = sem("f_dma")
        K_T = arena[:, 0:TL]
        pen_f = arena[:, TL:2 * TL + 1]
        f_stage = arena[:, 2 * TL + 8:2 * TL + 8 + 512]
        f_rows = arena[0:1, 2 * TL + 520:2 * TL + 520 + 4 * P]
        pw_row, pb_row, pc_row = (carry[0:1, i * P:(i + 1) * P] for i in range(3))
        keys_keep = arena[:, 2 * TL + 1040:2 * TL + 1040 + SC]
        f_key = sem("f_key")
        with nc.Block() as block:
            @block.vector
            def _(dve):
                nc.vector.tensor_copy(keys_keep, keys_sorted).then_inc(f_key, 1)
        with nc.Block() as block:
            @block.scalar
            def _(act):
                def body(k):
                    need(act, f_ps, k)
                    nc.scalar.activation(f_stage.rearrange("p (j g h) -> p j g h", j=4, g=GROUPS),
                                         bcast_last(by_group(keys_keep)[:, bass.ds(4 * k, 4), :], H), ACT.Copy).then_inc(f_st, 1)
                turns(act, JC // 4, body)

            @block.tensor
            def _(pe):
                def body(k):
                    pe.wait_ge(f_st, k + 1)
                    need(pe, f_out, k)
                    for q in range(4):
                        last = nc.tensor.transpose(ps[:, q * P:(q + 1) * P], f_stage[:, q * P:(q + 1) * P], ident[:, :])
                    last.then_inc(f_ps, 1)
                turns(pe, JC // 4, body)
                pe.wait_ge(f_out, JC // 4)
                nc.tensor.matmul(ps[0:1, 512:512 + P], K_T[:, 0:1], ident[:, :], start=True, stop=True)
                nc.tensor.matmul(ps[0:1, 512 + P:512 + 2 * P], K_T[:, TL - 1:TL], ident[:, :], start=True, stop=True).then_inc(f_row, 1)

            @block.vector
            def _(dve):
                def body(k):
                    dve.wait_ge(f_ps, k + 1)
                    settle(nc.vector)
                    nc.vector.tensor_copy(K_T[:, bass.ds(512 * k, 512)], ps[:, 0:512]).then_inc(f_out, 1)
                turns(dve, JC // 4, body)
                dve.wait_ge(f_out, JC // 4)
                step = Chain(dve, f_v)
                step(nc.vector.memset(pen_f, 0.0))
                step(nc.vector.tensor_tensor(pen_f[:, 1:TL], K_T[:, 1:TL], K_T[:, 0:TL - 1], ALU.not_equal))
                step(nc.vector.tensor_scalar(pen_f[:, 1:TL], pen_f[:, 1:TL], -BIG, None, ALU.mult))
                dve.wait_ge(f_row, 1)
                first, last, cont, whole = (f_rows[:, i * P:(i + 1) * P] for i in range(4))
                step(nc.vector.tensor_copy(f_rows[:, 0:2 * P], ps[0:1, 512:512 + 2 * P]))
                step(nc.vector.memset(cont, 0.0))
                step(nc.vector.tensor_tensor(cont[:, H:P], first[:, H:P], last[:, 0:P - H], ALU.is_equal))
                step(nc.vector.tensor_tensor(whole, first, last, ALU.is_equal))

                def swapped(ap):
                    return ap.rearrange("p (g h) -> p h g", h=H)

                def rows(ap):
                    return ap.rearrange("p (h g) -> p h g", h=H)
                step(nc.vector.tensor_copy(rows(pc_row), swapped(cont)))
                step(nc.vector.tensor_copy(rows(pw_row), swapped(whole)))
                step(nc.vector.memset(pb_row, 0.0))
                step(nc.vector.tensor_tensor(rows(pb_row)[:, :, 0:GROUPS - 1], rows(pw_row)[:, :, 0:GROUPS - 1], rows(pc_row)[:, :, 1:GROUPS], ALU.mult))
                step(nc.vector.tensor_tensor(pw_row, pw_row, pc_row, ALU.mult))
                step(nc.vector.tensor_scalar(carry[0:1, :], carry[0:1, :], -1.0, BIG, ALU.add, ALU.mult))

            @block.sync
            def _(sp):
                sp.wait_ge(f_v, 3)
                sp.dma_start(penT, pen_f).then_inc(f_dma, 16)
                sp.wait_ge(f_dma, 16)

        def softmax_weights(which):
            new_stage()
            pre = which + "_sm_"
            s_in, s_st, s_ps, s_out, s_v = (sem(pre + n) for n in ("in", "st", "ps", "out", "v"))
            s_row, s_col, s_d, s_ex, s_exps, s_back = (sem(pre + n) for n in ("row", "col", "d", "ex", "exps", "back"))
            eT = scan[0][:, 0:TL]
            pen = scan[1]
            top = scan[2][:, 0:TL]
            fwd = e_all
            st = stage_T[:, 0:512]
            c_col = small[:, 300:301]
            rows = small[0:1, 0:2 * P]
            by_head = e_all.rearrange("p (g j h) -> p j g h", g=GROUPS, h=H)
            with nc.Block() as block:
                @block.sync
                def _(sp):
                    sp.dma_start(pen, penT).then_inc(s_in, 16)

                @block.scalar
                def _(act):
                    def lay(k):
                        need(act, s_ps, k)
                        nc.scalar.activation(st.rearrange("p (j g h) -> p j g h", j=4, g=GROUPS),
                                             by_head[:, bass.ds(4 * k, 4)], ACT.Copy).then_inc(s_st, 1)
                    turns(act, JC // 4, lay)
                    act.wait_ge(s_d, 1)
                    act.wait_ge(s_ps, JC // 4)

                    def exps(k):
                        need(act, s_exps, k)
                        nc.scalar.activation(st, eT[:, bass.ds(512 * k, 512)], ACT.Exp).then_inc(s_ex, 1)
                    turns(act, JC // 4, exps)

                @block.tensor
                def _(pe):
                    def lay(k):
                        pe.wait_ge(s_st, k + 1)
                        need(pe, s_out, k)
                        for q in range(4):
                            last = nc.tensor.transpose(ps[:, q * P:(q + 1) * P], st[:, q * P:(q + 1) * P], ident[:, :])
                        last.then_inc(s_ps, 1)
                    turns(pe, JC // 4, lay)
                    for d in range(2):
                        pe.wait_ge(s_v, 1 + 5 * d)
                        edge = fwd[:, TL - 1:TL] if d == 0 else top[:, 0:1]
                        nc.tensor.matmul(ps[0:1, 512:512 + P], edge, ident[:, :], start=True, stop=True).then_inc(s_row, 1)
                        pe.wait_ge(s_v, 4 + 5 * d)
                        nc.tensor.matmul(ps[:, 1024:1025], rows[:, P:2 * P], ones[0:1, 0:1], start=True, stop=True).then_inc(s_col, 1)

                    def back(k):
                        pe.wait_ge(s_ex, k + 1)
                        need(pe, s_back, k)
                        for q in range(4):
                            last = nc.tensor.transpose(ps[:, 1536 + q * P:1536 + (q + 1) * P], st[:, q * P:(q + 1) * P], ident[:, :])
                        last.then_inc(s_exps, 1)
                    turns(pe, JC // 4, back)

                @block.vector
                def _(dve):
                    def lay(k):
                        dve.wait_ge(s_ps, k + 1)
                        settle(nc.vector)
                        nc.vector.tensor_copy(eT[:, bass.ds(512 * k, 512)], ps[:, 0:512]).then_inc(s_out, 1)
                    turns(dve, JC // 4, lay)
                    dve.wait_ge(s_out, JC // 4)
                    dve.wait_ge(s_in, 16)
                    step = Chain(dve, s_v)

                    def hg(ap):
                        return ap.rearrange("p (h g) -> p h g", h=H)

                    def gh(ap):
                        return ap.rearrange("p (g h) -> p h g", h=H)
                    for d in range(2):
                        if d == 0:
                            data0, data1, res = pen[:, 0:TL], eT, fwd
                            f_row_ps, pen_row, shut = gh(ps[0:1, 512:512 + P]), pw_row, slice(0, 1)
                        else:
                            data0, data1, res = pen[:, 1:TL + 1][:, ::-1], fwd[:, ::-1], top[:, ::-1]
                            f_row_ps, pen_row, shut = gh(ps[0:1, 512:512 + P]), pb_row, slice(GROUPS - 1, GROUPS)
                        step(nc.vector.tensor_tensor_scan(res, data0, data1, -BIG, ALU.add, ALU.max))
                        dve.wait_ge(s_row, d + 1)
                        run = rows[:, 0:P]
                        step(nc.vector.tensor_copy(hg(run), f_row_ps))
                        if d == 0:
                            step(nc.vector.tensor_tensor_scan(run, pen_row, run, -BIG, ALU.add, ALU.max))
                        else:
                            step(nc.vector.tensor_tensor_scan(run[:, ::-1], pen_row[:, ::-1], run[:, ::-1], -BIG, ALU.add, ALU.max))
                        into = gh(rows[:, P:2 * P])
                        nc.vector.memset(into[:, :, shut], -BIG)
                        if d == 0:
                            step(nc.vector.tensor_tensor(into[:, :, 1:GROUPS], hg(run)[:, :, 0:GROUPS - 1], hg(pc_row)[:, :, 1:GROUPS], ALU.add))
                        else:
                            step(nc.vector.tensor_tensor(into[:, :, 0:GROUPS - 1], hg(run)[:, :, 1:GROUPS], hg(pc_row)[:, :, 1:GROUPS], ALU.add))
                        dve.wait_ge(s_col, d + 1)
                        nc.vector.tensor_copy(c_col, ps[:, 1024:1025]).then_inc(s_out, 1)
                        dve.wait_ge(s_out, JC // 4 + d + 1)
                        step(nc.vector.tensor_tensor_scan(res, data0, data1, c_col, ALU.add, ALU.max))
                    nc.vector.tensor_tensor(eT, eT, top, ALU.subtract).then_inc(s_d, 1)

                    def back(k):
                        dve.wait_ge(s_exps, k + 1)
                        settle(nc.vector)
                        nc.vector.tensor_copy(by_head[:, bass.ds(4 * k, 4)],
                                              ps[:, 1536:2048].rearrange("p (j g h) -> p j g h", j=4, g=GROUPS)).then_inc(s_back, 1)
                    turns(dve, JC // 4, back)

        class Norm:

            def __init__(self, pre, per):
                self.arg, self.root, self.per = sem(pre + "ln_arg"), sem(pre + "ln_root"), per

            def vector(self, step, r, sq, res, k, j):
                m, v, inv_std = small[:, 0:GT], small[:, 16:16 + GT], small[:, 32:32 + GT]
                step(nc.vector.tensor_reduce(m, r, AX.X, ALU.add))
                step(nc.vector.tensor_scalar(m, m, -1.0 / D, None, ALU.mult))
                step(nc.vector.tensor_tensor(r, r, bcast_last(m, D), ALU.add))
                step(nc.vector.tensor_tensor(sq, r, r, ALU.mult))
                step(nc.vector.tensor_reduce(v, sq, AX.X, ALU.add))
                step(nc.vector.tensor_scalar(v, v, 1.0 / D, EPS, ALU.mult, ALU.add))
                step.eng.sem_inc(self.arg, 1)
                step.eng.wait_ge(self.root, self.per * k + j + 1)
                step(nc.vector.tensor_tensor(res, r, bcast_last(inv_std, D), ALU.mult))

            def gpsimd(self, pool):
                def body(k):
                    for j in range(self.per):
                        pool.wait_ge(self.arg, self.per * k + j + 1)
                        nc.gpsimd.tensor_tensor(small[:, 32:32 + GT], small[:, 16:16 + GT], neg_half[:, 0:GT], ALU.pow).then_inc(self.root, 1)
                turns(pool, NG, body)

        def cols(ap, k, width=D):
            return ap[:, bass.ds(GT * width * k, GT * width)].rearrange("p (t f) -> p t f", f=width)

        def transposes(src, b):
            for i in range(GT):
                last = nc.tensor.transpose(ps[:, b * 512 + i * P:b * 512 + (i + 1) * P], src[:, i * D:(i + 1) * D], ident[:, :])
            return last

        def products(xT, weight, b, start=True, stop=True):
            for i in range(GT):
                last = nc.tensor.matmul(ps[:, b * 512 + i * D:b * 512 + (i + 1) * D], xT[:, i * P:(i + 1) * P], weight,
                                        start=start and i % 4 == 0, stop=stop, skip_group_check=True)
            return last

        def products_T(weight, xT, b, start=True, stop=True):
            for lo_c in (0, 512):
                hi_c = min(GC, lo_c + 512)
                last = nc.tensor.matmul(ps[:, b * 512 + lo_c:b * 512 + hi_c], weight, xT[:, lo_c:hi_c], start=start, stop=stop, skip_group_check=True)
            return last

        def pair(b):
            return ps[:, b * 512:b * 512 + GC]

        def table_rows(table):
            return table.rearrange("(t p) f -> p t f", p=P)

        new_stage()
        g_first = sem("g_first")
        g_dma = sem("g_dma")
        with nc.Block() as block:
            @block.vector
            def _(dve):
                nc.vector.tensor_tensor(tiled(acc_gcn), tiled(x_cur[:, :]), bcast_last(dinv[:, :], D), ALU.mult).then_inc(g_first, 1)

            @block.sync
            def _(sp):
                sp.wait_ge(g_first, 1)
                sp.dma_start(table_rows(t0), tiled(acc_gcn)).then_inc(g_dma, 16)
                sp.wait_ge(g_dma, 16)

        def convolve(which, table):
            new_stage()
            pre = which + "_"
            staged, lw_in, hot, mm = (sem(pre + n) for n in ("staged", "lw_in", "hot", "mm"))
            sums = Sums(pre, d_tile, acc_gcn, D)
            rows = arena[:, AT_BUF:AT_BUF + 16 * D].rearrange("p (s f) -> p s f", f=D)
            at = arena[:, AT_BUF + 16 * D:AT_BUF + 32 * D].rearrange("p (s f) -> p s f", f=D)
            lw_st = stage_lw[:, :].rearrange("p (s r) -> p s r", r=2)
            lw = d_lw[:, :].rearrange("p (c r) -> p c r", r=2)
            base = next_pass()

            def product(b, i):
                return ps[:, b * 1024 + i * D:b * 1024 + (i + 1) * D]
            with nc.Block() as block:
                @block.gpsimd
                def _(pool):
                    def free(k, b):
                        need(pool, mm, 2 * k + b - 1)
                    gathers(pool, table, rows, staged, free)

                @block.vector
                def _(dve):
                    sums.start(dve)
                    stage_first(d_src, staged)

                    def body(k):
                        for b in range(2):
                            n = 2 * k + b
                            stage_index(dve, d_src, staged, base, k, b)
                            settle(nc.vector)
                            nc.vector.tensor_copy(lw_st[:, 8 * b:8 * b + 8, :], lw[:, bass.ds(16 * k + 8 * b, 8), :]).then_inc(lw_in, 1)
                            adds = not isinstance(k, int) or b > 0
                            if adds:
                                sums.open(16 * k + 8 * b - 8, behind=not isinstance(k, int))
                                dve.wait_ge(mm, n)
                            dve.wait_ge(lw_in, n + 1)
                            for i in range(8):
                                s = 8 * b + i
                                one_hot = nc.vector.tensor_scalar(at[:, s, :], iota_row[:, :], lw_st[:, s, 0:1], lw_st[:, s, 1:2],
                                                                  ALU.is_equal, ALU.mult)
                                if i == 7:
                                    one_hot.then_inc(hot, 1)
                                if adds:
                                    sums.add(i, product(1 - b, i))
                    turns(dve, ITER, body)
                    sums.open(SC - 8)
                    dve.wait_ge(mm, HALVES)
                    for i in range(8):
                        sums.add(i, product(1, i))

                @block.tensor
                def _(pe):
                    def body(k):
                        for b in range(2):
                            n = 2 * k + b
                            pe.wait_ge(hot, n + 1)
                            need(pe, sums.drained, n - 1)
                            pe.wait_ge(landed[b], base + 128 * k + 128)
                            for i in range(8):
                                last = nc.tensor.matmul(product(b, i), at[:, 8 * b + i, :], rows[:, 8 * b + i, :], start=True, stop=True)
                            last.then_inc(mm, 1)
                    turns(pe, ITER, body)

        def scratch(o, n):
            return arena[:, o:o + n]

        convolve("c1", t0)

        new_stage()
        a_rdy, t_ps, t_sb, h_ps, n1_v, n1_dma = (sem("n1_" + n) for n in ("a", "tps", "tsb", "hps", "v", "dma"))
        A, aT, r = (scratch(AT_BUF + i * GC, GC) for i in range(3))
        with nc.Block() as block:
            @block.vector
            def _(dve):
                def body(k):
                    step = Chain(dve, n1_v, 3 * k)
                    step(nc.vector.tensor_tensor(tiled(A), cols(acc_gcn, k), bcast_last(dinv[:, bass.ds(GT * k, GT)], D), ALU.mult))
                    dve.sem_inc(a_rdy, 1)
                    dve.wait_ge(h_ps, k + 1)
                    step(nc.vector.tensor_tensor(tiled(r), tiled(pair(2)), bcast_mid(bias["L0_gnn_b1"], GT), ALU.add))
                    step(nc.vector.scalar_tensor_tensor(cols(acc_gcn, k), tiled(r), 0.0, bcast_last(dinv[:, bass.ds(GT * k, GT)], D), ALU.max, ALU.mult))
                turns(dve, NG, body)

            @block.tensor
            def _(pe):
                def body(k):
                    pe.wait_ge(a_rdy, k + 1)
                    transposes(A, 0).then_inc(t_ps, 1)
                    pe.wait_ge(t_sb, k + 1)
                    products(aT, w["L0_gnn_W1"], 2).then_inc(h_ps, 1)
                turns(pe, NG, body)

            @block.scalar
            def _(act):
                def body(k):
                    act.wait_ge(t_ps, k + 1)
                    nc.scalar.activation(aT, pair(0), ACT.Copy).then_inc(t_sb, 1)
                turns(act, NG, body)

            @block.sync
            def _(sp):
                sp.wait_ge(n1_v, 3 * NG)
                sp.dma_start(table_rows(t1), tiled(acc_gcn)).then_inc(n1_dma, 16)
                sp.wait_ge(n1_dma, 16)

        convolve("c2", t1)

        new_stage()
        a_rdy, t_ps, t_sb, h_ps, h_sb, y_ps, v_n, dma_n = (sem("n2_" + n) for n in ("a", "tps", "tsb", "hps", "hsb", "yps", "v", "dma"))
        z_rdy, zt_ps, zt_sb, xi_ps, xi_sb, uv_ps = (sem("n2_" + n) for n in ("z", "ztps", "ztsb", "xips", "xisb", "uvps"))
        norm = Norm("n2_", 2)
        A, aT, hT, r, sq = (scratch(AT_BUF + i * GC, GC) for i in range(5))
        rows2 = scratch(AT_BUF + 5 * GC, GT * (D + H)).rearrange("p (t f) -> p t f", f=D + H)
        with nc.Block() as block:
            @block.vector
            def _(dve):
                def body(k):
                    step = Chain(dve, v_n, 23 * k)
                    step(nc.vector.tensor_tensor(tiled(A), cols(acc_gcn, k), bcast_last(dinv[:, bass.ds(GT * k, GT)], D), ALU.mult))
                    dve.sem_inc(a_rdy, 1)
                    dve.wait_ge(y_ps, k + 1)
                    step(nc.vector.tensor_tensor(tiled(r), tiled(pair(4)), cols(x_cur, k), ALU.add))
                    step(nc.vector.tensor_tensor(tiled(r), tiled(r), bcast_mid(bias["L0_gnn_bfc"], GT), ALU.add))
                    norm.vector(step, tiled(r), tiled(sq), cols(x_cur, k), k, 0)
                    settle(nc.vector)
                    step(nc.vector.tensor_copy(tiled(r), cols(x_cur, k)))
                    norm.vector(step, tiled(r), tiled(sq), tiled(A), k, 1)
                    step(nc.vector.tensor_tensor(tiled(A), tiled(A), bcast_mid(bias["L1_gnn_ln_gamma"], GT), ALU.mult))
                    step(nc.vector.tensor_tensor(tiled(A), tiled(A), bcast_mid(bias["L1_gnn_ln_beta"], GT), ALU.add))
                    dve.sem_inc(z_rdy, 1)
                    dve.wait_ge(xi_ps, k + 1)
                    need(dve, dma_n, 16 * k)
                    step(nc.vector.tensor_tensor(rows2[:, :, 0:D], tiled(pair(2)), bcast_mid(bias["L1_gnn_b_in"], GT), ALU.add))
                    dve.wait_ge(uv_ps, k + 1)
                    uv = ps[:, 2048:2048 + GT * 2 * H].rearrange("p (t f) -> p t f", f=2 * H)
                    step(nc.vector.tensor_tensor(rows2[:, :, D:D + H], uv[:, :, 0:H], bcast_mid(b_u[:, :], GT), ALU.add))
                    settle(nc.vector)
                    step(nc.vector.tensor_copy(cols(v_tab, k, H), uv[:, :, H:2 * H]))
                    assert step.n == 23, step.n
                turns(dve, NG, body)

            @block.gpsimd
            def _(pool):
                norm.gpsimd(pool)

            @block.tensor
            def _(pe):
                def body(k):
                    pe.wait_ge(a_rdy, k + 1)
                    transposes(A, 0).then_inc(t_ps, 1)
                    pe.wait_ge(t_sb, k + 1)
                    products_T(w["L0_gnn_W2"], aT, 2).then_inc(h_ps, 1)
                    pe.wait_ge(h_sb, k + 1)
                    products(hT, w["L0_gnn_Wfc"], 4).then_inc(y_ps, 1)
                    pe.wait_ge(z_rdy, k + 1)
                    transposes(A, 0).then_inc(zt_ps, 1)
                    pe.wait_ge(zt_sb, k + 1)
                    products_T(w["L1_gnn_W_in"], aT, 6)
                    products(aT, w["L1_gnn_W_in"], 2).then_inc(xi_ps, 1)
                    pe.wait_ge(xi_sb, k + 1)
                    for i in range(GT):
                        last = nc.tensor.matmul(ps[:, 2048 + i * 2 * H:2048 + (i + 1) * 2 * H], hT[:, i * P:(i + 1) * P], w_uv[:, :], start=True, stop=True)
                    last.then_inc(uv_ps, 1)
                turns(pe, NG, body)

            @block.scalar
            def _(act):
                def body(k):
                    act.wait_ge(t_ps, k + 1)
                    nc.scalar.activation(aT, pair(0), ACT.Copy).then_inc(t_sb, 1)
                    act.wait_ge(h_ps, k + 1)
                    nc.scalar.activation(hT, pair(2), ACT.Relu, bias=col["L0_gnn_b2"]).then_inc(h_sb, 1)
                    act.wait_ge(zt_ps, k + 1)
                    nc.scalar.activation(aT, pair(0), ACT.Copy).then_inc(zt_sb, 1)
                    act.wait_ge(xi_ps, k + 1)
                    nc.scalar.activation(hT, pair(6), ACT.Identity, bias=col["L1_gnn_b_in"]).then_inc(xi_sb, 1)
                turns(act, NG, body)

            @block.sync
            def _(sp):
                def body(k):
                    sp.wait_ge(v_n, 23 * k + 23)
                    sp.dma_start(table_rows(t2)[:, bass.ds(GT * k, GT), :], rows2).then_inc(dma_n, 16)
                turns(sp, NG, body)
                sp.wait_ge(dma_n, 16 * NG)

        def score_pass(which, idx, table, width, keep, tab, tab_w):
            new_stage()
            pre = which + "_"
            staged, oT_hot, exp_ps, scored, v_s = (sem(pre + n) for n in ("staged", "hot", "expps", "scored", "v"))
            lo_in = [sem(pre + "lo0"), sem(pre + "lo1")]
            spilled = [sem(pre + "sp0"), sem(pre + "sp1")]
            gat = which == "gat"
            o = AT_BUF
            rows = arena[:, o:o + 16 * width].rearrange("p (s f) -> p s f", f=width)
            o += 16 * width
            if gat:
                o = AT_BUF + 16 * (D + H)
            lo_b = arena[:, o:o + 2048].rearrange("p (b c) -> p b c", b=2)
            hot_T = (arena[:, o + 2048:o + 4096] if gat else arena[:, AT_ACC + 2048:AT_ACC + 4096]).rearrange("p (b c) -> p b c", b=2)
            prod = arena[:, AT_ACC:AT_ACC + 2048].rearrange("p (b c) -> p b c", b=4)
            assert o + 2048 <= AW
            base = next_pass()
            lo_rows = d_loT.rearrange("(n c) e -> n (c e)", c=8)
            steps = 2 if gat else 4
            with nc.Block() as block:
                @block.gpsimd
                def _(pool):
                    def free(k, b):
                        need(pool, scored, 2 * k + b - 1)
                        need(pool, spilled[b], 16 * k)
                    gathers(pool, table, rows, staged, free)

                @block.sync
                def _(sp):
                    def body(k):
                        for b in range(2):
                            n = 2 * k + b
                            need(sp, oT_hot, n - 1)
                            sp.dma_start(lo_b[:, b, :], lo_rows[bass.ds(n, 1), :].to_broadcast([P, 8 * P])).then_inc(lo_in[b], 16)
                    turns(sp, ITER, body)

                @block.scalar
                def _(act):
                    def body(k):
                        for b in range(2):
                            n = 2 * k + b
                            act.wait_ge(landed[b], base + 128 * k + 128)
                            act.dma_start(spill[bass.ds(n, 1)].rearrange("o p (c f) -> p (o c) f", f=D),
                                          rows[:, 8 * b:8 * b + 8, keep:keep + D]).then_inc(spilled[b], 16)
                    turns(act, ITER, body)
                    for b in range(2):
                        act.wait_ge(spilled[b], 16 * ITER)

                @block.tensor
                def _(pe):
                    regs = registers(pe, pre + "tile")

                    def body(k):
                        for b in range(2):
                            n = 2 * k + b
                            tiles = tile_numbers(pe, regs, d_tile, 16 * k + 8 * b)
                            need(pe, scored, n - 1)
                            pe.wait_ge(oT_hot, n + 1)
                            for i in range(8):
                                o_ps = b * 1024 + i * tab_w
                                last = nc.tensor.matmul(ps[:, o_ps:o_ps + tab_w], hot_T[:, b, i * P:(i + 1) * P],
                                                        tab[:, bass.ds(tiles[i] * tab_w, tab_w)], start=True, stop=True)
                            last.then_inc(exp_ps, 1)
                    turns(pe, ITER, body)

                @block.vector
                def _(dve):
                    stage_first(idx, staged)

                    def body(k):
                        for b in range(2):
                            n = 2 * k + b
                            step = Chain(dve, v_s, steps * n)
                            stage_index(dve, idx, staged, base, k, b)
                            dve.wait_ge(lo_in[b], 16 * k + 16)
                            nc.vector.tensor_scalar(hot_T[:, b, :], lo_b[:, b, :], iota_part[:, 0:1], None, ALU.is_equal).then_inc(oT_hot, 1)
                            dve.wait_ge(landed[b], base + 128 * k + 128)
                            dve.wait_ge(exp_ps, n + 1)
                            e_out = e_all[:, bass.ds(64 * n, 64)]
                            if gat:
                                raw = prod[:, b, 0:64].rearrange("p (c h) -> p c h", h=H)
                                step(nc.vector.tensor_tensor(raw, ps[:, b * 1024:b * 1024 + 64].rearrange("p (c h) -> p c h", h=H),
                                                             rows[:, 8 * b:8 * b + 8, D:D + H], ALU.add))
                                step(nc.vector.scalar_tensor_tensor(e_out, prod[:, b, 0:64], 0.2, prod[:, b, 0:64], ALU.mult, ALU.max))
                            else:
                                for z in range(2):
                                    pr = prod[:, 2 * b + z, :]
                                    step(nc.vector.tensor_tensor(tiled(pr), tiled(ps[:, b * 1024 + z * 512:b * 1024 + z * 512 + 512]),
                                                                 rows[:, 8 * b + 4 * z:8 * b + 4 * z + 4, 0:D], ALU.mult))
                                    step(nc.vector.tensor_reduce(e_out[:, 32 * z:32 * z + 32], pr.rearrange("p (c d) -> p c d", d=DK), AX.X, ALU.add))
                            dve.sem_inc(scored, 1)
                    turns(dve, ITER, body)

        def weigh_pass(which, head_last):
            new_stage()
            pre = which + "_w_"
            W = D + H
            msg, mm, msg_v, zero, hot, lw_in = (sem(pre + n) for n in ("msg", "mm", "v", "zero", "hot", "lw_in"))
            lw_st = stage_lw[:, :].rearrange("p (s r) -> p s r", r=2)
            back_in = [sem(pre + "in0"), sem(pre + "in1")]
            sums = Sums(pre, d_tile, acc_att, W)
            rows = arena[:, AT_Q:AT_Q + 2048].rearrange("p (b c) -> p b c", b=2)
            at = arena[:, AT_Q + 2048:AT_Q + 4096].rearrange("p (b c n) -> p b c n", b=2, c=8)
            m = arena[:, AT_Q + 4096:AT_Q + 4096 + 16 * W].rearrange("p (b c f) -> p b c f", b=2, c=8)
            lw = d_lw[:, :].rearrange("p (c r) -> p c r", r=2)

            def product(b, i):
                o = b * 2048 + i // 3 * 512 + i % 3 * W
                return ps[:, o:o + W]
            with nc.Block() as block:
                @block.sync
                def _(sp):
                    def body(k):
                        for b in range(2):
                            n = 2 * k + b
                            need(sp, msg, n - 1)
                            sp.dma_start(rows[:, b, :], spill[bass.ds(n, 1)].rearrange("o p c -> p (o c)")).then_inc(back_in[b], 16)
                    turns(sp, ITER, body)

                @block.scalar
                def _(act):
                    def body(k):
                        for b in range(2):
                            n = 2 * k + b
                            need(act, mm, n - 1)
                            nc.scalar.activation(m[:, b, :, D:W], e_all[:, bass.ds(64 * n, 64)].rearrange("p (c h) -> p c h", h=H), ACT.Copy).then_inc(msg_v, 1)
                    turns(act, ITER, body)

                @block.gpsimd
                def _(pool):
                    def body(k):
                        for b in range(2):
                            n = 2 * k + b
                            need(pool, mm, n - 1)
                            pool.wait_ge(back_in[b], 16 * k + 16)
                            for i in range(8):
                                ex = e_all[:, bass.ds(64 * n + 8 * i, 8)]
                                if head_last:
                                    out_m = m[:, b, i, 0:D].rearrange("p (d h) -> p d h", h=H)
                                    in_m = rows[:, b, i * D:(i + 1) * D].rearrange("p (d h) -> p d h", h=H)
                                    ex = bcast_mid(ex, DK)
                                else:
                                    out_m = m[:, b, i, 0:D].rearrange("p (h d) -> p h d", h=H)
                                    in_m = rows[:, b, i * D:(i + 1) * D].rearrange("p (h d) -> p h d", h=H)
                                    ex = bcast_last(ex, DK)
                                last = nc.gpsimd.tensor_tensor(out_m, in_m, ex, ALU.mult)
                            last.then_inc(msg, 1)
                    turns(pool, ITER, body)

                @block.tensor
                def _(pe):
                    def body(k):
                        for b in range(2):
                            n = 2 * k + b
                            pe.wait_ge(hot, n + 1)
                            need(pe, sums.drained, n - 1)
                            pe.wait_ge(msg_v, n + 1)
                            pe.wait_ge(msg, n + 1)
                            for i in range(8):
                                last = nc.tensor.matmul(product(b, i), at[:, b, i], m[:, b, i], start=True, stop=True)
                            last.then_inc(mm, 1)
                    turns(pe, ITER, body)

                @block.vector
                def _(dve):
                    sums.start(dve)
                    nc.vector.memset(acc_att, 0.0).then_inc(zero, 1)
                    dve.wait_ge(zero, 1)

                    def nodes(n, b):
                        nc.vector.tensor_copy(lw_st[:, 8 * b:8 * b + 8, :], lw[:, bass.ds(8 * n, 8), :]).then_inc(lw_in, 1)

                    def one_hot(b, i):
                        return nc.vector.tensor_scalar(at[:, b, i], iota_row[:, :], lw_st[:, 8 * b + i, 0:1], None, ALU.is_equal)

                    nodes(0, 0)
                    dve.wait_ge(lw_in, 1)
                    for i in range(8):
                        first = one_hot(0, i)
                    first.then_inc(hot, 1)

                    def body(k):
                        for b in range(2):
                            n = 2 * k + b
                            adds = not isinstance(k, int) or b > 0
                            nodes(n + 1, 1 - b)
                            if adds:
                                sums.open(16 * k + 8 * b - 8, behind=not isinstance(k, int))
                                dve.wait_ge(mm, n)
                            dve.wait_ge(lw_in, n + 2)
                            for i in range(8):
                                last = one_hot(1 - b, i)
                                if i == 7:
                                    last.then_inc(hot, 1)
                                if adds:
                                    sums.add(i, product(1 - b, i))
                    turns(dve, ITER, body)
                    sums.open(SC - 8)
                    dve.wait_ge(mm, HALVES)
                    for i in range(8):
                        sums.add(i, product(1, i))

        score_pass("gat", d_src, t2, D + H, 0, v_tab, H)
        softmax_weights("gat")
        weigh_pass("gat", True)

        new_stage()
        wt_in, wt_v, wt_blk = sem("wt_in"), sem("wt_v"), sem("wt_blk")
        basis = {n: scratch(AT_Q + i * NB * D, NB * D).rearrange("p (b o) -> p b o", b=NB) for i, n in enumerate("akqv")}
        comp = {n: scratch(AT_Q + 16 * D + i * TN * NB, TN * NB).rearrange("p (t b) -> p t b", b=NB) for i, n in enumerate("akqv")}
        w_tmp = scratch(AT_Q + 20 * D, TN * D).rearrange("p (t o) -> p t o", t=TN)
        pri = scratch(AT_Q + 30 * D, TN * H)
        with nc.Block() as block:
            @block.sync
            def _(sp):
                for n in "akqv":
                    sp.dma_start(basis[n], t["L2_gnn_w_basis_" + n].rearrange("b (i o) -> i b o", o=D)).then_inc(wt_in, 16)
                    sp.dma_start(comp[n].rearrange("p t b -> p (t b)"), t["L2_gnn_w_comp_" + n].rearrange("t b -> (t b)").partition_broadcast(P)).then_inc(wt_in, 16)
                sp.dma_start(pri, t["L2_gnn_relation_pri"].rearrange("t h -> (t h)").partition_broadcast(P)).then_inc(wt_in, 16)
                sp.wait_ge(wt_v, 2)
                for n in ("att", "msg"):
                    for h in range(H):
                        sp.dma_start(rel[n][h * DK:(h + 1) * DK, :].rearrange("p (t o) -> p t o", t=TN)[:, :, h * DK:(h + 1) * DK],
                                     t["L2_gnn_relation_" + n][:, h].rearrange("t i j -> i t j")).then_inc(wt_blk, 16)
                sp.wait_ge(wt_blk, 16 * 2 * H)

            @block.vector
            def _(dve):
                step = Chain(dve, wt_v)
                step(nc.vector.memset(rel["att"], 0.0))
                step(nc.vector.memset(rel["msg"], 0.0))
                dve.wait_ge(wt_in, 16 * 9)
                for n in "akqv":
                    for b in range(NB):
                        res = w_typed[n] if b == 0 else w_tmp
                        step(nc.vector.tensor_tensor(res, bcast_mid(basis[n][:, b, :], TN), bcast_last(comp[n][:, :, b], D), ALU.mult))
                        if b:
                            step(nc.vector.tensor_tensor(w_typed[n], w_typed[n], w_tmp, ALU.add))
                dve.wait_ge(wt_blk, 16 * 2 * H)
                step(nc.vector.tensor_scalar(pri, pri, DK ** -0.5, None, ALU.mult))
                att = rel["att"].rearrange("p (c j) -> p c j", j=DK)
                step(nc.vector.tensor_tensor(att, att, bcast_last(pri, DK), ALU.mult))

        def load_types(sp, done):
            sp.dma_start(ntb[:, 0:N], t["node_type_8"].partition_broadcast(P)).then_inc(done, 16)

        def attention_out(step, k, out_ap, head_last):
            den = small[:, 64:64 + GT * H].rearrange("p (t h) -> p t h", h=H)
            acc = cols(acc_att, k, D + H)
            step(nc.vector.tensor_scalar(den, acc[:, :, D:D + H], 1e-30, None, ALU.max))
            step(nc.vector.reciprocal(den, den))
            if head_last:
                step(nc.vector.tensor_tensor(out_ap.rearrange("p (t d h) -> p t d h", t=GT, h=H), acc[:, :, 0:D].rearrange("p t (d h) -> p t d h", h=H),
                                             den.unsqueeze(2).to_broadcast([P, GT, DK, H]), ALU.mult))
            else:
                step(nc.vector.tensor_tensor(out_ap.rearrange("p (t h d) -> p t h d", t=GT, h=H), acc[:, :, 0:D].rearrange("p t (h d) -> p t h d", h=H),
                                             den.unsqueeze(3).to_broadcast([P, GT, H, DK]), ALU.mult))

        new_stage()
        a_rdy, t_ps, t_sb, y_ps, x_rdy, xt_ps, xt_sb, xm_rdy, xm_used, v_n = (sem("n3_" + n) for n in (
            "a", "tps", "tsb", "yps", "x", "xtps", "xtsb", "xm", "xmused", "v"))
        kv_sb, q_sb, kv_ps, k_out, v_out, nt_in, nt_pad = (sem("n3_" + n) for n in ("kvsb", "qsb", "kvps", "kout", "vout", "nt", "ntpad"))
        kv_dma = [sem("n3_dma0"), sem("n3_dma1")]
        norm = Norm("n3_", 1)
        S = [scratch(AT_BUF + i * GC, GC) for i in range(5)]
        A, aT, r, sq, x2T = S
        kT, vT, xm = S[0], S[1], [S[2], S[3]]
        kv_st = scratch(AT_BUF + 5 * GC, 2 * 1024).rearrange("p (z t f) -> p z t f", z=2, f=2 * D)
        t3_rows = t3.rearrange("(t n) f -> n t f", t=TN)
        with nc.Block() as block:
            @block.sync
            def _(sp):
                sp.wait_ge(nt_pad, 1)
                load_types(sp, nt_in)

                def body(k):
                    for i in range(GT):
                        for z in range(2):
                            n = 2 * GT * k + 2 * i + z
                            sp.wait_ge(k_out, n + 1)
                            sp.wait_ge(v_out, n + 1)
                            sp.dma_start(t3_rows[bass.ds(P * (GT * k + i), P), 4 * z:4 * z + 4, :], kv_st[:, z]).then_inc(kv_dma[z], 16)
                turns(sp, NG, body)
                for z in range(2):
                    sp.wait_ge(kv_dma[z], 16 * GT * NG)

            @block.gpsimd
            def _(pool):
                norm.gpsimd(pool)

            @block.vector
            def _(dve):
                nc.vector.memset(ntb[:, N:NP], 0).then_inc(nt_pad, 1)

                def body(k):
                    step = Chain(dve, v_n, 14 * k)
                    attention_out(step, k, A, True)
                    dve.sem_inc(a_rdy, 1)
                    dve.wait_ge(y_ps, k + 1)
                    need(dve, xm_used, 8 * k)
                    step(nc.vector.tensor_tensor(tiled(r), tiled(pair(2)), cols(x_cur, k), ALU.add))
                    step(nc.vector.tensor_tensor(tiled(r), tiled(r), bcast_mid(bias["L1_gnn_b_ff"], GT), ALU.add))
                    norm.vector(step, tiled(r), tiled(sq), tiled(sq), k, 0)
                    dve.sem_inc(x_rdy, 1)
                    settle(nc.vector)
                    step(nc.vector.tensor_copy(cols(x_cur, k), tiled(sq)))
                    dve.wait_ge(xt_sb, k + 1)
                    if isinstance(k, int):
                        dve.wait_ge(nt_in, 16)
                    for ty in range(TN):
                        if ty >= 2:
                            dve.wait_ge(xm_used, TN * k + ty - 1)
                        nc.vector.scalar_tensor_tensor(xm[ty % 2], ntb[:, bass.ds(GC * k, GC)], float(ty), x2T, ALU.is_equal, ALU.mult).then_inc(xm_rdy, 1)
                    dve.wait_ge(xm_used, TN * k + TN)
                    settle(nc.vector)
                    step(nc.vector.tensor_copy(q_tab[:, bass.ds(GC * k, GC)], pair(6)))
                    dve.sem_inc(q_sb, 1)
                    assert step.n == 14, step.n
                    for i in range(GT):
                        for z in range(2):
                            n = 2 * GT * k + 2 * i + z
                            dve.wait_ge(kv_ps, GT * k + i + 1)
                            need(dve, kv_dma[z], 16 * (GT * k + i))
                            b = 4 * (i % 2) + 2 + z
                            nc.vector.tensor_copy(kv_st[:, z, :, D:2 * D], tiled(bank(b))).then_inc(v_out, 1)
                turns(dve, NG, body)

            @block.tensor
            def _(pe):
                def body(k):
                    pe.wait_ge(a_rdy, k + 1)
                    need(pe, v_out, 2 * GT * k)
                    need(pe, k_out, 2 * GT * k)
                    transposes(A, 0).then_inc(t_ps, 1)
                    pe.wait_ge(t_sb, k + 1)
                    products(aT, w["L1_gnn_W_ff"], 2).then_inc(y_ps, 1)
                    pe.wait_ge(x_rdy, k + 1)
                    for i in range(GT):
                        tile = sq[:, i * D:(i + 1) * D]
                        last = nc.tensor.transpose(ps[:, i * P:(i + 1) * P], tile, ident[:, :])
                    last.then_inc(xt_ps, 1)
                    for ty in range(TN):
                        pe.wait_ge(xm_rdy, TN * k + ty + 1)
                        f = dict(start=ty == 0, stop=ty == TN - 1)
                        products_T(w_typed["k"][:, ty, :], xm[ty % 2], 2, **f)
                        products_T(w_typed["v"][:, ty, :], xm[ty % 2], 4, **f)
                        products(xm[ty % 2], w_typed["q"][:, ty, :], 6, **f).then_inc(xm_used, 1)
                    pe.wait_ge(kv_sb, 2 * k + 2)
                    pe.wait_ge(q_sb, k + 1)
                    for i in range(GT):
                        if i >= 2:
                            pe.wait_ge(k_out, 2 * GT * k + 2 * (i - 1))
                            pe.wait_ge(v_out, 2 * GT * k + 2 * (i - 1))
                        for src_T, name, b in ((kT, "att", 4 * (i % 2)), (vT, "msg", 4 * (i % 2) + 2)):
                            for z in range(2):
                                last = nc.tensor.matmul(bank(b + z), src_T[:, i * P:(i + 1) * P], rel[name][:, z * 512:(z + 1) * 512], start=True, stop=True)
                        last.then_inc(kv_ps, 1)
                turns(pe, NG, body)

            @block.scalar
            def _(act):
                def body(k):
                    act.wait_ge(t_ps, k + 1)
                    nc.scalar.activation(aT, pair(0), ACT.Copy).then_inc(t_sb, 1)
                    act.wait_ge(xt_ps, k + 1)
                    nc.scalar.activation(x2T, pair(0), ACT.Copy).then_inc(xt_sb, 1)
                    act.wait_ge(xm_used, TN * k + TN)
                    nc.scalar.activation(kT, pair(2), ACT.Copy).then_inc(kv_sb, 1)
                    nc.scalar.activation(vT, pair(4), ACT.Copy).then_inc(kv_sb, 1)
                    for i in range(GT):
                        for z in range(2):
                            act.wait_ge(kv_ps, GT * k + i + 1)
                            need(act, kv_dma[z], 16 * (GT * k + i))
                            nc.scalar.activation(kv_st[:, z, :, 0:D], tiled(bank(4 * (i % 2) + z)), ACT.Copy).then_inc(k_out, 1)
                turns(act, NG, body)

        score_pass("hgt", d_typed, t3, 2 * D, D, q_tab, D)
        softmax_weights("hgt")
        weigh_pass("hgt", False)

        AT_L3 = 21000
        acc_l3 = arena[:, AT_L3:AT_L3 + NT * 2 * D]
        U_T, W_T, VDE = l3_T[:, 0:D], l3_T[:, D:2 * D], l3_T[:, 2 * D:6 * D]
        new_stage()
        a_rdy, t_ps, t_sb, xm_rdy, xm_used, o_ps, x_rdy, v_n = (sem("n4_" + n) for n in ("a", "tps", "tsb", "xm", "xmused", "ops", "x", "v"))
        xt_ps, xt_sb, h_ps, h_sb, w_ps, vde_ps, vde_used, nt_in, nt_pad, rows_rdy = (sem("n4_" + n) for n in (
            "xtps", "xtsb", "hps", "hsb", "wps", "vdeps", "vdeused", "nt", "ntpad", "rows"))
        dma_n = sem("n4_dma")
        norm = Norm("n4_", 1)
        rows4 = scratch(1024, GT * 3 * D).rearrange("p (t f) -> p t f", f=3 * D)
        xm = [scratch(1024, GC), scratch(1024 + GC, GC)]
        A, aT, sq = scratch(3712, GC), scratch(3712 + GC, GC), scratch(3712 + 2 * GC, GC)
        r = scratch(19720, GC)
        x2T, x3T, hT = sq, aT, A
        p_st, d_st = r, sq
        with nc.Block() as block:
            @block.sync
            def _(sp):
                sp.wait_ge(nt_pad, 1)
                load_types(sp, nt_in)

                def body(k):
                    sp.wait_ge(rows_rdy, k + 1)
                    sp.dma_start(table_rows(t4)[:, bass.ds(GT * k, GT), :], rows4).then_inc(dma_n, 16)
                    sp.dma_start(p_dram[:, bass.ds(GC * k, GC)], p_st).then_inc(dma_n, 16)
                    sp.dma_start(dp_dram[:, bass.ds(GC * k, GC)], d_st).then_inc(dma_n, 16)
                turns(sp, NG, body)
                sp.wait_ge(dma_n, 48 * NG)

            @block.gpsimd
            def _(pool):
                norm.gpsimd(pool)

            @block.vector
            def _(dve):
                nc.vector.memset(ntb[:, N:NP], 0).then_inc(nt_pad, 1)
                PER = 3 + 1 + 2 + 8 + 2 + 5 * GT + 4

                def body(k):
                    step = Chain(dve, v_n, PER * k)
                    inv_b = bcast_last(inv[:, bass.ds(GT * k, GT)], D)
                    attention_out(step, k, A, False)
                    need(dve, dma_n, 48 * k)
                    settle(nc.vector)
                    step(nc.vector.tensor_copy(tiled(sq), cols(x_cur, k)))
                    dve.sem_inc(a_rdy, 1)
                    dve.wait_ge(t_sb, 2 * k + 2)
                    if isinstance(k, int):
                        dve.wait_ge(nt_in, 16)
                    for ty in range(TN):
                        if ty >= 2:
                            dve.wait_ge(xm_used, TN * k + ty - 1)
                        nc.vector.scalar_tensor_tensor(xm[ty % 2], ntb[:, bass.ds(GC * k, GC)], float(ty), aT, ALU.is_equal, ALU.mult).then_inc(xm_rdy, 1)
                    dve.wait_ge(o_ps, k + 1)
                    step(nc.vector.tensor_tensor(tiled(r), tiled(pair(2)), bcast_mid(bias["L2_gnn_bias"], GT), ALU.add))
                    step(nc.vector.scalar_tensor_tensor(tiled(r), tiled(r), 0.0, cols(x_cur, k), ALU.max, ALU.add))
                    norm.vector(step, tiled(r), tiled(sq), tiled(sq), k, 0)
                    dve.sem_inc(x_rdy, 1)
                    settle(nc.vector)
                    step(nc.vector.tensor_copy(cols(x_cur, k), tiled(sq)))
                    dve.wait_ge(w_ps, k + 1)
                    y = rows4[:, :, 2 * D:3 * D]
                    step(nc.vector.tensor_tensor(y, tiled(pair(2)), bcast_mid(bias["L3_gnn_W_b"], GT), ALU.add))
                    step(nc.vector.tensor_tensor(y, y, inv_b, ALU.mult))
                    for i in range(GT):
                        dve.wait_ge(vde_ps, GT * k + i + 1)
                        b = 6 + i % 2
                        z = rows4[:, i, D:2 * D]
                        part = [ps[:, b * 512 + j * D:b * 512 + (j + 1) * D] for j in range(4)]
                        step(nc.vector.tensor_tensor(p_st[:, i * D:(i + 1) * D], part[0], bias["L3_gnn_V_b"], ALU.add))
                        step(nc.vector.tensor_copy(rows4[:, i, 0:D], part[1]))
                        step(nc.vector.tensor_tensor(d_st[:, i * D:(i + 1) * D], part[2], bias["L3_gnn_D_b"], ALU.add))
                        step(nc.vector.tensor_tensor(z, part[3], bias["L3_gnn_E_b"], ALU.add))
                        dve.sem_inc(vde_used, 1)
                        step(nc.vector.tensor_tensor(z, z, rows4[:, i, 2 * D:3 * D], ALU.mult))
                    dve.sem_inc(rows_rdy, 1)
                    acc = cols(acc_l3, k, 2 * D)
                    step(nc.vector.tensor_tensor(acc[:, :, 0:D], tiled(p_st), rows4[:, :, 0:D], ALU.add))
                    step(nc.vector.scalar_tensor_tensor(acc[:, :, 0:D], acc[:, :, 0:D], 0.0, y, ALU.max, ALU.mult))
                    step(nc.vector.tensor_tensor(acc[:, :, 0:D], acc[:, :, 0:D], rows4[:, :, D:2 * D], ALU.add))
                    step(nc.vector.tensor_copy(acc[:, :, D:2 * D], y))
                    assert step.n == PER, (step.n, PER)
                turns(dve, NG, body)

            @block.tensor
            def _(pe):
                def body(k):
                    pe.wait_ge(a_rdy, k + 1)
                    transposes(A, 0).then_inc(t_ps, 1)
                    for i in range(GT):
                        last = nc.tensor.transpose(ps[:, 2048 + i * P:2048 + (i + 1) * P], sq[:, i * D:(i + 1) * D], ident[:, :])
                    last.then_inc(t_ps, 1)
                    for ty in range(TN):
                        pe.wait_ge(xm_rdy, TN * k + ty + 1)
                        products(xm[ty % 2], w_typed["a"][:, ty, :], 2, start=ty == 0, stop=False).then_inc(xm_used, 1)
                    products(x2T, w["L2_gnn_loop_weight"], 2, start=False, stop=True).then_inc(o_ps, 1)
                    pe.wait_ge(x_rdy, k + 1)
                    for i in range(GT):
                        last = nc.tensor.transpose(ps[:, i * P:(i + 1) * P], sq[:, i * D:(i + 1) * D], ident[:, :])
                    last.then_inc(xt_ps, 1)
                    pe.wait_ge(xt_sb, k + 1)
                    products_T(U_T, x3T, 4).then_inc(h_ps, 1)
                    products(x3T, W_T, 2).then_inc(w_ps, 1)
                    pe.wait_ge(h_sb, k + 1)
                    for i in range(GT):
                        need(pe, vde_used, GT * k + i - 1)
                        nc.tensor.matmul(bank(6 + i % 2), hT[:, i * P:(i + 1) * P], VDE, start=True, stop=True).then_inc(vde_ps, 1)
                turns(pe, NG, body)

            @block.scalar
            def _(act):
                def body(k):
                    act.wait_ge(t_ps, 2 * k + 1)
                    nc.scalar.activation(aT, pair(0), ACT.Copy).then_inc(t_sb, 1)
                    act.wait_ge(t_ps, 2 * k + 2)
                    nc.scalar.activation(x2T, pair(4), ACT.Copy).then_inc(t_sb, 1)
                    act.wait_ge(xt_ps, k + 1)
                    nc.scalar.activation(x3T, pair(0), ACT.Copy).then_inc(xt_sb, 1)
                    act.wait_ge(h_ps, k + 1)
                    nc.scalar.activation(hT, pair(4), ACT.Identity, bias=col["L3_gnn_U_b"]).then_inc(h_sb, 1)
                turns(act, NG, body)

        new_stage()
        staged, oT_hot, hot, p_ps, mm, v_s = (sem("l3_" + n) for n in ("staged", "hotT", "hot", "pps", "mm", "v"))
        lo_in = [sem("l3_lo0"), sem("l3_lo1")]
        got_rows = [[sem(f"l3_rows{b}{z}") for z in range(2)] for b in range(2)]
        p_in, a_abs, minus, minus_in = sem("l3_p_in"), sem("l3_abs"), sem("l3_minus"), sem("l3_minus_in")
        sums = Sums("l3_", s_tile, acc_l3, 2 * D)
        p_tab = arena[:, 1024:1024 + NP]
        o = 1024 + NP
        rows = arena[:, o:o + 16 * 3 * D].rearrange("p (s f) -> p s f", f=3 * D)
        o += 16 * 3 * D
        lo_b = arena[:, o:o + 2048].rearrange("p (b c) -> p b c", b=2)
        o += 2048
        hot_T = arena[:, o:o + 2048].rearrange("p (b c) -> p b c", b=2)
        o += 2048
        at = arena[:, o:o + 2048].rearrange("p (b c n) -> p b c n", b=2, c=8)
        o += 2048
        prod = arena[:, o:o + 1024].rearrange("p (z c) -> p z c", z=2)
        o += 1024
        minus_part, minus_lo = small[:, 0:1], small[:, 8:24]
        assert o <= AT_L3, o
        lo_rows = s_loT.rearrange("(n c) e -> n (c e)", c=8)

        def product(i):
            return ps[:, 2048 + i * 2 * D:2048 + (i + 1) * 2 * D]
        with nc.Block() as block:
            @block.gpsimd
            def _(pool):
                def body(k):
                    for b in range(2):
                        n = 2 * k + b
                        pool.wait_ge(staged, n + 1)
                        for z in range(2):
                            need(pool, mm, 2 * n + z - 3)
                            settle(pool)
                            for i in range(8 * b + 4 * z, 8 * b + 4 * z + 4):
                                pool.indirect_dma_start(out=rows[:, i, :], out_offset=None, in_=t4,
                                                        in_offset=bass.IndirectOffsetOnAxis(ap=stage_idx[:, i:i + 1], axis=0)).then_inc(got_rows[b][z], 16)
                turns(pool, ITER, body)

            @block.sync
            def _(sp):
                sp.dma_start(p_tab, p_dram).then_inc(p_in, 16)

                def body(k):
                    for b in range(2):
                        n = 2 * k + b
                        need(sp, oT_hot, n - 1)
                        sp.dma_start(lo_b[:, b, :], lo_rows[bass.ds(n, 1), :].to_broadcast([P, 8 * P])).then_inc(lo_in[b], 16)
                turns(sp, ITER, body)

            @block.scalar
            def _(act):
                act.wait_ge(minus, 1)

                def body(k):
                    for b in range(2):
                        n = 2 * k + b
                        need(act, p_ps, 2 * n - 2)
                        act.wait_ge(lo_in[b], 16 * k + 16)
                        nc.scalar.activation(hot_T[:, b, :], lo_b[:, b, :], ACT.Abs, bias=minus_part).then_inc(a_abs, 1)
                        act.wait_ge(a_abs, 2 * n + 1)
                        nc.scalar.activation(hot_T[:, b, :], hot_T[:, b, :], ACT.Relu, bias=ones[:, 0:1], scale=-1.0).then_inc(oT_hot, 1)
                        nc.scalar.activation(minus_lo[:, 8 * b:8 * b + 8], s_lo[:, bass.ds(8 * n, 8)], ACT.Copy, scale=-1.0).then_inc(minus_in, 1)
                        need(act, mm, 2 * n - 2)
                        act.wait_ge(minus_in, n + 1)
                        for i in range(8):
                            last = nc.scalar.activation(at[:, b, i], iota_row[:, :], ACT.Abs, bias=minus_lo[:, 8 * b + i:8 * b + i + 1])
                        last.then_inc(a_abs, 1)
                        act.wait_ge(a_abs, 2 * n + 2)
                        nc.scalar.activation(at[:, b], at[:, b], ACT.Relu, bias=ones[:, 0:1], scale=-1.0).then_inc(hot, 1)
                turns(act, ITER, body)

            @block.tensor
            def _(pe):
                regs = registers(pe, "l3_p_tile")
                pe.wait_ge(p_in, 16)

                def expand(k, b):
                    n = 2 * k + b
                    tiles = tile_numbers(pe, regs, s_tile, 16 * k + 8 * b)
                    pe.wait_ge(oT_hot, n + 1)
                    need(pe, v_s, 6 * n - 6)
                    for i in range(8):
                        o_ps = b * 1024 + i * D
                        last = nc.tensor.matmul(ps[:, o_ps:o_ps + D], hot_T[:, b, i * P:(i + 1) * P],
                                                p_tab[:, bass.ds(tiles[i] * D, D)], start=True, stop=True)
                        if i % 4 == 3:
                            last.then_inc(p_ps, 1)

                def sum_up(n, b):
                    pe.wait_ge(hot, n + 1)
                    for z in range(2):
                        need(pe, sums.drained, 2 * n + z - 1)
                        pe.wait_ge(v_s, 6 * n + 3 * z + 3)
                        for i in range(4 * z, 4 * z + 4):
                            last = nc.tensor.matmul(product(i), at[:, b, i], rows[:, 8 * b + i, D:3 * D], start=True, stop=True)
                        last.then_inc(mm, 1)

                def body(k):
                    for b in range(2):
                        expand(k, b)
                        if not isinstance(k, int) or b > 0:
                            sum_up(2 * k + b - 1, 1 - b)
                turns(pe, ITER, body)
                sum_up(HALVES - 1, 1)

            @block.vector
            def _(dve):
                sums.start(dve)
                nc.vector.tensor_scalar(minus_part, iota_part[:, 0:1], -1.0, None, ALU.mult).then_inc(minus, 1)
                stage_first(s_dst, staged)

                def body(k):
                    for b in range(2):
                        n = 2 * k + b
                        adds = not isinstance(k, int) or b > 0
                        for z in range(2):
                            need(dve, got_rows[1 - b][z], 64 * (k + b))
                        settle(nc.vector)
                        nc.vector.tensor_copy(stage_idx[:, 8 * (1 - b):8 * (1 - b) + 8], s_dst[:, bass.ds(8 * n + 8, 8)]).then_inc(staged, 1)
                        if adds:
                            sums.open(16 * k + 8 * b - 8, behind=not isinstance(k, int))
                        need(dve, v_s, 6 * n)
                        for z in range(2):
                            got = rows[:, 8 * b + 4 * z:8 * b + 4 * z + 4, :]
                            pr = tiled(prod[:, z, :])
                            if adds:
                                dve.wait_ge(mm, 2 * n - 1 + z)
                                sums.add(4 * z, product(4 * z))
                            dve.wait_ge(got_rows[b][z], 64 * k + 64)
                            dve.wait_ge(p_ps, 2 * n + z + 1)
                            nc.vector.tensor_tensor(pr, tiled(ps[:, b * 1024 + z * 512:b * 1024 + z * 512 + 512]), got[:, :, 0:D], ALU.add).then_inc(v_s, 1)
                            if adds:
                                sums.add(4 * z + 1, product(4 * z + 1))
                            dve.wait_ge(v_s, 6 * n + 3 * z + 1)
                            nc.vector.scalar_tensor_tensor(pr, pr, 0.0, got[:, :, 2 * D:3 * D], ALU.max, ALU.mult).then_inc(v_s, 1)
                            if adds:
                                sums.add(4 * z + 2, product(4 * z + 2))
                            dve.wait_ge(v_s, 6 * n + 3 * z + 2)
                            nc.vector.tensor_tensor(got[:, :, D:2 * D], pr, got[:, :, D:2 * D], ALU.add).then_inc(v_s, 1)
                            if adds:
                                sums.add(4 * z + 3, product(4 * z + 3))
                                if z == 0:
                                    sums.drain(4)
                turns(dve, ITER, body)
                sums.open(SC - 8)
                for i in range(8):
                    if i % 4 == 0:
                        dve.wait_ge(mm, 2 * HALVES - 1 + i // 4)
                    sums.add(i, product(i))

        new_stage()
        dp_in, v_n, out_dma = sem("n5_dp"), sem("n5_v"), sem("n5_out")
        norm = Norm("n5_", 1)
        dp_all = arena[:, 1024:1024 + NP]
        r, sq = scratch(8192, GC), scratch(8192 + GC, GC)
        with nc.Block() as block:
            @block.gpsimd
            def _(pool):
                norm.gpsimd(pool)

            @block.vector
            def _(dve):
                dve.wait_ge(dp_in, 16)

                def body(k):
                    step = Chain(dve, v_n, 11 * k)
                    acc = cols(acc_l3, k, 2 * D)
                    step(nc.vector.tensor_tensor(tiled(r), cols(dp_all, k), acc[:, :, D:2 * D], ALU.mult))
                    step(nc.vector.tensor_tensor(tiled(r), tiled(r), acc[:, :, 0:D], ALU.add))
                    step(nc.vector.tensor_tensor(tiled(r), tiled(r), bcast_last(inv[:, bass.ds(GT * k, GT)], D), ALU.mult))
                    step(nc.vector.tensor_tensor(tiled(r), tiled(r), cols(x_cur, k), ALU.add))
                    norm.vector(step, tiled(r), tiled(sq), cols(x_cur, k), k, 0)
                turns(dve, NG, body)

            @block.sync
            def _(sp):
                sp.dma_start(dp_all, dp_dram).then_inc(dp_in, 16)
                sp.wait_ge(v_n, 11 * NG)
                sp.dma_start(out[0:(NT - 1) * P, :].rearrange("(t p) f -> p t f", p=P), tiled(x_cur[:, 0:(NT - 1) * D])).then_inc(out_dma, 16)
                sp.dma_start(out[(NT - 1) * P:N, :], x_cur[0:LAST, (NT - 1) * D:NT * D]).then_inc(out_dma, 16)
                sp.wait_ge(out_dma, 32)


def kernel(**inputs):
    import numpy as np
    import concourse.bacc as bacc
    from concourse.bass_utils import run_bass_kernel_spmd as run

    nc = bacc.Bacc("TRN2", target_bir_lowering=False, num_devices=1)
    arrays, t = {}, {}
    for n in inputs:
        a = np.ascontiguousarray(inputs[n])
        arrays["in_" + n] = a
        t[n] = nc.dram_tensor("in_" + n, a.shape, mybir.dt.from_np(a.dtype), kind="ExternalInput").ap()
    out = nc.dram_tensor("out", (N, D), F32, kind="ExternalOutput").ap()
    build(nc, t, out)
    r = run(nc, [arrays], core_ids=[0])
    return r.results[0]["out"]
```

```python
import concourse.bass as bass
from concourse import mybir
from contextlib import ExitStack

F32 = mybir.dt.float32
BF16 = mybir.dt.bfloat16
I32 = mybir.dt.int32
ALU = mybir.AluOpType
ACT = mybir.ActivationFunctionType
AX = mybir.AxisListType

N = 6250
E = 100000
D = 128
P = 128
NT = -(-N // P)
NP = NT * P
GT = 7
NG = NT // GT
GC = GT * D
LAST = N - (NT - 1) * P
EC = 125
UC = E // EC
UG = UC // 8
GROUPS = 16
JC = 52
SC = GROUPS * JC
HALVES = SC // 8
ITER = HALVES // 2
ROWS = SC * P
H = 8
DK = D // H
TN = 8
NB = 4
TL = JC * P
SX = SC + 8
BIG = 1.0e30
PAD_KEY = 1.0e6
HALF = (P - 1) / 2
EPS = 1e-5
AW = 34100
assert SC >= (E + NT * (P - 1)) // P and NG * GT == NT and UG % 2 == 0


class Chain:

    def __init__(self, eng, sem, base=0):
        self.eng, self.sem, self.base, self.n = eng, sem, base, 0

    def __call__(self, ins):
        self.n += 1
        ins.then_inc(self.sem, 1)
        self.eng.wait_ge(self.sem, self.base + self.n)


def settle(eng):
    eng.nop(nofuse=True)


def turns(eng, count, body):
    body(0)
    with eng.Fori(1, count) as k:
        body(k)


def need(eng, sem, value):
    if not isinstance(value, int) or value > 0:
        eng.wait_ge(sem, value)


def bcast_last(ap, n):
    shape = list(ap.shape) + [n]
    return ap.unsqueeze(len(shape) - 1).to_broadcast(shape)


def bcast_mid(ap, n):
    return ap.unsqueeze(1).to_broadcast([ap.shape[0], n] + list(ap.shape[1:]))


def build(nc, t, out):
    ctx = ExitStack()
    with ctx:
        def sb(name, cols, dt=F32):
            return ctx.enter_context(nc.sbuf_tensor(name, [P, cols], dt))

        stage_sems = []

        def sem(name):
            stage_sems.append(nc.alloc_semaphore(name))
            return stage_sems[-1]

        def new_stage():
            nc.clear_and_free_semaphores(list(stage_sems))
            nc.all_engine_barrier()
            stage_sems.clear()

        def dram(name, shape, dt=F32):
            return nc.dram_tensor(name, shape, dt).ap()

        x_cur = sb("x_cur", NT * D)
        iota_row = sb("iota_row", P)
        iota_part = sb("iota_part", 1)
        ident = sb("ident", P)
        earlier = sb("earlier", P)
        before = sb("before", P)
        ones = sb("ones", P)
        int_tmp = sb("int_tmp", P, I32)
        int_tmp2 = sb("int_tmp2", 1, I32)
        d_src = sb("d_src", SX, I32)
        d_typed = sb("d_typed", SX, I32)
        d_lw = sb("d_lw", SX * 2)
        s_dst = sb("s_dst", SX, I32)
        s_lo = sb("s_lo", SX)
        d_tile = sb("d_tile", SC, I32)
        s_tile = sb("s_tile", SC, I32)
        dinv = sb("dinv", NT)
        inv = sb("inv", NT)
        small = sb("small", 512)
        neg_half = sb("neg_half", 64)
        stage_idx = sb("stage_idx", 16, I32)
        stage_lw = sb("stage_lw", 32)
        bias_names = ["L0_gnn_b1", "L0_gnn_bfc", "L1_gnn_ln_gamma", "L1_gnn_ln_beta", "L1_gnn_b_in", "L1_gnn_b_ff",
                      "L2_gnn_bias", "L3_gnn_W_b", "L3_gnn_V_b", "L3_gnn_D_b", "none", "L3_gnn_E_b"]
        bias_sb = sb("bias_sb", len(bias_names) * D)
        bias = {n: bias_sb[:, i * D:(i + 1) * D] for i, n in enumerate(bias_names)}
        V_AT = bias_names.index("L3_gnn_V_b") * D
        vde_bias = bias_sb[:, V_AT:V_AT + 4 * D]
        b_u = sb("b_u", H)
        col_names = ["L0_gnn_b2", "L1_gnn_b_in", "L3_gnn_U_b"]
        col_sb = sb("col_sb", len(col_names))
        col = {n: col_sb[:, i:i + 1] for i, n in enumerate(col_names)}
        w_names = ["L0_gnn_W1", "L0_gnn_W2", "L0_gnn_Wfc", "L1_gnn_W_in", "L1_gnn_W_ff", "L2_gnn_loop_weight"]
        w_sb = sb("w_sb", len(w_names) * D)
        w = {n: w_sb[:, i * D:(i + 1) * D] for i, n in enumerate(w_names)}
        w_uv = sb("w_uv", 2 * H)
        l3_T = sb("l3_T", 6 * D)
        arena = sb("arena", AW)

        ps = ctx.enter_context(nc.psum_tensor("ps", [P, 8 * 512], F32))

        def bank(b, n=512, parts=P):
            return ps[0:parts, b * 512:b * 512 + n]

        d_rec = dram("d_rec", [ROWS, 4])
        s_rec = dram("s_rec", [ROWS, 2])
        d_loT = dram("d_loT", [SC, P])
        s_loT = dram("s_loT", [SC, P])
        penT = dram("penT", [P, TL + 1])
        t0 = dram("t0", [NP, D])
        t1 = dram("t1", [NP, D])
        t2 = dram("t2", [NP, D + H])
        t3 = dram("t3", [TN * NP, 2 * D])
        t4 = dram("t4", [NP, 3 * D])
        spill = dram("spill", [HALVES, P, 8 * D])
        p_dram = dram("p_dram", [P, NT * D])
        dp_dram = dram("dp_dram", [P, NT * D])

        landed = [ctx.enter_context(nc.semaphore("landed0")), ctx.enter_context(nc.semaphore("landed1"))]
        gather_pass = [0]
        carry = sb("carry", 3 * P)

        e_in = {}
        o = 0
        for n in ("src", "dst", "typ", "wgt"):
            e_in[n] = arena[0:EC, o:o + UC]
            o += UC
        ld_i = arena[:, o:o + 3 * 7 * EC].bitcast(I32).rearrange("p (a j e) -> p a j e", a=3, j=7)
        o += 3 * 7 * EC
        ld_f = arena[:, o:o + 4 * 7 * EC].rearrange("p (a j e) -> p a j e", a=4, j=7)
        l3_raw = arena[:, o + 4 * 7 * EC:o + 4 * 7 * EC + 6 * D]
        SORT0 = 4 * UC
        loads = sem("loads")
        iotas = sem("iotas")
        zeroed = sem("zeroed")
        v_set = sem("v_set")
        edge_T = sem("edge_T")
        edge_f = sem("edge_f")
        l3_up = sem("l3_up")
        n_loads = [0]
        with nc.Block() as block:
            @block.sync
            def _(sp):
                def load(dst, src):
                    n_loads[0] += 16
                    sp.dma_start(dst, src).then_inc(loads, 16)

                sp.wait_ge(zeroed, 1)
                full = UC // P
                for a, name in enumerate(("src", "dst", "edge_type_8", "edge_weight")):
                    dst = ld_i[:, a] if a < 3 else ld_f[:, 3]
                    load(dst[:, 0:full, :], t[name][0:full * P * EC].rearrange("(j p e) -> p j e", p=P, e=EC))
                    load(dst[0:UC - full * P, full, :], t[name][full * P * EC:E].rearrange("(p e) -> p e", e=EC))
                for i, name in enumerate(("L3_gnn_U_w", "L3_gnn_W_w")):
                    load(l3_raw[:, i * D:(i + 1) * D], t[name])
                load(l3_raw[:, 2 * D:3 * D], t["L3_gnn_V_w"][:, 0:D])
                load(l3_raw[:, 3 * D:4 * D], t["L3_gnn_D_w"])
                load(l3_raw[:, 4 * D:5 * D], t["L3_gnn_V_w"][:, D:2 * D])
                load(l3_raw[:, 5 * D:6 * D], t["L3_gnn_E_w"])
                for n in w_names:
                    load(w[n], t[n])
                load(w_uv[:, 0:H], t["L1_gnn_W_u"])
                load(w_uv[:, H:2 * H], t["L1_gnn_W_v"])
                for n in bias_names:
                    if n != "none":
                        load(bias[n], t[n].partition_broadcast(P))
                load(b_u[:, :], t["L1_gnn_b_u"].partition_broadcast(P))
                for n in col_names:
                    load(col[n], t[n].rearrange("(p o) -> p o", o=1))
                xt = x_cur[:, :].rearrange("p (t f) -> p t f", f=D)
                load(xt[:, 0:NT - 1, :], t["x"][0:(NT - 1) * P, :].rearrange("(t p) f -> p t f", p=P))
                load(xt[0:LAST, NT - 1, :], t["x"][(NT - 1) * P:N, :])
                sp.wait_ge(loads, n_loads[0])

            @block.gpsimd
            def _(pool):
                nc.gpsimd.iota(int_tmp[:, :], [[1, P]], base=0, channel_multiplier=0).then_inc(iotas, 1)
                nc.gpsimd.iota(int_tmp2[:, :], [[1, 1]], base=0, channel_multiplier=1).then_inc(iotas, 1)

            n_all = 16 * (8 + 6 + len(w_names) + 2 + len(bias_names) - 1 + 1 + len(col_names) + 2)

            @block.vector
            def _(dve):
                step = Chain(dve, v_set)
                nc.vector.memset(x_cur[:, (NT - 1) * D:NT * D], 0.0)
                nc.vector.memset(ld_i[:, :, 6, :], 0)
                nc.vector.memset(ld_f[:, 3, 6, :], 0.0).then_inc(zeroed, 1)
                nc.vector.memset(ones[:, :], 1.0)
                nc.vector.memset(bias["none"], 0.0)
                nc.vector.memset(neg_half[:, :], -0.5)
                nc.vector.memset(d_src[:, :], 0)
                nc.vector.memset(d_typed[:, :], 0)
                nc.vector.memset(d_lw[:, :], 0.0)
                step(nc.vector.memset(s_dst[:, :], 0))
                dve.wait_ge(iotas, 2)
                step(nc.vector.tensor_copy(iota_row[:, :], int_tmp[:, :]))
                step(nc.vector.tensor_copy(iota_part[:, :], int_tmp2[:, :]))
                for m, op in ((ident, ALU.is_equal), (earlier, ALU.is_lt), (before, ALU.is_gt)):
                    step(nc.vector.tensor_scalar(m[:, :], iota_row[:, :], iota_part[:, 0:1], None, op))
                dve.wait_ge(loads, n_all)
                nc.vector.tensor_copy(ld_f[:, 0:3], ld_i).then_inc(edge_f, 1)
                for a, n in enumerate(("src", "dst", "typ", "wgt")):
                    dve.wait_ge(edge_T, a + 1)
                    b = 2 * (a % 2)
                    step(nc.vector.tensor_copy(e_in[n], ps[0:EC, b * 512:b * 512 + UC]))
                step(nc.vector.scalar_tensor_tensor(e_in["typ"], e_in["typ"], float(NP), e_in["src"], ALU.mult, ALU.add))
                dve.wait_ge(l3_up, 1)
                step(nc.vector.tensor_copy(l3_T[:, :], ps[:, 2048:2048 + 6 * D]))

            @block.tensor
            def _(pe):
                pe.wait_ge(edge_f, 1)
                for a in range(4):
                    if a >= 2:
                        pe.wait_ge(v_set, 6 + a - 1)
                    for j in range(7):
                        b = 2 * (a % 2) * 512 + j * P
                        k = min(P, UC - j * P)
                        last = nc.tensor.transpose(ps[0:EC, b:b + k], ld_f[0:k, a, j, :], ident[0:k, 0:k])
                    last.then_inc(edge_T, 1)
                for i in range(6):
                    last = nc.tensor.transpose(ps[:, 2048 + i * D:2048 + (i + 1) * D], l3_raw[:, i * D:(i + 1) * D], ident[:, :])
                last.then_inc(l3_up, 1)

        sort_top = SORT0

        def part(n, dt=F32):
            nonlocal sort_top
            sort_top += n
            assert sort_top <= AW, sort_top
            ap = arena[:, sort_top - n:sort_top]
            return ap if dt == F32 else ap.bitcast(dt)

        class Side:

            def __init__(self, name, key, fields, key_dram, rec, loT, tile_row):
                self.name, self.key, self.key_dram, self.fields = name, key, key_dram, fields
                self.rec, self.loT, self.tile_row, self.R = rec, loT, tile_row, len(fields)
                self.lo = part(UC)[0:EC]
                self.hi = part(UC)[0:EC]
                self.recs = part(UC * self.R)[0:EC].rearrange("p (c r) -> p c r", r=self.R)
                self.start = part(NT)
                self.tile_rep = part(SC)

        by_src = Side("s", e_in["src"], [e_in["dst"], e_in["src"]], t["src"], s_rec, s_loT, s_tile)
        by_dst = Side("d", e_in["dst"], [e_in["src"], e_in["dst"], e_in["typ"], e_in["wgt"]], t["dst"], d_rec, d_loT, d_tile)
        SORT1 = sort_top

        new_stage()
        HW = 4 * NT
        s_lo_hot = part(8 * P, BF16)[0:EC].rearrange("p (b i l) -> p b i l", b=2, i=8)
        s_hi_hot = part(8 * NT, BF16)[0:EC].rearrange("p (b i l) -> p b i l", b=2, i=8)
        s_hi_diff = part(16 * NT)[0:EC].rearrange("p (b i l) -> p b i l", b=2, i=8)
        d_lo_hot = part(8 * P, BF16)[0:EC].rearrange("p (b i l) -> p b i l", b=2, i=8)
        d_hi_hot = part(8 * HW, BF16)[0:EC].rearrange("p (b i l) -> p b i l", b=2, i=8)
        w_part = part(3 * UC // 2, BF16)[0:EC].rearrange("p (a c) -> p a c", a=3)
        w_rest = part(UC)[0:EC]
        zeros = part(HW)[0:EC]
        hi_int = [part(UC)[0:EC].bitcast(I32) for _ in range(2)]
        fill = [part(JC * 16 * side.R) for side in (by_src, by_dst)]
        counts, n_chunks, tmp, first_chunk = (part(NT) for _ in range(4))
        chunks_int = part(NT).bitcast(I32)
        first_col = part(1)
        tile_ge = part(SC)
        iota_c = part(SC)
        iota_ci = part(SC).bitcast(I32)
        split, filled, fill_set, iota_done = (sem("h_" + n) for n in ("split", "filled", "fill_set", "iota_done"))
        d_tiles, weighed, nodes, diff, dist, hot_a, free, hist_done = (sem("h_" + n) for n in (
            "d_tiles", "weighed", "nodes", "diff", "dist", "hot_a", "free", "done"))
        base_v, base_p, root_in, root_out = (sem("h_" + n) for n in ("base_v", "base_p", "root_in", "root_out"))
        s_counts, d_counts = bank(0, NT), bank(1, HW)
        with nc.Block() as block:
            @block.gpsimd
            def _(pool):
                nc.gpsimd.iota(iota_ci, [[1, SC]], base=0, channel_multiplier=0).then_inc(iota_done, 1)
                pool.wait_ge(split, 12)

                def body(k):
                    for b in range(2):
                        n = 2 * k + b
                        need(pool, free, n - 1)
                        need(pool, hot_a, n - 1)
                        nc.gpsimd.tensor_tensor(s_hi_diff[:, b], bcast_mid(iota_row[0:EC, 0:NT], 8),
                                                bcast_last(by_src.hi[:, bass.ds(8 * n, 8)], NT), ALU.subtract).then_inc(diff, 1)
                        pool.wait_ge(d_tiles, n + 1)
                        for a in range(3):
                            nc.gpsimd.tensor_tensor(d_hi_hot[:, b, :, (a + 1) * NT:(a + 2) * NT], d_hi_hot[:, b, :, 0:NT],
                                                    bcast_last(w_part[:, a, bass.ds(8 * n, 8)], NT), ALU.mult).then_inc(weighed, 1)
                turns(pool, UG // 2, body)
                for i in range(2):
                    pool.wait_ge(root_in, i + 1)
                    nc.gpsimd.tensor_tensor(small[:, 128:128 + NT], small[:, 0:NT], neg_half[:, 0:NT], ALU.pow).then_inc(root_out, 1)

            @block.sync
            def _(sp):
                sp.wait_ge(fill_set, 2)
                for side, f in ((by_src, fill[0]), (by_dst, fill[1])):
                    sp.dma_start(side.rec.rearrange("(p c) r -> p (c r)", p=P), f).then_inc(filled, 16)
                sp.wait_ge(filled, 32)

            @block.scalar
            def _(act):
                for side in (by_src, by_dst):
                    for f, a in enumerate(side.fields):
                        nc.scalar.activation(side.recs[:, :, f], a, ACT.Copy)

                def body(k):
                    for b in range(2):
                        n = 2 * k + b
                        act.wait_ge(diff, n + 1)
                        nc.scalar.activation(s_hi_diff[:, b], s_hi_diff[:, b], ACT.Abs).then_inc(dist, 1)
                        need(act, free, n - 1)
                        act.wait_ge(dist, n + 1)
                        nc.scalar.activation(s_hi_hot[:, b], s_hi_diff[:, b], ACT.Relu, bias=ones[0:EC, 0:1], scale=-1.0).then_inc(hot_a, 1)
                turns(act, UG // 2, body)

            @block.vector
            def _(dve):
                step = Chain(dve, split)
                step(nc.vector.memset(zeros, 0.0))
                for side, h in ((by_src, hi_int[0]), (by_dst, hi_int[1])):
                    step(nc.vector.tensor_scalar(h, side.key, -HALF, 1.0 / P, ALU.add, ALU.mult))
                    step(nc.vector.tensor_copy(side.hi, h))
                    step(nc.vector.scalar_tensor_tensor(side.lo, side.hi, -float(P), side.key, ALU.mult, ALU.add))
                step(nc.vector.tensor_copy(w_part[:, 0], e_in["wgt"]))
                for a in range(2):
                    step(nc.vector.tensor_tensor(w_rest, w_rest if a else e_in["wgt"], w_part[:, a], ALU.subtract))
                    step(nc.vector.tensor_copy(w_part[:, a + 1], w_rest))

                def body(k):
                    for b in range(2):
                        n = 2 * k + b
                        need(dve, free, n - 1)
                        nc.vector.tensor_tensor(d_hi_hot[:, b, :, 0:NT], bcast_mid(iota_row[0:EC, 0:NT], 8),
                                                bcast_last(by_dst.hi[:, bass.ds(8 * n, 8)], NT), ALU.is_equal).then_inc(d_tiles, 1)
                        nc.vector.tensor_tensor(s_lo_hot[:, b], bcast_mid(iota_row[0:EC, :], 8),
                                                bcast_last(by_src.lo[:, bass.ds(8 * n, 8)], P), ALU.is_equal).then_inc(nodes, 1)
                        nc.vector.tensor_tensor(d_lo_hot[:, b], bcast_mid(iota_row[0:EC, :], 8),
                                                bcast_last(by_dst.lo[:, bass.ds(8 * n, 8)], P), ALU.is_equal).then_inc(nodes, 1)
                turns(dve, UG // 2, body)
                for f in fill:
                    step(nc.vector.memset(f, 0.0))
                for side, f in ((by_src, fill[0]), (by_dst, fill[1])):
                    nc.vector.memset(f.rearrange("p (c r) -> p c r", r=side.R)[:, :, 1], PAD_KEY).then_inc(fill_set, 1)
                dve.wait_ge(iota_done, 1)
                step(nc.vector.tensor_copy(iota_c, iota_ci))
                dve.wait_ge(hist_done, 1)
                step = Chain(dve, base_v)
                deg, linked = small[:, 0:NT], small[:, 64:64 + NT]
                for i, (side, ps_counts) in enumerate(((by_src, s_counts), (by_dst, d_counts[:, 0:NT]))):
                    step(nc.vector.tensor_copy(counts, ps_counts))
                    dve.wait_ge(base_p, 3 * i + 1)
                    step(nc.vector.tensor_scalar(chunks_int, bank(2, NT), P - 1 - HALF, 1.0 / P, ALU.add, ALU.mult))
                    step(nc.vector.tensor_copy(n_chunks, chunks_int))
                    step(nc.vector.memset(tmp, 0.0))
                    step(nc.vector.tensor_tensor_scan(first_chunk, n_chunks, tmp, 0.0, ALU.add, ALU.add))
                    step(nc.vector.tensor_tensor(first_chunk, first_chunk, n_chunks, ALU.subtract))
                    step(nc.vector.scalar_tensor_tensor(side.start, first_chunk, float(P), bank(3, NT), ALU.mult, ALU.add))
                    dve.wait_ge(base_p, 3 * i + 2)
                    step(nc.vector.tensor_copy(first_col[0:NT], bank(4, 1, NT)))
                    step(nc.vector.tensor_scalar(tile_ge[0:NT], iota_c[0:NT], first_col[0:NT, 0:1], None, ALU.is_ge))
                    dve.wait_ge(base_p, 3 * i + 3)
                    step(nc.vector.tensor_scalar(side.tile_rep, ps[:, 2560:2560 + SC], -1.0, None, ALU.add))
                    step(nc.vector.tensor_copy(side.tile_row[0:1, :], side.tile_rep[0:1, :]))
                    assert step.n == 11 * (i + 1)
                step(nc.vector.tensor_scalar(deg, s_counts, 1.0, None, ALU.add))
                dve.sem_inc(root_in, 1)
                dve.wait_ge(root_out, 1)
                step(nc.vector.tensor_copy(inv[:, :], small[:, 128:128 + NT]))
                step(nc.vector.tensor_scalar(deg, d_counts[:, NT:2 * NT], 1.0, None, ALU.add))
                for a in range(2, 4):
                    step(nc.vector.tensor_tensor(deg, deg, d_counts[:, a * NT:(a + 1) * NT], ALU.add))
                step(nc.vector.tensor_scalar(linked, deg, 0.0, None, ALU.is_gt))
                step(nc.vector.tensor_tensor(deg, deg, linked, ALU.mult))
                step(nc.vector.scalar_tensor_tensor(deg, deg, 1.0, linked, ALU.add, ALU.subtract))
                dve.sem_inc(root_in, 1)
                dve.wait_ge(root_out, 2)
                step(nc.vector.tensor_tensor(dinv[:, :], small[:, 128:128 + NT], linked, ALU.mult))

            @block.tensor
            def _(pe):
                pe.wait_ge(split, 1)
                nc.tensor.matmul(s_counts, zeros[:, 0:P], zeros[:, 0:NT], start=True, stop=False, skip_group_check=True)
                nc.tensor.matmul(d_counts, zeros[:, 0:P], zeros[:, 0:HW], start=True, stop=False, skip_group_check=True)

                def body(k):
                    for b in range(2):
                        n = 2 * k + b
                        pe.wait_ge(weighed, 3 * n + 3)
                        pe.wait_ge(hot_a, n + 1)
                        pe.wait_ge(nodes, 2 * n + 2)
                        for i in range(8):
                            nc.tensor.matmul(s_counts, s_lo_hot[:, b, i], s_hi_hot[:, b, i], start=False, stop=False, skip_group_check=True)
                            last = nc.tensor.matmul(d_counts, d_lo_hot[:, b, i], d_hi_hot[:, b, i], start=False, stop=False, skip_group_check=True)
                        last.then_inc(free, 1)
                turns(pe, UG // 2, body)
                nc.tensor.matmul(s_counts, zeros[:, 0:P], zeros[:, 0:NT], start=False, stop=True, skip_group_check=True)
                nc.tensor.matmul(d_counts, zeros[:, 0:P], zeros[:, 0:HW], start=False, stop=True, skip_group_check=True).then_inc(hist_done, 1)
                for i in range(2):
                    pe.wait_ge(base_v, 11 * i + 1)
                    nc.tensor.matmul(bank(2, NT), ones[:, :], counts, start=True, stop=True)
                    nc.tensor.matmul(bank(3, NT), before[:, :], counts, start=True, stop=True).then_inc(base_p, 1)
                    pe.wait_ge(base_v, 11 * i + 6)
                    nc.tensor.matmul(bank(4, 1, NT), first_chunk[0:1, :], ones[0:1, 0:1], start=True, stop=True).then_inc(base_p, 1)
                    pe.wait_ge(base_v, 11 * i + 9)
                    for j in range(2):
                        last = nc.tensor.matmul(ps[:, 2560 + j * 512:2560 + min(SC, (j + 1) * 512)], ones[0:NT, :],
                                                tile_ge[0:NT, j * 512:min(SC, (j + 1) * 512)], start=True, stop=True)
                    last.then_inc(base_p, 1)

        def place_edges(side):
            nonlocal sort_top
            new_stage()
            sort_top = SORT1
            R, key, lo, hi, rec, recs = side.R, side.key, side.lo, side.hi, side.rec, side.recs
            at_lo = part(8 * P, BF16)[0:EC].rearrange("p (b i l) -> p b i l", b=2, i=8)
            at_hi = part(8 * NT, BF16)[0:EC].rearrange("p (b i l) -> p b i l", b=2, i=8)
            at_run = part(2 * 8 * NT).rearrange("p (b i l) -> p b i l", b=2, i=8)
            keys_all = part(2 * 8 * EC).bitcast(I32).rearrange("p (b c) -> p b c", b=2)
            at_loT = part(2 * 8 * EC).rearrange("p (b c) -> p b c", b=2)
            lo_all = part(2 * 8 * EC).bitcast(I32).rearrange("p (b c) -> p b c", b=2)
            same = part(8 * EC)[0:EC].rearrange("p (i e) -> p i e", i=8)
            rank, val, key_st = (part(16)[0:EC] for _ in range(3))
            q, row = (part(16)[0:EC].bitcast(I32) for _ in range(2))
            picks = part(8 * NT)[0:EC].rearrange("p (i l) -> p i l", i=8)
            recs_st = part(16 * R)[0:EC].rearrange("p (c r) -> p c r", r=R)
            minus_part = part(1)
            srt = part(SC * R).rearrange("p (c r) -> p c r", r=R)
            lo_s = part(SC)
            lo_T = part(7 * P)
            pre = side.name + "_"
            keys_in = [sem(pre + "keys_in0"), sem(pre + "keys_in1")]
            placed = [sem(pre + "placed0"), sem(pre + "placed1")]
            begun, hot_c, masked, dist, hot_T, counted, run_set, found, v_grp, ranked, picked = (sem(pre + n) for n in (
                "begun", "hot_c", "masked", "dist", "hot_T", "counted", "run_set", "found", "v_grp", "ranked", "picked"))
            key_rows = side.key_dram.rearrange("(g c) -> g c", c=8 * EC)
            TURNS = UG // 2
            GH = 8 * NT
            PICK = 7

            def count_bank(b):
                return ps[:, b * 512:b * 512 + GH]

            def pick_bank(b):
                return ps[0:EC, (2 + b) * 512:(2 + b) * 512 + GH]
            with nc.Block() as block:
                @block.sync
                def _(sp):
                    def body(k):
                        for b in range(2):
                            n = 2 * k + b
                            need(sp, ranked, n - 1)
                            sp.dma_start(keys_all[:, b, :], key_rows[bass.ds(n, 1), :].to_broadcast([P, 8 * EC])).then_inc(keys_in[b], 16)
                    turns(sp, TURNS, body)

                @block.scalar
                def _(act):
                    act.wait_ge(begun, 2)

                    def body(k):
                        for b in range(2):
                            n = 2 * k + b
                            need(act, found, n - 1)
                            act.wait_ge(masked, n + 1)
                            nc.scalar.activation(at_loT[:, b], lo_all[:, b], ACT.Abs, bias=minus_part).then_inc(dist, 1)
                            act.wait_ge(dist, n + 1)
                            nc.scalar.activation(at_loT[:, b], at_loT[:, b], ACT.Relu, bias=ones[:, 0:1], scale=-1.0).then_inc(hot_T, 1)
                    turns(act, TURNS, body)

                @block.vector
                def _(dve):
                    nc.vector.tensor_copy(at_run[:, 1, 7], side.start).then_inc(begun, 1)
                    nc.vector.tensor_scalar(minus_part, iota_part[:, 0:1], -1.0, None, ALU.mult).then_inc(begun, 1)
                    dve.wait_ge(begun, 2)

                    def run_on(n, b):
                        dve.wait_ge(counted, n + 1)
                        need(dve, run_set, n)
                        nc.vector.tensor_tensor(at_run[:, b], count_bank(b).rearrange("p (i l) -> p i l", i=8),
                                                bcast_mid(at_run[:, 1 - b, 7], 8), ALU.add).then_inc(run_set, 1)

                    def one_hots(k, b):
                        n = 2 * k + b
                        nc.vector.tensor_tensor(at_lo[:, b], bcast_mid(iota_row[0:EC, :], 8),
                                                bcast_last(lo[:, bass.ds(8 * n, 8)], P), ALU.is_equal)
                        nc.vector.tensor_tensor(at_hi[:, b], bcast_mid(iota_row[0:EC, 0:NT], 8),
                                                bcast_last(hi[:, bass.ds(8 * n, 8)], NT), ALU.is_equal).then_inc(hot_c, 1)
                        nc.vector.tensor_copy(key_st[:, 8 * b:8 * b + 8], key[:, bass.ds(8 * n, 8)]).then_inc(v_grp, 1)
                        need(dve, hot_T, n - 1)
                        dve.wait_ge(keys_in[b], 16 * k + 16)
                        nc.vector.tensor_scalar(lo_all[:, b], keys_all[:, b, :], P - 1, None, ALU.bitwise_and).then_inc(masked, 1)

                    def ranks(k, b):
                        n = 2 * k + b
                        need(dve, ranked, n)
                        dve.wait_ge(v_grp, n + 1)
                        for i in range(8):
                            last = nc.vector.scalar_tensor_tensor(same[:, i], keys_all[0:EC, b, i * EC:(i + 1) * EC], key_st[:, 8 * b + i:8 * b + i + 1],
                                                                  earlier[0:EC, 0:EC], ALU.is_equal, ALU.mult,
                                                                  accum_out=rank[:, 8 * b + i:8 * b + i + 1])
                        last.then_inc(ranked, 1)

                    def places(k, b, n, scatters):
                        sl = slice(8 * b, 8 * b + 8)
                        step = Chain(dve, picked, PICK * n)
                        dve.wait_ge(found, n + 1)
                        step(nc.vector.tensor_tensor(picks, pick_bank(b).rearrange("p (i l) -> p i l", i=8), at_hi[:, b], ALU.mult))
                        step(nc.vector.tensor_reduce(val[:, sl], picks, AX.X, ALU.add))
                        step(nc.vector.tensor_tensor(val[:, sl], val[:, sl], rank[:, sl], ALU.add))
                        need(dve, placed[b], scatters)
                        settle(nc.vector)
                        step(nc.vector.tensor_copy(recs_st[:, sl, :], recs[:, bass.ds(8 * n, 8), :]))
                        step(nc.vector.tensor_scalar(q[:, sl], val[:, sl], -HALF, 1.0 / P, ALU.add, ALU.mult))
                        step(nc.vector.scalar_tensor_tensor(rank[:, sl], q[:, sl], -float(P), val[:, sl], ALU.mult, ALU.add))
                        step(nc.vector.scalar_tensor_tensor(row[:, sl], rank[:, sl], float(SC), q[:, sl], ALU.mult, ALU.add))
                        assert step.n == PICK

                    def body(k):
                        for b in range(2):
                            first = isinstance(k, int) and b == 0
                            n = 2 * k + b
                            if not first:
                                run_on(n - 1, 1 - b)
                            one_hots(k, b)
                            ranks(k, b)
                            if not first:
                                places(k, 1 - b, n - 1, 128 * (k - 1 + b))
                    turns(dve, TURNS, body)
                    run_on(UG - 1, 1)
                    dve.wait_ge(ranked, UG)
                    places(TURNS - 1, 1, UG - 1, 128 * (TURNS - 1))

                @block.tensor
                def _(pe):
                    def look_up(n, b):
                        pe.wait_ge(hot_T, n + 1)
                        need(pe, picked, PICK * n - PICK)
                        pe.wait_ge(run_set, n + 1)
                        for i in range(8):
                            run = at_run[:, b, i - 1] if i else at_run[:, 1 - b, 7]
                            last = nc.tensor.matmul(pick_bank(b)[:, i * NT:(i + 1) * NT], at_loT[:, b, i * EC:(i + 1) * EC], run, start=True, stop=True)
                        last.then_inc(found, 1)

                    def body(k):
                        for b in range(2):
                            first = isinstance(k, int) and b == 0
                            n = 2 * k + b
                            if not first:
                                look_up(n - 1, 1 - b)
                            pe.wait_ge(hot_c, n + 1)
                            need(pe, run_set, n - 1)
                            for i in range(8):
                                last = nc.tensor.matmul(count_bank(b)[:, i * NT:GH], at_lo[:, b, i], bcast_mid(at_hi[:, b, i], 8 - i),
                                                        start=i == 0, stop=i == 7, skip_group_check=True)
                            last.then_inc(counted, 1)
                    turns(pe, TURNS, body)
                    look_up(UG - 1, 1)

                @block.gpsimd
                def _(pool):
                    with pool.Fori(0, TURNS) as k:
                        for b in range(2):
                            pool.wait_ge(picked, 2 * PICK * k + PICK * (b + 1))
                            settle(pool)
                            for i in range(8):
                                pool.indirect_dma_start(out=rec[:, :], out_offset=bass.IndirectOffsetOnAxis(ap=row[:, 8 * b + i:8 * b + i + 1], axis=0),
                                                        in_=recs_st[:, 8 * b + i, :], in_offset=None).then_inc(placed[b], 16)
                    for b in range(2):
                        pool.wait_ge(placed[b], 128 * TURNS)

            back, v_back, lo_up, lo_out = (sem(pre + n) for n in ("back", "v_back", "lo_up", "lo_out"))
            with nc.Block() as block:
                @block.sync
                def _(sp):
                    sp.dma_start(srt, rec.rearrange("(p c) r -> p c r", p=P)).then_inc(back, 16)
                    sp.wait_ge(lo_up, 2)
                    lt = lo_T.rearrange("p (j e) -> p j e", j=7)
                    sp.dma_start(side.loT[0:6 * P, :].rearrange("(j p) e -> p j e", p=P), lt[:, 0:6, :]).then_inc(lo_out, 16)
                    sp.dma_start(side.loT[6 * P:SC, :], lt[0:SC - 6 * P, 6, :]).then_inc(lo_out, 16)
                    sp.wait_ge(lo_out, 32)

                @block.vector
                def _(dve):
                    step = Chain(dve, v_back)
                    dve.wait_ge(back, 16)
                    step(nc.vector.scalar_tensor_tensor(lo_s, side.tile_rep, -float(P), srt[:, :, 1], ALU.mult, ALU.add))
                    if side is by_dst:
                        lw = d_lw[:, :].rearrange("p (c r) -> p c r", r=2)
                        nc.vector.tensor_copy(d_src[:, 0:SC], srt[:, :, 0])
                        nc.vector.tensor_copy(d_typed[:, 0:SC], srt[:, :, 2])
                        nc.vector.tensor_copy(lw[:, 0:SC, 1], srt[:, :, 3])
                        step(nc.vector.tensor_copy(lw[:, 0:SC, 0], lo_s))
                    else:
                        nc.vector.tensor_copy(s_dst[:, 0:SC], srt[:, :, 0])
                        step(nc.vector.tensor_copy(s_lo[:, 0:SC], lo_s))
                    dve.wait_ge(lo_up, 1)
                    nc.vector.tensor_copy(lo_T, ps[:, 0:7 * P]).then_inc(lo_up, 1)

                @block.tensor
                def _(pe):
                    pe.wait_ge(v_back, 1)
                    nc.tensor.matmul(ps[:, 6 * P:7 * P], ident[:, :], ident[:, :], start=True, stop=True)
                    for j in range(7):
                        k = min(P, SC - j * P)
                        last = nc.tensor.transpose(ps[0:k, j * P:(j + 1) * P], lo_s[:, j * P:j * P + k], ident[:, :])
                    last.then_inc(lo_up, 1)
            return srt

        place_edges(by_src)
        srt = place_edges(by_dst)
        keys_sorted = srt[:, :, 1]

        W0 = 0
        AT_E = 6400
        AT_ACC = 13056
        AT_Q = 19720
        AT_BUF = 25992
        w_typed = {n: arena[:, W0 + i * TN * D:W0 + (i + 1) * TN * D].rearrange("p (t o) -> p t o", t=TN)
                   for i, n in enumerate(("a", "k", "q", "v"))}
        rel = {n: arena[:, W0 + (4 + i) * TN * D:W0 + (5 + i) * TN * D] for i, n in enumerate(("att", "msg"))}
        e_all = arena[:, AT_E:AT_E + SC * H]
        ntb = arena[:, AT_E:AT_E + NP].bitcast(I32)
        acc_att = arena[:, AT_ACC:AT_ACC + NT * (D + H)]
        acc_gcn = arena[:, AT_ACC:AT_ACC + NP]
        q_tab = arena[:, AT_Q:AT_Q + NP]
        v_tab = arena[:, AT_Q:AT_Q + NT * H]

        def tiled(ap, width=D):
            return ap.rearrange("p (t f) -> p t f", f=width)

        def stage_index(dve, idx, staged, base, k, b):
            n_before = 128 * (k + b)
            need(dve, landed[1 - b], base + n_before if not isinstance(n_before, int) or n_before else 0)
            settle(nc.vector)
            nc.vector.tensor_copy(stage_idx[:, 8 * (1 - b):8 * (1 - b) + 8], idx[:, bass.ds(16 * k + 8 * b + 8, 8)]).then_inc(staged, 1)

        def stage_first(idx, staged):
            nc.vector.tensor_copy(stage_idx[:, 0:8], idx[:, 0:8]).then_inc(staged, 1)

        def gathers(pool, table, rows, staged, buffer_free):
            def body(k):
                for b in range(2):
                    pool.wait_ge(staged, 2 * k + b + 1)
                    buffer_free(k, b)
                    settle(pool)
                    for i in range(8):
                        pool.indirect_dma_start(out=rows[:, 8 * b + i, :], out_offset=None, in_=table,
                                                in_offset=bass.IndirectOffsetOnAxis(ap=stage_idx[:, 8 * b + i:8 * b + i + 1], axis=0)).then_inc(landed[b], 16)
            turns(pool, ITER, body)

        def next_pass():
            gather_pass[0] += 1
            return (gather_pass[0] - 1) * 128 * ITER

        tile_loads = [0]

        def tile_numbers(eng, tile_row, c):
            tile_loads[0] += 1
            regs = [eng.alloc_register(f"tile{tile_loads[0]}_{i}") for i in range(8)]
            eng.load(regs, tile_row[0:1, bass.ds(c, 8)])
            return [eng.snap(r, donate=True, min_val=0, max_val=NT - 1) for r in regs]

        class Sums:

            def __init__(self, pre, tile_row, accs, width):
                self.added, self.drained = sem(pre + "added"), sem(pre + "drained")
                self.tile_row, self.accs, self.width = tile_row, accs, width

            def start(self, dve):
                self.dve = dve

            def open(self, c, behind=True):
                self.tiles = tile_numbers(self.dve, self.tile_row, c)
                if behind:
                    self.drain(8)
                    self.dve.sem_inc(self.added, -8)

            def add(self, i, product):
                before = i + 1 - len(self.accs)
                if before > 0:
                    self.dve.wait_ge(self.added, before)
                at = self.accs[i % len(self.accs)][:, bass.ds(self.tiles[i] * self.width, self.width)]
                nc.vector.tensor_tensor(at, at, product, ALU.add).then_inc(self.added, 1)

            def drain(self, count):
                self.dve.wait_ge(self.added, count)
                self.dve.sem_inc(self.drained, 1)

        AT_T = AT_ACC
        scan = [arena[:, AT_T + i * (TL + 1):AT_T + (i + 1) * (TL + 1)] for i in range(3)]
        stage_T = arena[:, AT_T + 3 * (TL + 1):AT_T + 3 * (TL + 1) + 1024]
        assert AT_T + 3 * (TL + 1) + 1024 <= AW

        def by_group(ap):
            return ap.rearrange("p (g j) -> p j g", g=GROUPS)

        new_stage()
        f_st = sem("f_st")
        f_ps = sem("f_ps")
        f_out = sem("f_out")
        f_v = sem("f_v")
        f_row = sem("f_row")
        f_dma = sem("f_dma")
        K_T = arena[:, 0:TL]
        pen_f = arena[:, TL:2 * TL + 1]
        f_stage = arena[:, 2 * TL + 8:2 * TL + 8 + 512]
        f_rows = arena[0:1, 2 * TL + 520:2 * TL + 520 + 4 * P]
        pw_row, pb_row, pc_row = (carry[0:1, i * P:(i + 1) * P] for i in range(3))
        keys_keep = arena[:, 2 * TL + 1040:2 * TL + 1040 + SC]
        f_key = sem("f_key")
        with nc.Block() as block:
            @block.vector
            def _(dve):
                nc.vector.tensor_copy(keys_keep, keys_sorted).then_inc(f_key, 1)
        with nc.Block() as block:
            @block.scalar
            def _(act):
                def body(k):
                    need(act, f_ps, k)
                    nc.scalar.activation(f_stage.rearrange("p (j g h) -> p j g h", j=4, g=GROUPS),
                                         bcast_last(by_group(keys_keep)[:, bass.ds(4 * k, 4), :], H), ACT.Copy).then_inc(f_st, 1)
                turns(act, JC // 4, body)

            @block.tensor
            def _(pe):
                def body(k):
                    pe.wait_ge(f_st, k + 1)
                    need(pe, f_out, k)
                    for q in range(4):
                        last = nc.tensor.transpose(ps[:, q * P:(q + 1) * P], f_stage[:, q * P:(q + 1) * P], ident[:, :])
                    last.then_inc(f_ps, 1)
                turns(pe, JC // 4, body)
                pe.wait_ge(f_out, JC // 4)
                nc.tensor.matmul(ps[0:1, 512:512 + P], K_T[:, 0:1], ident[:, :], start=True, stop=True)
                nc.tensor.matmul(ps[0:1, 512 + P:512 + 2 * P], K_T[:, TL - 1:TL], ident[:, :], start=True, stop=True).then_inc(f_row, 1)

            @block.vector
            def _(dve):
                def body(k):
                    dve.wait_ge(f_ps, k + 1)
                    settle(nc.vector)
                    nc.vector.tensor_copy(K_T[:, bass.ds(512 * k, 512)], ps[:, 0:512]).then_inc(f_out, 1)
                turns(dve, JC // 4, body)
                dve.wait_ge(f_out, JC // 4)
                step = Chain(dve, f_v)
                step(nc.vector.memset(pen_f, 0.0))
                step(nc.vector.tensor_tensor(pen_f[:, 1:TL], K_T[:, 1:TL], K_T[:, 0:TL - 1], ALU.not_equal))
                step(nc.vector.tensor_scalar(pen_f[:, 1:TL], pen_f[:, 1:TL], -BIG, None, ALU.mult))
                dve.wait_ge(f_row, 1)
                first, last, cont, whole = (f_rows[:, i * P:(i + 1) * P] for i in range(4))
                step(nc.vector.tensor_copy(f_rows[:, 0:2 * P], ps[0:1, 512:512 + 2 * P]))
                step(nc.vector.memset(cont, 0.0))
                step(nc.vector.tensor_tensor(cont[:, H:P], first[:, H:P], last[:, 0:P - H], ALU.is_equal))
                step(nc.vector.tensor_tensor(whole, first, last, ALU.is_equal))

                def swapped(ap):
                    return ap.rearrange("p (g h) -> p h g", h=H)

                def rows(ap):
                    return ap.rearrange("p (h g) -> p h g", h=H)
                step(nc.vector.tensor_copy(rows(pc_row), swapped(cont)))
                step(nc.vector.tensor_copy(rows(pw_row), swapped(whole)))
                step(nc.vector.memset(pb_row, 0.0))
                step(nc.vector.tensor_tensor(rows(pb_row)[:, :, 0:GROUPS - 1], rows(pw_row)[:, :, 0:GROUPS - 1], rows(pc_row)[:, :, 1:GROUPS], ALU.mult))
                step(nc.vector.tensor_tensor(pw_row, pw_row, pc_row, ALU.mult))
                step(nc.vector.tensor_scalar(carry[0:1, :], carry[0:1, :], -1.0, BIG, ALU.add, ALU.mult))

            @block.sync
            def _(sp):
                sp.wait_ge(f_v, 3)
                sp.dma_start(penT, pen_f).then_inc(f_dma, 16)
                sp.wait_ge(f_dma, 16)

        def in_pairs(eng, count, one):
            one(0, 0)
            one(1, 1)
            with eng.Fori(1, count // 2) as k:
                for b in range(2):
                    one(2 * k + b, b)
            one(count - 1, 0)

        def softmax_weights(which):
            new_stage()
            pre = which + "_sm_"
            s_in, s_st, s_ps, s_out, s_v = (sem(pre + n) for n in ("in", "st", "ps", "out", "v"))
            s_row, s_col, s_d, s_ex, s_exps, s_back = (sem(pre + n) for n in ("row", "col", "d", "ex", "exps", "back"))
            eT = scan[0][:, 0:TL]
            pen = scan[1]
            top = scan[2][:, 0:TL]
            fwd = e_all
            st = [stage_T[:, b * 512:(b + 1) * 512] for b in range(2)]
            c_col = small[:, 300:301]
            rows = small[0:1, 0:2 * P]
            by_head = e_all.rearrange("p (g j h) -> p j g h", g=GROUPS, h=H)
            with nc.Block() as block:
                @block.sync
                def _(sp):
                    sp.dma_start(pen, penT).then_inc(s_in, 16)

                @block.scalar
                def _(act):
                    def lay(n, b):
                        need(act, s_ps, n - 1)
                        nc.scalar.activation(st[b].rearrange("p (j g h) -> p j g h", j=4, g=GROUPS),
                                             by_head[:, bass.ds(4 * n, 4)], ACT.Copy).then_inc(s_st, 1)
                    in_pairs(act, JC // 4, lay)
                    act.wait_ge(s_d, 1)
                    act.wait_ge(s_ps, JC // 4)

                    def exps(n, b):
                        need(act, s_exps, n - 1)
                        nc.scalar.activation(st[b], eT[:, bass.ds(512 * n, 512)], ACT.Exp).then_inc(s_ex, 1)
                    in_pairs(act, JC // 4, exps)

                @block.tensor
                def _(pe):
                    def lay(n, b):
                        pe.wait_ge(s_st, n + 1)
                        need(pe, s_out, n - 1)
                        for q in range(4):
                            last = nc.tensor.transpose(ps[:, b * 512 + q * P:b * 512 + (q + 1) * P], st[b][:, q * P:(q + 1) * P], ident[:, :])
                        last.then_inc(s_ps, 1)
                    in_pairs(pe, JC // 4, lay)
                    pe.wait_ge(s_out, JC // 4)
                    for d in range(2):
                        pe.wait_ge(s_v, 1 + 5 * d)
                        edge = fwd[:, TL - 1:TL] if d == 0 else top[:, 0:1]
                        nc.tensor.matmul(ps[0:1, 512:512 + P], edge, ident[:, :], start=True, stop=True).then_inc(s_row, 1)
                        pe.wait_ge(s_v, 4 + 5 * d)
                        nc.tensor.matmul(ps[:, 1024:1025], rows[:, P:2 * P], ones[0:1, 0:1], start=True, stop=True).then_inc(s_col, 1)

                    def back(n, b):
                        pe.wait_ge(s_ex, n + 1)
                        need(pe, s_back, n - 1)
                        for q in range(4):
                            last = nc.tensor.transpose(ps[:, 1536 + b * 512 + q * P:1536 + b * 512 + (q + 1) * P], st[b][:, q * P:(q + 1) * P], ident[:, :])
                        last.then_inc(s_exps, 1)
                    in_pairs(pe, JC // 4, back)

                @block.vector
                def _(dve):
                    def lay(n, b):
                        dve.wait_ge(s_ps, n + 1)
                        settle(nc.vector)
                        nc.vector.tensor_copy(eT[:, bass.ds(512 * n, 512)], ps[:, b * 512:(b + 1) * 512]).then_inc(s_out, 1)
                    in_pairs(dve, JC // 4, lay)
                    dve.wait_ge(s_out, JC // 4)
                    dve.wait_ge(s_in, 16)
                    step = Chain(dve, s_v)

                    def hg(ap):
                        return ap.rearrange("p (h g) -> p h g", h=H)

                    def gh(ap):
                        return ap.rearrange("p (g h) -> p h g", h=H)
                    for d in range(2):
                        if d == 0:
                            data0, data1, res = pen[:, 0:TL], eT, fwd
                            f_row_ps, pen_row, shut = gh(ps[0:1, 512:512 + P]), pw_row, slice(0, 1)
                        else:
                            data0, data1, res = pen[:, 1:TL + 1][:, ::-1], fwd[:, ::-1], top[:, ::-1]
                            f_row_ps, pen_row, shut = gh(ps[0:1, 512:512 + P]), pb_row, slice(GROUPS - 1, GROUPS)
                        step(nc.vector.tensor_tensor_scan(res, data0, data1, -BIG, ALU.add, ALU.max))
                        dve.wait_ge(s_row, d + 1)
                        run = rows[:, 0:P]
                        step(nc.vector.tensor_copy(hg(run), f_row_ps))
                        if d == 0:
                            step(nc.vector.tensor_tensor_scan(run, pen_row, run, -BIG, ALU.add, ALU.max))
                        else:
                            step(nc.vector.tensor_tensor_scan(run[:, ::-1], pen_row[:, ::-1], run[:, ::-1], -BIG, ALU.add, ALU.max))
                        into = gh(rows[:, P:2 * P])
                        nc.vector.memset(into[:, :, shut], -BIG)
                        if d == 0:
                            step(nc.vector.tensor_tensor(into[:, :, 1:GROUPS], hg(run)[:, :, 0:GROUPS - 1], hg(pc_row)[:, :, 1:GROUPS], ALU.add))
                        else:
                            step(nc.vector.tensor_tensor(into[:, :, 0:GROUPS - 1], hg(run)[:, :, 1:GROUPS], hg(pc_row)[:, :, 1:GROUPS], ALU.add))
                        dve.wait_ge(s_col, d + 1)
                        nc.vector.tensor_copy(c_col, ps[:, 1024:1025]).then_inc(s_out, 1)
                        dve.wait_ge(s_out, JC // 4 + d + 1)
                        step(nc.vector.tensor_tensor_scan(res, data0, data1, c_col, ALU.add, ALU.max))
                    nc.vector.tensor_tensor(eT, eT, top, ALU.subtract).then_inc(s_d, 1)

                    def back(n, b):
                        dve.wait_ge(s_exps, n + 1)
                        settle(nc.vector)
                        nc.vector.tensor_copy(by_head[:, bass.ds(4 * n, 4)],
                                              ps[:, 1536 + b * 512:2048 + b * 512].rearrange("p (j g h) -> p j g h", j=4, g=GROUPS)).then_inc(s_back, 1)
                    in_pairs(dve, JC // 4, back)

        class Norm:

            def __init__(self, pre, per):
                self.arg, self.root, self.per = sem(pre + "ln_arg"), sem(pre + "ln_root"), per

            def vector(self, step, r, sq, res, k, j):
                m, v, inv_std = small[:, 0:GT], small[:, 16:16 + GT], small[:, 32:32 + GT]
                step(nc.vector.tensor_reduce(m, r, AX.X, ALU.add))
                step(nc.vector.tensor_scalar(m, m, -1.0 / D, None, ALU.mult))
                step(nc.vector.tensor_tensor(r, r, bcast_last(m, D), ALU.add))
                step(nc.vector.tensor_tensor(sq, r, r, ALU.mult))
                step(nc.vector.tensor_reduce(v, sq, AX.X, ALU.add))
                step(nc.vector.tensor_scalar(v, v, 1.0 / D, EPS, ALU.mult, ALU.add))
                step.eng.sem_inc(self.arg, 1)
                step.eng.wait_ge(self.root, self.per * k + j + 1)
                step(nc.vector.tensor_tensor(res, r, bcast_last(inv_std, D), ALU.mult))

            def gpsimd(self, pool):
                def body(k):
                    for j in range(self.per):
                        pool.wait_ge(self.arg, self.per * k + j + 1)
                        nc.gpsimd.tensor_tensor(small[:, 32:32 + GT], small[:, 16:16 + GT], neg_half[:, 0:GT], ALU.pow).then_inc(self.root, 1)
                turns(pool, NG, body)

        def ahead(eng, first, turn):
            first(0)
            turn(0, True)
            with eng.Fori(1, NG - 1) as k:
                turn(k, True)
            turn(NG - 1, False)

        def cols(ap, k, width=D):
            return ap[:, bass.ds(GT * width * k, GT * width)].rearrange("p (t f) -> p t f", f=width)

        def transposes(src, b):
            for i in range(GT):
                last = nc.tensor.transpose(ps[:, b * 512 + i * P:b * 512 + (i + 1) * P], src[:, i * D:(i + 1) * D], ident[:, :])
            return last

        def products(xT, weight, b, start=True, stop=True):
            for i in range(GT):
                last = nc.tensor.matmul(ps[:, b * 512 + i * D:b * 512 + (i + 1) * D], xT[:, i * P:(i + 1) * P], weight,
                                        start=start and i % 4 == 0, stop=stop, skip_group_check=True)
            return last

        def products_T(weight, xT, b, start=True, stop=True):
            for lo_c in (0, 512):
                hi_c = min(GC, lo_c + 512)
                last = nc.tensor.matmul(ps[:, b * 512 + lo_c:b * 512 + hi_c], weight, xT[:, lo_c:hi_c], start=start, stop=stop, skip_group_check=True)
            return last

        def pair(b):
            return ps[:, b * 512:b * 512 + GC]

        def table_rows(table):
            return table.rearrange("(t p) f -> p t f", p=P)

        new_stage()
        g_first = sem("g_first")
        g_dma = sem("g_dma")
        with nc.Block() as block:
            @block.vector
            def _(dve):
                nc.vector.tensor_tensor(tiled(acc_gcn), tiled(x_cur[:, :]), bcast_last(dinv[:, :], D), ALU.mult).then_inc(g_first, 1)

            @block.sync
            def _(sp):
                sp.wait_ge(g_first, 1)
                sp.dma_start(table_rows(t0), tiled(acc_gcn)).then_inc(g_dma, 16)
                sp.wait_ge(g_dma, 16)

        def convolve(which, table):
            new_stage()
            pre = which + "_"
            staged, lw_in, hot, mm = (sem(pre + n) for n in ("staged", "lw_in", "hot", "mm"))
            sums = Sums(pre, d_tile, [acc_gcn], D)
            rows = arena[:, AT_BUF:AT_BUF + 16 * D].rearrange("p (s f) -> p s f", f=D)
            at = arena[:, AT_BUF + 16 * D:AT_BUF + 32 * D].rearrange("p (s f) -> p s f", f=D)
            lw_st = stage_lw[:, :].rearrange("p (s r) -> p s r", r=2)
            lw = d_lw[:, :].rearrange("p (c r) -> p c r", r=2)
            base = next_pass()

            def product(b, i):
                return ps[:, b * 1024 + i * D:b * 1024 + (i + 1) * D]
            with nc.Block() as block:
                @block.gpsimd
                def _(pool):
                    def free(k, b):
                        need(pool, mm, 2 * k + b - 1)
                    gathers(pool, table, rows, staged, free)

                @block.vector
                def _(dve):
                    sums.start(dve)
                    stage_first(d_src, staged)

                    def body(k):
                        for b in range(2):
                            n = 2 * k + b
                            stage_index(dve, d_src, staged, base, k, b)
                            settle(nc.vector)
                            nc.vector.tensor_copy(lw_st[:, 8 * b:8 * b + 8, :], lw[:, bass.ds(16 * k + 8 * b, 8), :]).then_inc(lw_in, 1)
                            adds = not isinstance(k, int) or b > 0
                            if adds:
                                sums.open(16 * k + 8 * b - 8, behind=not isinstance(k, int))
                                dve.wait_ge(mm, n)
                            dve.wait_ge(lw_in, n + 1)
                            for i in range(8):
                                s = 8 * b + i
                                one_hot = nc.vector.tensor_scalar(at[:, s, :], iota_row[:, :], lw_st[:, s, 0:1], lw_st[:, s, 1:2],
                                                                  ALU.is_equal, ALU.mult)
                                if i == 7:
                                    one_hot.then_inc(hot, 1)
                                if adds:
                                    sums.add(i, product(1 - b, i))
                    turns(dve, ITER, body)
                    sums.open(SC - 8)
                    dve.wait_ge(mm, HALVES)
                    for i in range(8):
                        sums.add(i, product(1, i))

                @block.tensor
                def _(pe):
                    def body(k):
                        for b in range(2):
                            n = 2 * k + b
                            pe.wait_ge(hot, n + 1)
                            need(pe, sums.drained, n - 1)
                            pe.wait_ge(landed[b], base + 128 * k + 128)
                            for i in range(8):
                                last = nc.tensor.matmul(product(b, i), at[:, 8 * b + i, :], rows[:, 8 * b + i, :], start=True, stop=True)
                            last.then_inc(mm, 1)
                    turns(pe, ITER, body)

        def scratch(o, n):
            return arena[:, o:o + n]

        convolve("c1", t0)

        new_stage()
        a_rdy, t_ps, t_sb, h_ps, n1_v, n1_dma = (sem("n1_" + n) for n in ("a", "tps", "tsb", "hps", "v", "dma"))
        A, aT, r = (scratch(AT_BUF + i * GC, GC) for i in range(3))
        with nc.Block() as block:
            @block.vector
            def _(dve):
                def body(k):
                    step = Chain(dve, n1_v, 3 * k)
                    step(nc.vector.tensor_tensor(tiled(A), cols(acc_gcn, k), bcast_last(dinv[:, bass.ds(GT * k, GT)], D), ALU.mult))
                    dve.sem_inc(a_rdy, 1)
                    dve.wait_ge(h_ps, k + 1)
                    step(nc.vector.tensor_tensor(tiled(r), tiled(pair(2)), bcast_mid(bias["L0_gnn_b1"], GT), ALU.add))
                    step(nc.vector.scalar_tensor_tensor(cols(acc_gcn, k), tiled(r), 0.0, bcast_last(dinv[:, bass.ds(GT * k, GT)], D), ALU.max, ALU.mult))
                turns(dve, NG, body)

            @block.tensor
            def _(pe):
                def body(k):
                    pe.wait_ge(a_rdy, k + 1)
                    transposes(A, 0).then_inc(t_ps, 1)
                    pe.wait_ge(t_sb, k + 1)
                    products(aT, w["L0_gnn_W1"], 2).then_inc(h_ps, 1)
                turns(pe, NG, body)

            @block.scalar
            def _(act):
                def body(k):
                    act.wait_ge(t_ps, k + 1)
                    nc.scalar.activation(aT, pair(0), ACT.Copy).then_inc(t_sb, 1)
                turns(act, NG, body)

            @block.sync
            def _(sp):
                sp.wait_ge(n1_v, 3 * NG)
                sp.dma_start(table_rows(t1), tiled(acc_gcn)).then_inc(n1_dma, 16)
                sp.wait_ge(n1_dma, 16)

        convolve("c2", t1)

        new_stage()
        a_rdy, t_ps, t_sb, h_ps, h_sb, y_ps, dma_n = (sem("n2_" + n) for n in ("a", "tps", "tsb", "hps", "hsb", "yps", "dma"))
        z_rdy, zt_ps, zt_sb, xi_ps, xi_sb, uv_ps, v_n, v_o = (sem("n2_" + n) for n in ("z", "ztps", "ztsb", "xips", "xisb", "uvps", "v", "vo"))
        norm = Norm("n2_", 2)
        A, aT, hT, z, zT, xiT, r, sq = (scratch(i * GC, GC) for i in range(8))
        rows2 = scratch(8 * GC, GT * (D + H)).rearrange("p (t f) -> p t f", f=D + H)
        assert 8 * GC + GT * (D + H) <= AT_ACC
        LNS, OUTS = 19, 3
        with nc.Block() as block:
            @block.vector
            def _(dve):
                def first(k):
                    need(dve, t_ps, k)
                    nc.vector.tensor_tensor(tiled(A), cols(acc_gcn, k), bcast_last(dinv[:, bass.ds(GT * k, GT)], D), ALU.mult).then_inc(a_rdy, 1)

                def rows(k):
                    step = Chain(dve, v_o, OUTS * k)
                    dve.wait_ge(xi_ps, k + 1)
                    need(dve, dma_n, 16 * k)
                    step(nc.vector.tensor_tensor(rows2[:, :, 0:D], tiled(pair(4)), bcast_mid(bias["L1_gnn_b_in"], GT), ALU.add))
                    dve.wait_ge(uv_ps, k + 1)
                    uv = ps[:, 3072:3072 + GT * 2 * H].rearrange("p (t f) -> p t f", f=2 * H)
                    step(nc.vector.tensor_tensor(rows2[:, :, D:D + H], uv[:, :, 0:H], bcast_mid(b_u[:, :], GT), ALU.add))
                    settle(nc.vector)
                    step(nc.vector.tensor_copy(cols(v_tab, k, H), uv[:, :, H:2 * H]))
                    assert step.n == OUTS

                def turn(k, more):
                    if more:
                        first(k + 1)
                    step = Chain(dve, v_n, LNS * k)
                    dve.wait_ge(y_ps, k + 1)
                    step(nc.vector.tensor_tensor(tiled(r), tiled(pair(0)), cols(x_cur, k), ALU.add))
                    step(nc.vector.tensor_tensor(tiled(r), tiled(r), bcast_mid(bias["L0_gnn_bfc"], GT), ALU.add))
                    norm.vector(step, tiled(r), tiled(sq), cols(x_cur, k), k, 0)
                    settle(nc.vector)
                    step(nc.vector.tensor_copy(tiled(r), cols(x_cur, k)))
                    if not isinstance(k, int) or k > 0:
                        rows(k - 1)
                    need(dve, zt_ps, k)
                    norm.vector(step, tiled(r), tiled(sq), tiled(z), k, 1)
                    step(nc.vector.tensor_tensor(tiled(z), tiled(z), bcast_mid(bias["L1_gnn_ln_gamma"], GT), ALU.mult))
                    step(nc.vector.tensor_tensor(tiled(z), tiled(z), bcast_mid(bias["L1_gnn_ln_beta"], GT), ALU.add))
                    dve.sem_inc(z_rdy, 1)
                    assert step.n == LNS, step.n
                ahead(dve, first, turn)
                rows(NG - 1)

            @block.gpsimd
            def _(pool):
                norm.gpsimd(pool)

            @block.tensor
            def _(pe):
                def first(k):
                    pe.wait_ge(a_rdy, k + 1)
                    need(pe, v_n, LNS * k - LNS + 1)
                    transposes(A, 0).then_inc(t_ps, 1)
                    pe.wait_ge(t_sb, k + 1)
                    products_T(w["L0_gnn_W2"], aT, 2).then_inc(h_ps, 1)
                    pe.wait_ge(h_sb, k + 1)
                    products(hT, w["L0_gnn_Wfc"], 0).then_inc(y_ps, 1)

                def turn(k, more):
                    if more:
                        first(k + 1)
                    pe.wait_ge(z_rdy, k + 1)
                    need(pe, v_o, OUTS * k)
                    transposes(z, 4).then_inc(zt_ps, 1)
                    pe.wait_ge(zt_sb, k + 1)
                    products_T(w["L1_gnn_W_in"], zT, 6)
                    products(zT, w["L1_gnn_W_in"], 4).then_inc(xi_ps, 1)
                    pe.wait_ge(xi_sb, k + 1)
                    for i in range(GT):
                        last = nc.tensor.matmul(ps[:, 3072 + i * 2 * H:3072 + (i + 1) * 2 * H], xiT[:, i * P:(i + 1) * P], w_uv[:, :], start=True, stop=True)
                    last.then_inc(uv_ps, 1)
                ahead(pe, first, turn)

            @block.scalar
            def _(act):
                def first(k):
                    act.wait_ge(t_ps, k + 1)
                    nc.scalar.activation(aT, pair(0), ACT.Copy).then_inc(t_sb, 1)
                    act.wait_ge(h_ps, k + 1)
                    nc.scalar.activation(hT, pair(2), ACT.Relu, bias=col["L0_gnn_b2"]).then_inc(h_sb, 1)

                def turn(k, more):
                    if more:
                        first(k + 1)
                    act.wait_ge(zt_ps, k + 1)
                    nc.scalar.activation(zT, pair(4), ACT.Copy).then_inc(zt_sb, 1)
                    act.wait_ge(xi_ps, k + 1)
                    nc.scalar.activation(xiT, pair(6), ACT.Identity, bias=col["L1_gnn_b_in"]).then_inc(xi_sb, 1)
                ahead(act, first, turn)

            @block.sync
            def _(sp):
                def body(k):
                    sp.wait_ge(v_o, OUTS * k + OUTS)
                    sp.dma_start(table_rows(t2)[:, bass.ds(GT * k, GT), :], rows2).then_inc(dma_n, 16)
                turns(sp, NG, body)
                sp.wait_ge(dma_n, 16 * NG)

        def score_pass(which, idx, table, width, keep, tab, tab_w):
            new_stage()
            pre = which + "_"
            staged, oT_hot, exp_ps, scored, v_s = (sem(pre + n) for n in ("staged", "hot", "expps", "scored", "v"))
            lo_in = [sem(pre + "lo0"), sem(pre + "lo1")]
            spilled = [sem(pre + "sp0"), sem(pre + "sp1")]
            gat = which == "gat"
            o = AT_BUF
            rows = arena[:, o:o + 16 * width].rearrange("p (s f) -> p s f", f=width)
            o += 16 * width
            if gat:
                o = AT_BUF + 16 * (D + H)
            lo_b = arena[:, o:o + 2048].rearrange("p (b c) -> p b c", b=2)
            hot_T = (arena[:, o + 2048:o + 4096] if gat else arena[:, AT_ACC + 2048:AT_ACC + 4096]).rearrange("p (b c) -> p b c", b=2)
            prod = arena[:, AT_ACC:AT_ACC + 2048].rearrange("p (b c) -> p b c", b=4)
            assert o + 2048 <= AW
            base = next_pass()
            lo_rows = d_loT.rearrange("(n c) e -> n (c e)", c=8)
            steps = 2 if gat else 4
            with nc.Block() as block:
                @block.gpsimd
                def _(pool):
                    def free(k, b):
                        need(pool, scored, 2 * k + b - 1)
                        need(pool, spilled[b], 16 * k)
                    gathers(pool, table, rows, staged, free)

                @block.sync
                def _(sp):
                    def body(k):
                        for b in range(2):
                            n = 2 * k + b
                            need(sp, oT_hot, n - 1)
                            sp.dma_start(lo_b[:, b, :], lo_rows[bass.ds(n, 1), :].to_broadcast([P, 8 * P])).then_inc(lo_in[b], 16)
                    turns(sp, ITER, body)

                @block.scalar
                def _(act):
                    def body(k):
                        for b in range(2):
                            n = 2 * k + b
                            act.wait_ge(landed[b], base + 128 * k + 128)
                            act.dma_start(spill[bass.ds(n, 1)].rearrange("o p (c f) -> p (o c) f", f=D),
                                          rows[:, 8 * b:8 * b + 8, keep:keep + D]).then_inc(spilled[b], 16)
                    turns(act, ITER, body)
                    for b in range(2):
                        act.wait_ge(spilled[b], 16 * ITER)

                @block.tensor
                def _(pe):
                    def body(k):
                        for b in range(2):
                            n = 2 * k + b
                            tiles = tile_numbers(pe, d_tile, 16 * k + 8 * b)
                            need(pe, scored, n - 1)
                            pe.wait_ge(oT_hot, n + 1)
                            for i in range(8):
                                o_ps = b * 1024 + i * tab_w
                                last = nc.tensor.matmul(ps[:, o_ps:o_ps + tab_w], hot_T[:, b, i * P:(i + 1) * P],
                                                        tab[:, bass.ds(tiles[i] * tab_w, tab_w)], start=True, stop=True)
                            last.then_inc(exp_ps, 1)
                    turns(pe, ITER, body)

                @block.vector
                def _(dve):
                    stage_first(idx, staged)

                    def body(k):
                        for b in range(2):
                            n = 2 * k + b
                            step = Chain(dve, v_s, steps * n)
                            stage_index(dve, idx, staged, base, k, b)
                            dve.wait_ge(lo_in[b], 16 * k + 16)
                            nc.vector.tensor_scalar(hot_T[:, b, :], lo_b[:, b, :], iota_part[:, 0:1], None, ALU.is_equal).then_inc(oT_hot, 1)
                            dve.wait_ge(landed[b], base + 128 * k + 128)
                            dve.wait_ge(exp_ps, n + 1)
                            e_out = e_all[:, bass.ds(64 * n, 64)]
                            if gat:
                                raw = prod[:, b, 0:64].rearrange("p (c h) -> p c h", h=H)
                                step(nc.vector.tensor_tensor(raw, ps[:, b * 1024:b * 1024 + 64].rearrange("p (c h) -> p c h", h=H),
                                                             rows[:, 8 * b:8 * b + 8, D:D + H], ALU.add))
                                step(nc.vector.scalar_tensor_tensor(e_out, prod[:, b, 0:64], 0.2, prod[:, b, 0:64], ALU.mult, ALU.max))
                            else:
                                for z in range(2):
                                    pr = prod[:, 2 * b + z, :]
                                    step(nc.vector.tensor_tensor(tiled(pr), tiled(ps[:, b * 1024 + z * 512:b * 1024 + z * 512 + 512]),
                                                                 rows[:, 8 * b + 4 * z:8 * b + 4 * z + 4, 0:D], ALU.mult))
                                    step(nc.vector.tensor_reduce(e_out[:, 32 * z:32 * z + 32], pr.rearrange("p (c d) -> p c d", d=DK), AX.X, ALU.add))
                            dve.sem_inc(scored, 1)
                    turns(dve, ITER, body)

        def weigh_pass(which, head_last):
            new_stage()
            pre = which + "_w_"
            W = D + H
            msg, mm, msg_v, zero, hot, hot_dve, dist, minus_in = (sem(pre + n) for n in ("msg", "mm", "v", "zero", "hot", "hot_dve", "dist", "minus_in"))
            BY_ACT = 4
            minus_lo = stage_lw[:, 0:16]
            acc_odd = arena[:, AT_BUF:AT_BUF + NT * W]
            back_in = [sem(pre + "in0"), sem(pre + "in1")]
            sums = Sums(pre, d_tile, [acc_att, acc_odd], W)
            rows = arena[:, AT_Q:AT_Q + 2048].rearrange("p (b c) -> p b c", b=2)
            at = arena[:, AT_Q + 2048:AT_Q + 4096].rearrange("p (b c n) -> p b c n", b=2, c=8)
            m = arena[:, AT_Q + 4096:AT_Q + 4096 + 16 * W].rearrange("p (b c f) -> p b c f", b=2, c=8)
            lw = d_lw[:, :].rearrange("p (c r) -> p c r", r=2)

            def product(b, i):
                o = b * 2048 + i // 3 * 512 + i % 3 * W
                return ps[:, o:o + W]
            with nc.Block() as block:
                @block.sync
                def _(sp):
                    def body(k):
                        for b in range(2):
                            n = 2 * k + b
                            need(sp, msg, n - 1)
                            sp.dma_start(rows[:, b, :], spill[bass.ds(n, 1)].rearrange("o p c -> p (o c)")).then_inc(back_in[b], 16)
                    turns(sp, ITER, body)

                @block.scalar
                def _(act):
                    def body(k):
                        for b in range(2):
                            n = 2 * k + b
                            nc.scalar.activation(minus_lo[:, 8 * b:8 * b + 8], lw[:, bass.ds(8 * n, 8), 0], ACT.Copy, scale=-1.0).then_inc(minus_in, 1)
                            need(act, mm, n - 1)
                            nc.scalar.activation(m[:, b, :, D:W], e_all[:, bass.ds(64 * n, 64)].rearrange("p (c h) -> p c h", h=H), ACT.Copy).then_inc(msg_v, 1)
                            act.wait_ge(minus_in, n + 1)
                            for i in range(BY_ACT):
                                last = nc.scalar.activation(at[:, b, i], iota_row[:, :], ACT.Abs, bias=minus_lo[:, 8 * b + i:8 * b + i + 1])
                            last.then_inc(dist, 1)
                            act.wait_ge(dist, n + 1)
                            nc.scalar.activation(at[:, b, 0:BY_ACT], at[:, b, 0:BY_ACT], ACT.Relu, bias=ones[:, 0:1], scale=-1.0).then_inc(hot, 1)
                    turns(act, ITER, body)

                @block.gpsimd
                def _(pool):
                    def body(k):
                        for b in range(2):
                            n = 2 * k + b
                            need(pool, mm, n - 1)
                            pool.wait_ge(back_in[b], 16 * k + 16)
                            for i in range(8):
                                ex = e_all[:, bass.ds(64 * n + 8 * i, 8)]
                                if head_last:
                                    out_m = m[:, b, i, 0:D].rearrange("p (d h) -> p d h", h=H)
                                    in_m = rows[:, b, i * D:(i + 1) * D].rearrange("p (d h) -> p d h", h=H)
                                    ex = bcast_mid(ex, DK)
                                else:
                                    out_m = m[:, b, i, 0:D].rearrange("p (h d) -> p h d", h=H)
                                    in_m = rows[:, b, i * D:(i + 1) * D].rearrange("p (h d) -> p h d", h=H)
                                    ex = bcast_last(ex, DK)
                                last = nc.gpsimd.tensor_tensor(out_m, in_m, ex, ALU.mult)
                            last.then_inc(msg, 1)
                    turns(pool, ITER, body)

                @block.tensor
                def _(pe):
                    def body(k):
                        for b in range(2):
                            n = 2 * k + b
                            pe.wait_ge(hot, n + 1)
                            pe.wait_ge(hot_dve, n + 1)
                            need(pe, sums.drained, n - 1)
                            pe.wait_ge(msg_v, n + 1)
                            pe.wait_ge(msg, n + 1)
                            for i in range(8):
                                last = nc.tensor.matmul(product(b, i), at[:, b, i], m[:, b, i], start=True, stop=True)
                            last.then_inc(mm, 1)
                    turns(pe, ITER, body)

                @block.vector
                def _(dve):
                    sums.start(dve)
                    nc.vector.memset(acc_odd, 0.0).then_inc(zero, 1)
                    nc.vector.memset(acc_att, 0.0).then_inc(zero, 1)
                    dve.wait_ge(zero, 2)

                    def one_hots(n, b):
                        nc.vector.tensor_tensor(at[:, b, BY_ACT:8], bcast_mid(iota_row[:, :], 8 - BY_ACT),
                                                bcast_last(lw[:, bass.ds(8 * n + BY_ACT, 8 - BY_ACT), 0], P), ALU.is_equal).then_inc(hot_dve, 1)
                    one_hots(0, 0)

                    def body(k):
                        for b in range(2):
                            n = 2 * k + b
                            need(dve, mm, n)
                            settle(nc.vector)
                            one_hots(n + 1, 1 - b)
                            sums.open(8 * n, behind=not isinstance(k, int) or b > 0)
                            dve.wait_ge(mm, n + 1)
                            for i in range(8):
                                sums.add(i, product(b, i))
                    turns(dve, ITER, body)
                    dve.wait_ge(sums.added, 8)
                    nc.vector.tensor_tensor(acc_att, acc_att, acc_odd, ALU.add)

        score_pass("gat", d_src, t2, D + H, 0, v_tab, H)
        softmax_weights("gat")
        weigh_pass("gat", True)

        new_stage()
        wt_in, wt_v, wt_blk = sem("wt_in"), sem("wt_v"), sem("wt_blk")
        basis = {n: scratch(AT_Q + i * NB * D, NB * D).rearrange("p (b o) -> p b o", b=NB) for i, n in enumerate("akqv")}
        comp = {n: scratch(AT_Q + 16 * D + i * TN * NB, TN * NB).rearrange("p (t b) -> p t b", b=NB) for i, n in enumerate("akqv")}
        w_tmp = scratch(AT_Q + 20 * D, TN * D).rearrange("p (t o) -> p t o", t=TN)
        pri = scratch(AT_Q + 30 * D, TN * H)
        with nc.Block() as block:
            @block.sync
            def _(sp):
                for n in "akqv":
                    sp.dma_start(basis[n], t["L2_gnn_w_basis_" + n].rearrange("b (i o) -> i b o", o=D)).then_inc(wt_in, 16)
                    sp.dma_start(comp[n].rearrange("p t b -> p (t b)"), t["L2_gnn_w_comp_" + n].rearrange("t b -> (t b)").partition_broadcast(P)).then_inc(wt_in, 16)
                sp.dma_start(pri, t["L2_gnn_relation_pri"].rearrange("t h -> (t h)").partition_broadcast(P)).then_inc(wt_in, 16)
                sp.wait_ge(wt_v, 2)
                for n in ("att", "msg"):
                    for h in range(H):
                        sp.dma_start(rel[n][h * DK:(h + 1) * DK, :].rearrange("p (t o) -> p t o", t=TN)[:, :, h * DK:(h + 1) * DK],
                                     t["L2_gnn_relation_" + n][:, h].rearrange("t i j -> i t j")).then_inc(wt_blk, 16)
                sp.wait_ge(wt_blk, 16 * 2 * H)

            @block.vector
            def _(dve):
                step = Chain(dve, wt_v)
                step(nc.vector.memset(rel["att"], 0.0))
                step(nc.vector.memset(rel["msg"], 0.0))
                dve.wait_ge(wt_in, 16 * 9)
                for n in "akqv":
                    for b in range(NB):
                        res = w_typed[n] if b == 0 else w_tmp
                        step(nc.vector.tensor_tensor(res, bcast_mid(basis[n][:, b, :], TN), bcast_last(comp[n][:, :, b], D), ALU.mult))
                        if b:
                            step(nc.vector.tensor_tensor(w_typed[n], w_typed[n], w_tmp, ALU.add))
                dve.wait_ge(wt_blk, 16 * 2 * H)
                step(nc.vector.tensor_scalar(pri, pri, DK ** -0.5, None, ALU.mult))
                att = rel["att"].rearrange("p (c j) -> p c j", j=DK)
                step(nc.vector.tensor_tensor(att, att, bcast_last(pri, DK), ALU.mult))

        def load_types(sp, done):
            sp.dma_start(ntb[:, 0:N], t["node_type_8"].partition_broadcast(P)).then_inc(done, 16)

        def attention_out(step, k, out_ap, head_last):
            den = small[:, 64:64 + GT * H].rearrange("p (t h) -> p t h", h=H)
            acc = cols(acc_att, k, D + H)
            step(nc.vector.tensor_scalar(den, acc[:, :, D:D + H], 1e-30, None, ALU.max))
            step(nc.vector.reciprocal(den, den))
            if head_last:
                step(nc.vector.tensor_tensor(out_ap.rearrange("p (t d h) -> p t d h", t=GT, h=H), acc[:, :, 0:D].rearrange("p t (d h) -> p t d h", h=H),
                                             den.unsqueeze(2).to_broadcast([P, GT, DK, H]), ALU.mult))
            else:
                step(nc.vector.tensor_tensor(out_ap.rearrange("p (t h d) -> p t h d", t=GT, h=H), acc[:, :, 0:D].rearrange("p t (h d) -> p t h d", h=H),
                                             den.unsqueeze(3).to_broadcast([P, GT, H, DK]), ALU.mult))

        new_stage()
        a_rdy, t_ps, t_sb, y_ps, x_rdy, xt_ps, xt_sb, xm_rdy, xm_used, v_n = (sem("n3_" + n) for n in (
            "a", "tps", "tsb", "yps", "x", "xtps", "xtsb", "xm", "xmused", "v"))
        kv_sb, q_sb, kv_ps, kv_out, nt_in, nt_pad = (sem("n3_" + n) for n in ("kvsb", "qsb", "kvps", "kvout", "nt", "ntpad"))
        kv_dma = [sem("n3_dma0"), sem("n3_dma1")]
        norm = Norm("n3_", 1)
        xm = [scratch(AT_BUF + i * GC, GC) for i in range(2)]
        xT, kT, vT = (scratch(AT_BUF + i * GC, GC) for i in range(2, 5))
        A = r = xm[0]
        sq = x_new = xm[1]
        aT = xT
        kv_st = scratch(AT_BUF + 5 * GC, 2 * 1024).rearrange("p (z t f) -> p z t f", z=2, f=2 * D)
        t3_rows = t3.rearrange("(t n) f -> n t f", t=TN)
        PIECES = 2 * GT
        LNS = 13

        def piece_banks(p):
            return 2 + 2 * (p % 3), 3 + 2 * (p % 3)
        with nc.Block() as block:
            @block.sync
            def _(sp):
                sp.wait_ge(nt_pad, 1)
                load_types(sp, nt_in)

                def body(k):
                    for i in range(GT):
                        for z in range(2):
                            n = PIECES * k + 2 * i + z
                            sp.wait_ge(kv_out, n + 1)
                            sp.dma_start(t3_rows[bass.ds(P * (GT * k + i), P), 4 * z:4 * z + 4, :], kv_st[:, z]).then_inc(kv_dma[z], 16)
                turns(sp, NG, body)
                for z in range(2):
                    sp.wait_ge(kv_dma[z], 16 * GT * NG)

            @block.gpsimd
            def _(pool):
                norm.gpsimd(pool)

            @block.vector
            def _(dve):
                nc.vector.memset(ntb[:, N:NP], 0).then_inc(nt_pad, 1)

                def first(k):
                    step = Chain(dve, v_n, LNS * k)
                    attention_out(step, k, A, True)
                    dve.sem_inc(a_rdy, 1)
                    dve.wait_ge(y_ps, k + 1)
                    step(nc.vector.tensor_tensor(tiled(r), tiled(pair(0)), cols(x_cur, k), ALU.add))
                    step(nc.vector.tensor_tensor(tiled(r), tiled(r), bcast_mid(bias["L1_gnn_b_ff"], GT), ALU.add))
                    norm.vector(step, tiled(r), tiled(sq), tiled(x_new), k, 0)
                    dve.sem_inc(x_rdy, 1)
                    settle(nc.vector)
                    step(nc.vector.tensor_copy(cols(x_cur, k), tiled(x_new)))
                    assert step.n == LNS, step.n

                def typed(k):
                    dve.wait_ge(xt_sb, k + 1)
                    if isinstance(k, int) and k == 0:
                        dve.wait_ge(nt_in, 16)
                    for ty in range(TN):
                        if ty >= 2:
                            dve.wait_ge(xm_used, TN * k + ty - 1)
                        nc.vector.scalar_tensor_tensor(xm[ty % 2], ntb[:, bass.ds(GC * k, GC)], float(ty), xT, ALU.is_equal, ALU.mult).then_inc(xm_rdy, 1)
                    dve.wait_ge(xm_used, TN * k + TN)
                    settle(nc.vector)
                    nc.vector.tensor_copy(q_tab[:, bass.ds(GC * k, GC)], pair(6)).then_inc(q_sb, 1)

                def rows(k, more):
                    if more:
                        first(k + 1)

                def turn(k, more):
                    typed(k)
                    rows(k, more)
                ahead(dve, first, turn)

            @block.tensor
            def _(pe):
                def transposed_sums(k):
                    pe.wait_ge(a_rdy, k + 1)
                    transposes(A, 0).then_inc(t_ps, 1)

                def project(k):
                    pe.wait_ge(t_sb, k + 1)
                    products(aT, w["L1_gnn_W_ff"], 0).then_inc(y_ps, 1)

                def transposed_features(k):
                    pe.wait_ge(x_rdy, k + 1)
                    transposes(x_new, 0).then_inc(xt_ps, 1)

                def first(k):
                    transposed_sums(k)
                    project(k)
                    transposed_features(k)

                def typed(k):
                    need(pe, kv_out, PIECES * k)
                    for ty in range(TN):
                        pe.wait_ge(xm_rdy, TN * k + ty + 1)
                        f = dict(start=ty == 0, stop=ty == TN - 1)
                        products_T(w_typed["k"][:, ty, :], xm[ty % 2], 2, **f)
                        products_T(w_typed["v"][:, ty, :], xm[ty % 2], 4, **f)
                        products(xm[ty % 2], w_typed["q"][:, ty, :], 6, **f).then_inc(xm_used, 1)

                def rows(k, more):
                    pe.wait_ge(kv_sb, 2 * k + 2)
                    pe.wait_ge(q_sb, k + 1)
                    for p in range(PIECES):
                        if p >= 3:
                            pe.wait_ge(kv_out, PIECES * k + p - 2)
                        i, z = p // 2, p % 2
                        for src_T, name, b in zip((kT, vT), ("att", "msg"), piece_banks(p)):
                            last = nc.tensor.matmul(bank(b), src_T[:, i * P:(i + 1) * P], rel[name][:, z * 512:(z + 1) * 512], start=True, stop=True)
                        last.then_inc(kv_ps, 1)
                        if more and p == 1:
                            transposed_sums(k + 1)
                        if more and p == 4:
                            project(k + 1)
                        if more and p == PIECES - 2:
                            transposed_features(k + 1)

                def turn(k, more):
                    typed(k)
                    rows(k, more)
                ahead(pe, first, turn)

            @block.scalar
            def _(act):
                def sums_T(k):
                    act.wait_ge(t_ps, k + 1)
                    nc.scalar.activation(aT, pair(0), ACT.Copy).then_inc(t_sb, 1)

                def features_T(k):
                    act.wait_ge(xt_ps, k + 1)
                    nc.scalar.activation(xT, pair(0), ACT.Copy).then_inc(xt_sb, 1)

                def first(k):
                    sums_T(k)
                    features_T(k)

                def typed(k):
                    act.wait_ge(xm_used, TN * k + TN)
                    nc.scalar.activation(kT, pair(2), ACT.Copy).then_inc(kv_sb, 1)
                    nc.scalar.activation(vT, pair(4), ACT.Copy).then_inc(kv_sb, 1)

                def rows(k, more):
                    for p in range(PIECES):
                        act.wait_ge(kv_ps, PIECES * k + p + 1)
                        need(act, kv_dma[p % 2], 16 * (GT * k + p // 2))
                        b = piece_banks(p)[0] * 512
                        nc.scalar.activation(kv_st[:, p % 2].rearrange("p t (a f) -> p a t f", a=2),
                                             ps[:, b:b + 1024].rearrange("p (a t f) -> p a t f", a=2, f=D), ACT.Copy).then_inc(kv_out, 1)
                        if more and p == 2:
                            sums_T(k + 1)
                        if more and p == PIECES - 2:
                            features_T(k + 1)

                def turn(k, more):
                    typed(k)
                    rows(k, more)
                ahead(act, first, turn)

        score_pass("hgt", d_typed, t3, 2 * D, D, q_tab, D)
        softmax_weights("hgt")
        weigh_pass("hgt", False)

        AT_L3 = AW - NT * 2 * D
        acc_l3 = arena[:, AT_L3:AT_L3 + NT * 2 * D]
        U_T, W_T, VDE = l3_T[:, 0:D], l3_T[:, D:2 * D], l3_T[:, 2 * D:6 * D]
        new_stage()
        a_rdy, t_ps, t_sb, xm_rdy, xm_used, o_ps, x_rdy = (sem("n4_" + n) for n in ("a", "tps", "tsb", "xm", "xmused", "ops", "x"))
        xt_ps, xt_sb, h_ps, h_sb, w_ps, vde_ps, nt_in, nt_pad, nt_set, rows_rdy = (sem("n4_" + n) for n in (
            "xtps", "xtsb", "hps", "hsb", "wps", "vdeps", "nt", "ntpad", "ntset", "rows"))
        dma_n, v_a, v_n, v_r = (sem("n4_" + n) for n in ("dma", "va", "vn", "vr"))
        norm = Norm("n4_", 1)
        o = TN * D
        types = scratch(o, NP // 2).bitcast(BF16)
        o += NP // 2
        R5 = 5 * D
        rows5 = scratch(o, GT * R5).rearrange("p (t f) -> p t f", f=R5)
        o += GT * R5
        A, xs, aT, x2T = (scratch(o + i * GC, GC) for i in range(4))
        xm = [A, xs]
        o += 4 * GC
        assert o <= AT_ACC
        r, x_new = (scratch(AT_Q + i * GC, GC) for i in range(2))
        assert AT_Q + 2 * GC <= AT_L3
        x3T, hT = x_new, r
        types_in = acc_l3[:, NT * 2 * D - NP:].bitcast(I32)
        ATT, LNS, ROWS_V = 4, 10, 2 + GT + 1 + 4
        with nc.Block() as block:
            @block.sync
            def _(sp):
                sp.wait_ge(nt_pad, 1)
                sp.dma_start(types_in[:, 0:N], t["node_type_8"].partition_broadcast(P)).then_inc(nt_in, 16)

                def body(k):
                    sp.wait_ge(rows_rdy, k + 1)
                    sp.dma_start(table_rows(t4)[:, bass.ds(GT * k, GT), :], rows5[:, :, 2 * D:R5]).then_inc(dma_n, 16)
                    sp.dma_start(cols(p_dram, k), rows5[:, :, 0:D]).then_inc(dma_n, 16)
                    sp.dma_start(cols(dp_dram, k), rows5[:, :, D:2 * D]).then_inc(dma_n, 16)
                turns(sp, NG, body)
                sp.wait_ge(dma_n, 48 * NG)

            @block.gpsimd
            def _(pool):
                norm.gpsimd(pool)

            @block.vector
            def _(dve):
                nc.vector.memset(types_in[:, N:NP], 0).then_inc(nt_pad, 1)

                def start(k):
                    need(dve, xm_used, TN * k)
                    step = Chain(dve, v_a, ATT * k)
                    attention_out(step, k, A, False)
                    settle(nc.vector)
                    step(nc.vector.tensor_copy(tiled(xs), cols(x_cur, k)))
                    dve.sem_inc(a_rdy, 1)

                def mask(k, ty):
                    if ty == 0:
                        dve.wait_ge(t_sb, 2 * k + 2)
                        if isinstance(k, int) and k == 0:
                            dve.wait_ge(nt_set, 1)
                    if ty >= 2:
                        dve.wait_ge(xm_used, TN * k + ty - 1)
                    nc.vector.scalar_tensor_tensor(xm[ty % 2], types[:, bass.ds(GC * k, GC)], float(ty), aT, ALU.is_equal, ALU.mult).then_inc(xm_rdy, 1)

                def first(k):
                    start(k)
                    for ty in range(TN):
                        mask(k, ty)

                def turn(k, more):
                    step = Chain(dve, v_n, LNS * k)
                    dve.wait_ge(o_ps, k + 1)
                    step(nc.vector.tensor_tensor(tiled(r), tiled(pair(2)), bcast_mid(bias["L2_gnn_bias"], GT), ALU.add))
                    step(nc.vector.scalar_tensor_tensor(tiled(r), tiled(r), 0.0, cols(x_cur, k), ALU.max, ALU.add))
                    if more:
                        start(k + 1)
                    norm.vector(step, tiled(r), tiled(x_new), tiled(x_new), k, 0)
                    dve.sem_inc(x_rdy, 1)
                    settle(nc.vector)
                    step(nc.vector.tensor_copy(cols(x_cur, k), tiled(x_new)))
                    assert step.n == LNS, step.n
                    if more:
                        mask(k + 1, 0)
                        mask(k + 1, 1)
                    step = Chain(dve, v_r, ROWS_V * k)
                    need(dve, dma_n, 48 * k)
                    dve.wait_ge(w_ps, k + 1)
                    y = rows5[:, :, 4 * D:R5]
                    step(nc.vector.tensor_tensor(y, tiled(pair(4)), bcast_mid(bias["L3_gnn_W_b"], GT), ALU.add))
                    step(nc.vector.tensor_tensor(y, y, bcast_last(inv[:, bass.ds(GT * k, GT)], D), ALU.mult))
                    for i in range(GT):
                        dve.wait_ge(vde_ps, GT * k + i + 1)
                        step(nc.vector.tensor_tensor(rows5[:, i, 0:4 * D], bank(6 + i % 2), vde_bias, ALU.add))
                        if more and i < GT - 1:
                            mask(k + 1, i + 2)
                    z = rows5[:, :, 3 * D:4 * D]
                    step(nc.vector.tensor_tensor(z, z, y, ALU.mult))
                    dve.sem_inc(rows_rdy, 1)
                    acc = cols(acc_l3, k, 2 * D)
                    step(nc.vector.tensor_tensor(acc[:, :, 0:D], rows5[:, :, 0:D], rows5[:, :, 2 * D:3 * D], ALU.add))
                    step(nc.vector.scalar_tensor_tensor(acc[:, :, 0:D], acc[:, :, 0:D], 0.0, y, ALU.max, ALU.mult))
                    step(nc.vector.tensor_tensor(acc[:, :, 0:D], acc[:, :, 0:D], z, ALU.add))
                    step(nc.vector.tensor_copy(acc[:, :, D:2 * D], y))
                    assert step.n == ROWS_V, step.n
                ahead(dve, first, turn)

            @block.tensor
            def _(pe):
                def start(k):
                    pe.wait_ge(a_rdy, k + 1)
                    transposes(A, 0).then_inc(t_ps, 1)
                    pe.wait_ge(t_sb, 2 * k + 1)
                    transposes(xs, 0).then_inc(t_ps, 1)

                def typed(k, ty):
                    if ty == 0:
                        need(pe, v_n, LNS * k - LNS + 1)
                    pe.wait_ge(xm_rdy, TN * k + ty + 1)
                    products(xm[ty % 2], w_typed["a"][:, ty, :], 2, start=ty == 0, stop=False).then_inc(xm_used, 1)
                    if ty == TN - 1:
                        pe.wait_ge(t_sb, 2 * k + 2)
                        products(x2T, w["L2_gnn_loop_weight"], 2, start=False, stop=True).then_inc(o_ps, 1)

                def first(k):
                    start(k)
                    for ty in range(TN):
                        typed(k, ty)

                def turn(k, more):
                    if more:
                        start(k + 1)
                    pe.wait_ge(x_rdy, k + 1)
                    need(pe, v_r, ROWS_V * k)
                    transposes(x_new, 4).then_inc(xt_ps, 1)
                    pe.wait_ge(xt_sb, k + 1)
                    products_T(U_T, x3T, 6).then_inc(h_ps, 1)
                    products(x3T, W_T, 4).then_inc(w_ps, 1)
                    if more:
                        typed(k + 1, 0)
                        typed(k + 1, 1)
                    pe.wait_ge(h_sb, k + 1)
                    for i in range(GT):
                        if i >= 2:
                            pe.wait_ge(v_r, ROWS_V * k + 2 + i - 1)
                        nc.tensor.matmul(bank(6 + i % 2), hT[:, i * P:(i + 1) * P], VDE, start=True, stop=True).then_inc(vde_ps, 1)
                        if more and i > 0:
                            typed(k + 1, i + 1)
                ahead(pe, first, turn)

            @block.scalar
            def _(act):
                def start(k):
                    act.wait_ge(t_ps, 2 * k + 1)
                    nc.scalar.activation(aT, pair(0), ACT.Copy).then_inc(t_sb, 1)
                    act.wait_ge(t_ps, 2 * k + 2)
                    need(act, o_ps, k)
                    nc.scalar.activation(x2T, pair(0), ACT.Copy).then_inc(t_sb, 1)

                def turn(k, more):
                    if more:
                        start(k + 1)
                    act.wait_ge(xt_ps, k + 1)
                    act.wait_ge(v_n, LNS * k + LNS)
                    nc.scalar.activation(x3T, pair(4), ACT.Copy).then_inc(xt_sb, 1)
                    act.wait_ge(h_ps, k + 1)
                    nc.scalar.activation(hT, pair(6), ACT.Identity, bias=col["L3_gnn_U_b"]).then_inc(h_sb, 1)
                act.wait_ge(nt_in, 16)
                nc.scalar.activation(types, types_in, ACT.Copy).then_inc(nt_set, 1)
                ahead(act, start, turn)

        new_stage()
        staged, oT_hot, hot, p_ps, mm, v_s = (sem("l3_" + n) for n in ("staged", "hotT", "hot", "pps", "mm", "v"))
        lo_in = [sem("l3_lo0"), sem("l3_lo1")]
        got_rows = [[sem(f"l3_rows{b}{z}") for z in range(2)] for b in range(2)]
        p_in, a_abs, minus, minus_in = sem("l3_p_in"), sem("l3_abs"), sem("l3_minus"), sem("l3_minus_in")
        sums = Sums("l3_", s_tile, [acc_l3], 2 * D)
        p_tab = arena[:, 1024:1024 + NP]
        o = 1024 + NP
        rows = arena[:, o:o + 16 * 3 * D].rearrange("p (s f) -> p s f", f=3 * D)
        o += 16 * 3 * D
        lo_b = arena[:, o:o + 2048].rearrange("p (b c) -> p b c", b=2)
        o += 2048
        hot_T = arena[:, o:o + 2048].rearrange("p (b c) -> p b c", b=2)
        o += 2048
        at = arena[:, o:o + 2048].rearrange("p (b c n) -> p b c n", b=2, c=8)
        o += 2048
        prod = arena[:, o:o + 1024].rearrange("p (z c) -> p z c", z=2)
        o += 1024
        minus_part, minus_lo = small[:, 0:1], small[:, 8:24]
        assert o <= AT_L3, o
        lo_rows = s_loT.rearrange("(n c) e -> n (c e)", c=8)

        def product(i):
            return ps[:, 2048 + i * 2 * D:2048 + (i + 1) * 2 * D]
        with nc.Block() as block:
            @block.gpsimd
            def _(pool):
                def body(k):
                    for b in range(2):
                        n = 2 * k + b
                        pool.wait_ge(staged, n + 1)
                        for z in range(2):
                            need(pool, mm, 2 * n + z - 3)
                            settle(pool)
                            for i in range(8 * b + 4 * z, 8 * b + 4 * z + 4):
                                pool.indirect_dma_start(out=rows[:, i, :], out_offset=None, in_=t4,
                                                        in_offset=bass.IndirectOffsetOnAxis(ap=stage_idx[:, i:i + 1], axis=0)).then_inc(got_rows[b][z], 16)
                turns(pool, ITER, body)

            @block.sync
            def _(sp):
                sp.dma_start(p_tab, p_dram).then_inc(p_in, 16)

                def body(k):
                    for b in range(2):
                        n = 2 * k + b
                        need(sp, oT_hot, n - 1)
                        sp.dma_start(lo_b[:, b, :], lo_rows[bass.ds(n, 1), :].to_broadcast([P, 8 * P])).then_inc(lo_in[b], 16)
                turns(sp, ITER, body)

            @block.scalar
            def _(act):
                act.wait_ge(minus, 1)

                def body(k):
                    for b in range(2):
                        n = 2 * k + b
                        need(act, p_ps, 2 * n - 2)
                        act.wait_ge(lo_in[b], 16 * k + 16)
                        nc.scalar.activation(hot_T[:, b, :], lo_b[:, b, :], ACT.Abs, bias=minus_part).then_inc(a_abs, 1)
                        act.wait_ge(a_abs, 2 * n + 1)
                        nc.scalar.activation(hot_T[:, b, :], hot_T[:, b, :], ACT.Relu, bias=ones[:, 0:1], scale=-1.0).then_inc(oT_hot, 1)
                        nc.scalar.activation(minus_lo[:, 8 * b:8 * b + 8], s_lo[:, bass.ds(8 * n, 8)], ACT.Copy, scale=-1.0).then_inc(minus_in, 1)
                        need(act, mm, 2 * n - 2)
                        act.wait_ge(minus_in, n + 1)
                        for i in range(8):
                            last = nc.scalar.activation(at[:, b, i], iota_row[:, :], ACT.Abs, bias=minus_lo[:, 8 * b + i:8 * b + i + 1])
                        last.then_inc(a_abs, 1)
                        act.wait_ge(a_abs, 2 * n + 2)
                        nc.scalar.activation(at[:, b], at[:, b], ACT.Relu, bias=ones[:, 0:1], scale=-1.0).then_inc(hot, 1)
                turns(act, ITER, body)

            @block.tensor
            def _(pe):
                pe.wait_ge(p_in, 16)

                def expand(k, b):
                    n = 2 * k + b
                    tiles = tile_numbers(pe, s_tile, 16 * k + 8 * b)
                    pe.wait_ge(oT_hot, n + 1)
                    need(pe, v_s, 6 * n - 6)
                    for i in range(8):
                        o_ps = b * 1024 + i * D
                        last = nc.tensor.matmul(ps[:, o_ps:o_ps + D], hot_T[:, b, i * P:(i + 1) * P],
                                                p_tab[:, bass.ds(tiles[i] * D, D)], start=True, stop=True)
                        if i % 4 == 3:
                            last.then_inc(p_ps, 1)

                def sum_up(n, b):
                    pe.wait_ge(hot, n + 1)
                    for z in range(2):
                        need(pe, sums.drained, 2 * n + z - 1)
                        pe.wait_ge(v_s, 6 * n + 3 * z + 3)
                        for i in range(4 * z, 4 * z + 4):
                            last = nc.tensor.matmul(product(i), at[:, b, i], rows[:, 8 * b + i, D:3 * D], start=True, stop=True)
                        last.then_inc(mm, 1)

                def body(k):
                    for b in range(2):
                        expand(k, b)
                        if not isinstance(k, int) or b > 0:
                            sum_up(2 * k + b - 1, 1 - b)
                turns(pe, ITER, body)
                sum_up(HALVES - 1, 1)

            @block.vector
            def _(dve):
                sums.start(dve)
                nc.vector.tensor_scalar(minus_part, iota_part[:, 0:1], -1.0, None, ALU.mult).then_inc(minus, 1)
                stage_first(s_dst, staged)

                def body(k):
                    for b in range(2):
                        n = 2 * k + b
                        adds = not isinstance(k, int) or b > 0
                        for z in range(2):
                            need(dve, got_rows[1 - b][z], 64 * (k + b))
                        settle(nc.vector)
                        nc.vector.tensor_copy(stage_idx[:, 8 * (1 - b):8 * (1 - b) + 8], s_dst[:, bass.ds(8 * n + 8, 8)]).then_inc(staged, 1)
                        if adds:
                            sums.open(16 * k + 8 * b - 8, behind=not isinstance(k, int))
                        need(dve, v_s, 6 * n)
                        for z in range(2):
                            got = rows[:, 8 * b + 4 * z:8 * b + 4 * z + 4, :]
                            pr = tiled(prod[:, z, :])
                            if adds:
                                dve.wait_ge(mm, 2 * n - 1 + z)
                                sums.add(4 * z, product(4 * z))
                            dve.wait_ge(got_rows[b][z], 64 * k + 64)
                            dve.wait_ge(p_ps, 2 * n + z + 1)
                            nc.vector.tensor_tensor(pr, tiled(ps[:, b * 1024 + z * 512:b * 1024 + z * 512 + 512]), got[:, :, 0:D], ALU.add).then_inc(v_s, 1)
                            if adds:
                                sums.add(4 * z + 1, product(4 * z + 1))
                            dve.wait_ge(v_s, 6 * n + 3 * z + 1)
                            nc.vector.scalar_tensor_tensor(pr, pr, 0.0, got[:, :, 2 * D:3 * D], ALU.max, ALU.mult).then_inc(v_s, 1)
                            if adds:
                                sums.add(4 * z + 2, product(4 * z + 2))
                            dve.wait_ge(v_s, 6 * n + 3 * z + 2)
                            nc.vector.tensor_tensor(got[:, :, D:2 * D], pr, got[:, :, D:2 * D], ALU.add).then_inc(v_s, 1)
                            if adds:
                                sums.add(4 * z + 3, product(4 * z + 3))
                                if z == 0:
                                    sums.drain(4)
                turns(dve, ITER, body)
                sums.open(SC - 8)
                for i in range(8):
                    if i % 4 == 0:
                        dve.wait_ge(mm, 2 * HALVES - 1 + i // 4)
                    sums.add(i, product(i))

        new_stage()
        dp_in, v_n, out_dma = sem("n5_dp"), sem("n5_v"), sem("n5_out")
        norm = Norm("n5_", 1)
        dp_all = arena[:, 1024:1024 + NP]
        r, sq = scratch(8192, GC), scratch(8192 + GC, GC)
        with nc.Block() as block:
            @block.gpsimd
            def _(pool):
                norm.gpsimd(pool)

            @block.vector
            def _(dve):
                dve.wait_ge(dp_in, 16)

                def body(k):
                    step = Chain(dve, v_n, 11 * k)
                    acc = cols(acc_l3, k, 2 * D)
                    step(nc.vector.tensor_tensor(tiled(r), cols(dp_all, k), acc[:, :, D:2 * D], ALU.mult))
                    step(nc.vector.tensor_tensor(tiled(r), tiled(r), acc[:, :, 0:D], ALU.add))
                    step(nc.vector.tensor_tensor(tiled(r), tiled(r), bcast_last(inv[:, bass.ds(GT * k, GT)], D), ALU.mult))
                    step(nc.vector.tensor_tensor(tiled(r), tiled(r), cols(x_cur, k), ALU.add))
                    norm.vector(step, tiled(r), tiled(sq), cols(x_cur, k), k, 0)
                turns(dve, NG, body)

            @block.sync
            def _(sp):
                sp.dma_start(dp_all, dp_dram).then_inc(dp_in, 16)
                x_tiles = tiled(x_cur[:, :])

                def body(k):
                    sp.wait_ge(v_n, 11 * k + 11)
                    sp.dma_start(out[bass.ds(GT * P * k, GT * P), :].rearrange("(t p) f -> p t f", p=P), x_tiles[:, bass.ds(GT * k, GT), :]).then_inc(out_dma, 16)
                turns(sp, NG - 1, body)
                full = (NG - 1) * GT
                sp.wait_ge(v_n, 11 * NG)
                sp.dma_start(out[full * P:(NT - 1) * P, :].rearrange("(t p) f -> p t f", p=P), x_tiles[:, full:NT - 1, :]).then_inc(out_dma, 16)
                sp.dma_start(out[(NT - 1) * P:N, :], x_cur[0:LAST, (NT - 1) * D:NT * D]).then_inc(out_dma, 16)
                sp.wait_ge(out_dma, 16 * (NG + 1))


def kernel(**inputs):
    import numpy as np
    import concourse.bacc as bacc
    from concourse.bass_utils import run_bass_kernel_spmd as run

    nc = bacc.Bacc("TRN2", target_bir_lowering=False, num_devices=1)
    arrays, t = {}, {}
    for n in inputs:
        a = np.ascontiguousarray(inputs[n])
        arrays["in_" + n] = a
        t[n] = nc.dram_tensor("in_" + n, a.shape, mybir.dt.from_np(a.dtype), kind="ExternalInput").ap()
    out = nc.dram_tensor("out", (N, D), F32, kind="ExternalOutput").ap()
    build(nc, t, out)
    r = run(nc, [arrays], core_ids=[0])
    return r.results[0]["out"]
```
